# Optimizing a Trainium2 kernel written in Bass

```python
import numpy as np
import jax
import jax.numpy as jnp

def _softmax(x, axis=-1):
    return jax.nn.softmax(x, axis=axis)

def _gelu(x):
    return jax.nn.gelu(x, approximate=True)

def _silu(x):
    return jax.nn.silu(x)

def _sigmoid(x):
    return jax.nn.sigmoid(x)

def _layernorm(x, axis=-1, eps=1e-05):
    m = jnp.mean(x, axis=axis, keepdims=True)
    v = jnp.var(x, axis=axis, keepdims=True)
    return (x - m) / jnp.sqrt(v + eps)

def _scatter_add(tgt, idx, src, axis=0):
    return tgt.at[idx].add(src)

def _segment_sum(src, seg, n):
    return jax.ops.segment_sum(src, seg, n)
kernel_name = 'mk_decoder_preln_d2_seqx_r4_6996e3'

def setup_inputs(seed: int=0):
    np.random.seed(seed)
    _w = jnp.asarray

    def _rec_inputs():
        import jax
        import jax.numpy as jnp
        _rk = jax.random.key(seed)
        x = -0.0003929 + 0.9999 * jax.random.normal(jax.random.fold_in(_rk, 1), (32, 128, 256), jnp.float32)
        _lenS = 128 - jax.random.randint(jax.random.fold_in(_rk, 7), (32,), 0, max(1, 128 // 4) + 1, jnp.int32)
        _lenS2 = 128 - jax.random.randint(jax.random.fold_in(_rk, 8), (32,), 0, max(1, 128 // 4) + 1, jnp.int32)
        _ctx_1024P = jax.random.normal(jax.random.fold_in(_rk, 11), (32, 16, 256), jnp.float32)
        _ctx_1024c = jax.random.dirichlet(jax.random.fold_in(_rk, 511), 0.3 * jnp.ones((16,), jnp.float32), (32, 128))
        _ctx_1024t = jnp.einsum('bsk,bkd->bsd', _ctx_1024c, _ctx_1024P)
        _ctx_1024t = _ctx_1024t * jax.lax.rsqrt(jnp.mean(jnp.square(_ctx_1024t)) + 1e-12) * 0.953939
        ctx_1024 = 2.81802e-05 + 1.00001 * (_ctx_1024t + 0.3 * jax.random.normal(jax.random.fold_in(_rk, 611), (32, 128, 256), jnp.float32))
        fside_BxS2_0 = jax.random.uniform(jax.random.fold_in(_rk, 12), (32, 128), jnp.float32, 0.0, 2047.4)
        return (x, ctx_1024, fside_BxS2_0)
    x, ctx_1024, fside_BxS2_0 = _rec_inputs()

    def _L0_attn_setup():
        import jax, jax.numpy as jnp
        import numpy as np
        B, L, D, N = (2, 512, 256, 16)
        H = D // N
        THETA = 10000.0

        def apply_rope(x):
            l, h = (x.shape[-2], x.shape[-1])
            freqs = THETA ** (-jnp.arange(0, h, 2, dtype=jnp.float32) / h)
            ang = jnp.arange(l, dtype=jnp.float32)[:, None] * freqs
            cos, sin = (jnp.cos(ang), jnp.sin(ang))
            x_even = x[..., 0::2]
            x_odd = x[..., 1::2]
            out_even = cos * x_even - sin * x_odd
            out_odd = sin * x_even + cos * x_odd
            return jnp.stack((out_even, out_odd), axis=-1).reshape(x.shape)
        key = jax.random.key(seed)
        ks = jax.random.split(key, 9)
        s = 0.02
        return {'x': jax.random.normal(ks[0], (B, L, D), dtype=jnp.float32), 'Wq': jax.random.normal(ks[1], (D, D), dtype=jnp.float32) * s, 'bq': jax.random.normal(ks[2], (D,), dtype=jnp.float32) * s, 'Wk': jax.random.normal(ks[3], (D, D), dtype=jnp.float32) * s, 'bk': jax.random.normal(ks[4], (D,), dtype=jnp.float32) * s, 'Wv': jax.random.normal(ks[5], (D, D), dtype=jnp.float32) * s, 'bv': jax.random.normal(ks[6], (D,), dtype=jnp.float32) * s, 'Wo': jax.random.normal(ks[7], (D, D), dtype=jnp.float32) * s, 'bo': jax.random.normal(ks[8], (D,), dtype=jnp.float32) * s, 'scale': jnp.ones((1,), dtype=jnp.float32) * H ** (-0.5)}
    _L0_attn_all = _L0_attn_setup()
    _L0_attn_in = {k: v for k, v in _L0_attn_all.items() if k in ('Wq', 'bq', 'Wk', 'bk', 'Wv', 'bv', 'Wo', 'bo', 'scale')}
    del _L0_attn_all

    def _L0_xattn_setup():
        import jax, jax.numpy as jnp
        import numpy as np
        B, S, DIN, DK, DV = (8, 512, 256, 256, 256)
        key = jax.random.key(seed)
        ks = jax.random.split(key, 9)
        s_in = 1.0 / np.sqrt(DIN)
        return {'query': jax.random.normal(ks[0], (B, S, DIN), jnp.float32), 'key_': jax.random.normal(ks[1], (B, S, DIN), jnp.float32), 'value': jax.random.normal(ks[2], (B, S, DIN), jnp.float32), 'Wq_w': jax.random.uniform(ks[3], (DK, DIN), jnp.float32, -s_in, s_in), 'Wq_b': jax.random.uniform(ks[4], (DK,), jnp.float32, -s_in, s_in), 'Wk_w': jax.random.uniform(ks[5], (DK, DIN), jnp.float32, -s_in, s_in), 'Wk_b': jax.random.uniform(ks[6], (DK,), jnp.float32, -s_in, s_in), 'Wv_w': jax.random.uniform(ks[7], (DV, DIN), jnp.float32, -s_in, s_in), 'Wv_b': jax.random.uniform(ks[8], (DV,), jnp.float32, -s_in, s_in)}
    _L0_xattn_all = _L0_xattn_setup()
    _L0_xattn_in = {k: v for k, v in _L0_xattn_all.items() if k in ('Wq_w', 'Wq_b', 'Wk_w', 'Wk_b', 'Wv_w', 'Wv_b')}
    del _L0_xattn_all

    def _L0_ffn_setup():
        import jax, jax.numpy as jnp
        import numpy as np
        B, S, H, E = (4, 512, 256, 8)
        key = jax.random.key(seed)
        k1, k2, k3 = jax.random.split(key, 3)
        scale_w = 1.0 / np.sqrt(H)
        return {'x': jax.random.normal(k1, (B, S, H), dtype=jnp.float32), 'router_w': jax.random.normal(k2, (H, E), dtype=jnp.float32) * scale_w, 'router_b': jnp.zeros((E,), dtype=jnp.float32), 'expert_w': jax.random.normal(k3, (E, H, H), dtype=jnp.float32) * scale_w, 'expert_b': jnp.zeros((E, H), dtype=jnp.float32)}
    _L0_ffn_all = _L0_ffn_setup()
    _L0_ffn_in = {k: v for k, v in _L0_ffn_all.items() if k in ('router_w', 'router_b', 'expert_w', 'expert_b')}
    del _L0_ffn_all

    def _L1_attn_setup():
        import jax, jax.numpy as jnp
        import numpy as np
        import math
        D_MODEL = 256
        N_HEADS = 16
        D_HEAD = D_MODEL // N_HEADS
        WINDOW = 64
        SCALE = 1.0 / math.sqrt(D_HEAD)

        def _window_mask(seq_len: int) -> jnp.ndarray:
            i = jnp.arange(seq_len)[:, None]
            j = jnp.arange(seq_len)[None, :]
            allowed = (j <= i) & (j > i - WINDOW)
            return jnp.where(allowed, 0.0, -jnp.inf).astype(jnp.float32)
        key = jax.random.key(seed)
        kx, kqkv, kout = jax.random.split(key, 3)
        x = jax.random.normal(kx, (2, 512, D_MODEL), dtype=jnp.float32)
        lim_qkv = math.sqrt(6.0 / (D_MODEL + 3 * D_MODEL))
        W_qkv = jax.random.uniform(kqkv, (D_MODEL, 3 * D_MODEL), dtype=jnp.float32, minval=-lim_qkv, maxval=lim_qkv)
        lim_out = math.sqrt(6.0 / (D_MODEL + D_MODEL))
        W_out = jax.random.uniform(kout, (D_MODEL, D_MODEL), dtype=jnp.float32, minval=-lim_out, maxval=lim_out)
        return {'x': x, 'W_qkv': W_qkv, 'W_out': W_out}
    _L1_attn_all = _L1_attn_setup()
    _L1_attn_in = {k: v for k, v in _L1_attn_all.items() if k in ('W_qkv', 'W_out')}
    del _L1_attn_all

    def _L1_xattn_setup():
        import jax, jax.numpy as jnp
        import numpy as np
        DIM = 256
        NUM_HEADS = 16
        HEAD_DIM = DIM // NUM_HEADS
        ROPE_THETA = 10000.0

        def rms_norm(x, w):
            eps = jnp.finfo(x.dtype).eps
            var = jnp.mean(jnp.square(x), axis=-1, keepdims=True)
            return x * jax.lax.rsqrt(var + eps) * w

        def rope(x, pos, theta=ROPE_THETA):
            d = x.shape[-1]
            inv_freq = theta ** (-jnp.arange(0, d, 2, dtype=x.dtype) / d)
            ang = pos[:, None, :, None] * inv_freq
            cos, sin = (jnp.cos(ang), jnp.sin(ang))
            x1, x2 = jnp.split(x, 2, axis=-1)
            return jnp.concatenate([x1 * cos - x2 * sin, x1 * sin + x2 * cos], axis=-1)
        key = jax.random.key(seed)
        ks = jax.random.split(key, 9)
        b, n = (2, 512)
        s = DIM ** (-0.5)
        return {'tgt': jax.random.normal(ks[0], (b, n, DIM), jnp.float32), 'src': jax.random.normal(ks[1], (b, n, DIM), jnp.float32), 'tgt_pos': jax.random.uniform(ks[2], (b, n), jnp.float32) * n, 'src_pos': jax.random.uniform(ks[3], (b, n), jnp.float32) * n, 'Wq': jax.random.normal(ks[4], (DIM, DIM), jnp.float32) * s, 'Wkv': jax.random.normal(ks[5], (DIM, 2 * DIM), jnp.float32) * s, 'Wo': jax.random.normal(ks[6], (DIM, DIM), jnp.float32) * s, 'q_norm_w': jnp.ones((HEAD_DIM,), jnp.float32), 'k_norm_w': jnp.ones((HEAD_DIM,), jnp.float32)}
    _L1_xattn_all = _L1_xattn_setup()
    _L1_xattn_in = {k: v for k, v in _L1_xattn_all.items() if k in ('Wq', 'Wkv', 'Wo', 'q_norm_w', 'k_norm_w')}
    del _L1_xattn_all

    def _L1_ffn_setup():
        import jax, jax.numpy as jnp
        import numpy as np
        QMAX = 127.0

        def _ste_round(v):
            return v + jax.lax.stop_gradient(jnp.round(v) - v)

        def _act_fake_quant(x, clip_factor):
            scale = jax.nn.sigmoid(clip_factor) * jnp.max(jnp.abs(x)) / QMAX
            return jnp.clip(_ste_round(x / scale), -QMAX - 1.0, QMAX) * scale

        def _weight_fake_quant(w):
            scale = jnp.max(jnp.abs(w), axis=1, keepdims=True) / QMAX
            return jnp.clip(_ste_round(w / scale), -QMAX - 1.0, QMAX) * scale
        key = jax.random.key(seed)
        k1, k2, k3, k4 = jax.random.split(key, 4)
        B, S, H, I = (8, 2048, 256, 704)
        return {'x': jax.random.normal(k1, (B, S, H), dtype=jnp.float32), 'clip_x': jnp.full((1,), 4.0, dtype=jnp.float32), 'clip_down': jnp.full((1,), 4.0, dtype=jnp.float32), 'w_gate': jax.random.normal(k2, (I, H), dtype=jnp.float32) * 0.02, 'w_up': jax.random.normal(k3, (I, H), dtype=jnp.float32) * 0.02, 'w_down': jax.random.normal(k4, (H, I), dtype=jnp.float32) * 0.02}
    _L1_ffn_all = _L1_ffn_setup()
    _L1_ffn_in = {k: v for k, v in _L1_ffn_all.items() if k in ('clip_x', 'clip_down', 'w_gate', 'w_up', 'w_down')}
    del _L1_ffn_all
    return {'x': x, 'ctx_1024': ctx_1024, 'fside_BxS2_0': fside_BxS2_0, 'L0_attn_Wq': _L0_attn_in['Wq'], 'L0_attn_bq': _L0_attn_in['bq'], 'L0_attn_Wk': _L0_attn_in['Wk'], 'L0_attn_bk': _L0_attn_in['bk'], 'L0_attn_Wv': _L0_attn_in['Wv'], 'L0_attn_bv': _L0_attn_in['bv'], 'L0_attn_Wo': _L0_attn_in['Wo'], 'L0_attn_bo': _L0_attn_in['bo'], 'L0_attn_scale': _L0_attn_in['scale'], 'L0_xattn_Wq_w': _L0_xattn_in['Wq_w'], 'L0_xattn_Wq_b': _L0_xattn_in['Wq_b'], 'L0_xattn_Wk_w': _L0_xattn_in['Wk_w'], 'L0_xattn_Wk_b': _L0_xattn_in['Wk_b'], 'L0_xattn_Wv_w': _L0_xattn_in['Wv_w'], 'L0_xattn_Wv_b': _L0_xattn_in['Wv_b'], 'L0_ffn_router_w': _L0_ffn_in['router_w'], 'L0_ffn_router_b': _L0_ffn_in['router_b'], 'L0_ffn_expert_w': _L0_ffn_in['expert_w'], 'L0_ffn_expert_b': _L0_ffn_in['expert_b'], 'L1_attn_W_qkv': _L1_attn_in['W_qkv'], 'L1_attn_W_out': _L1_attn_in['W_out'], 'L1_xattn_Wq': _L1_xattn_in['Wq'], 'L1_xattn_Wkv': _L1_xattn_in['Wkv'], 'L1_xattn_Wo': _L1_xattn_in['Wo'], 'L1_xattn_q_norm_w': _L1_xattn_in['q_norm_w'], 'L1_xattn_k_norm_w': _L1_xattn_in['k_norm_w'], 'L1_ffn_clip_x': _L1_ffn_in['clip_x'], 'L1_ffn_clip_down': _L1_ffn_in['clip_down'], 'L1_ffn_w_gate': _L1_ffn_in['w_gate'], 'L1_ffn_w_up': _L1_ffn_in['w_up'], 'L1_ffn_w_down': _L1_ffn_in['w_down']}

def reference(x, ctx_1024, fside_BxS2_0, L0_attn_Wq, L0_attn_bq, L0_attn_Wk, L0_attn_bk, L0_attn_Wv, L0_attn_bv, L0_attn_Wo, L0_attn_bo, L0_attn_scale, L0_xattn_Wq_w, L0_xattn_Wq_b, L0_xattn_Wk_w, L0_xattn_Wk_b, L0_xattn_Wv_w, L0_xattn_Wv_b, L0_ffn_router_w, L0_ffn_router_b, L0_ffn_expert_w, L0_ffn_expert_b, L1_attn_W_qkv, L1_attn_W_out, L1_xattn_Wq, L1_xattn_Wkv, L1_xattn_Wo, L1_xattn_q_norm_w, L1_xattn_k_norm_w, L1_ffn_clip_x, L1_ffn_clip_down, L1_ffn_w_gate, L1_ffn_w_up, L1_ffn_w_down):
    import jax
    import jax.numpy as jnp

    def _L0_attn_ref(x, Wq, bq, Wk, bk, Wv, bv, Wo, bo, scale):
        import jax, jax.numpy as jnp
        import numpy as np
        B, L, D, N = (2, 512, 256, 16)
        H = D // N
        THETA = 10000.0

        def apply_rope(x):
            l, h = (x.shape[-2], x.shape[-1])
            freqs = THETA ** (-jnp.arange(0, h, 2, dtype=jnp.float32) / h)
            ang = jnp.arange(l, dtype=jnp.float32)[:, None] * freqs
            cos, sin = (jnp.cos(ang), jnp.sin(ang))
            x_even = x[..., 0::2]
            x_odd = x[..., 1::2]
            out_even = cos * x_even - sin * x_odd
            out_odd = sin * x_even + cos * x_odd
            return jnp.stack((out_even, out_odd), axis=-1).reshape(x.shape)
        b, l, d = x.shape
        q = x @ Wq.T + bq
        k = x @ Wk.T + bk
        v = x @ Wv.T + bv
        q = q.reshape(b, l, N, H).transpose(0, 2, 1, 3)
        k = k.reshape(b, l, N, H).transpose(0, 2, 1, 3)
        v = v.reshape(b, l, N, H).transpose(0, 2, 1, 3)
        q = apply_rope(q) * scale
        k = apply_rope(k)
        dots = jnp.einsum('bnih,bnjh->bnij', q, k)
        i = jnp.arange(l)
        mask = i[:, None] < i[None, :]
        dots = jnp.where(mask, jnp.float32(-100000.0), dots)
        attn = jax.nn.softmax(dots, axis=-1)
        o = jnp.einsum('bnij,bnjh->bnih', attn, v)
        o = o.transpose(0, 2, 1, 3).reshape(b, l, d)
        return o @ Wo.T + bo

    def _L0_xattn_ref(query, key_, value, Wq_w, Wq_b, Wk_w, Wk_b, Wv_w, Wv_b):
        import jax, jax.numpy as jnp
        import numpy as np
        B, S, DIN, DK, DV = (8, 512, 256, 256, 256)
        Q = jnp.einsum('bsd,kd->bsk', query, Wq_w) + Wq_b
        K = jnp.einsum('bsd,kd->bsk', key_, Wk_w) + Wk_b
        V = jnp.einsum('bsd,vd->bsv', value, Wv_w) + Wv_b
        scale = 1.0 / jnp.sqrt(jnp.asarray(Q.shape[-1], Q.dtype))
        scores = jnp.einsum('bqk,bsk->bqs', Q, K) * scale
        attn = jax.nn.softmax(scores, axis=-1)
        return jnp.einsum('bqs,bsv->bqv', attn, V)

    def _L0_ffn_ref(x, router_w, router_b, expert_w, expert_b):
        import jax, jax.numpy as jnp
        import numpy as np
        B, S, H, E = (4, 512, 256, 8)
        b, s, h = x.shape
        xt = x.reshape(b * s, h)
        logits = xt @ router_w + router_b
        probs = jax.nn.softmax(logits, axis=-1)
        gate = jnp.max(probs, axis=-1)
        idx = jnp.argmax(probs, axis=-1)
        out_all = jnp.einsum('th,ehd->ted', xt, expert_w) + expert_b[None, :, :]
        e_out = jnp.take_along_axis(out_all, idx[:, None, None], axis=1)[:, 0, :]
        y = gate[:, None] * e_out
        return y.reshape(b, s, h)

    def _L1_attn_ref(x, W_qkv, W_out):
        import jax, jax.numpy as jnp
        import numpy as np
        import math
        D_MODEL = 256
        N_HEADS = 16
        D_HEAD = D_MODEL // N_HEADS
        WINDOW = 64
        SCALE = 1.0 / math.sqrt(D_HEAD)

        def _window_mask(seq_len: int) -> jnp.ndarray:
            i = jnp.arange(seq_len)[:, None]
            j = jnp.arange(seq_len)[None, :]
            allowed = (j <= i) & (j > i - WINDOW)
            return jnp.where(allowed, 0.0, -jnp.inf).astype(jnp.float32)
        B, S, _ = x.shape
        qkv = x @ W_qkv
        qkv = qkv.reshape(B, S, 3, N_HEADS, D_HEAD)
        qkv = jnp.transpose(qkv, (2, 0, 3, 1, 4))
        q, k, v = (qkv[0], qkv[1], qkv[2])
        scores = jnp.einsum('bhsd,bhtd->bhst', q, k) * SCALE
        scores = scores + _window_mask(S)[None, None]
        weights = jax.nn.softmax(scores, axis=-1)
        out = jnp.einsum('bhst,bhtd->bhsd', weights, v)
        out = jnp.transpose(out, (0, 2, 1, 3)).reshape(B, S, D_MODEL)
        return out @ W_out

    def _L1_xattn_ref(tgt, src, tgt_pos, src_pos, Wq, Wkv, Wo, q_norm_w, k_norm_w):
        import jax, jax.numpy as jnp
        import numpy as np
        DIM = 256
        NUM_HEADS = 16
        HEAD_DIM = DIM // NUM_HEADS
        ROPE_THETA = 10000.0

        def rms_norm(x, w):
            eps = jnp.finfo(x.dtype).eps
            var = jnp.mean(jnp.square(x), axis=-1, keepdims=True)
            return x * jax.lax.rsqrt(var + eps) * w

        def rope(x, pos, theta=ROPE_THETA):
            d = x.shape[-1]
            inv_freq = theta ** (-jnp.arange(0, d, 2, dtype=x.dtype) / d)
            ang = pos[:, None, :, None] * inv_freq
            cos, sin = (jnp.cos(ang), jnp.sin(ang))
            x1, x2 = jnp.split(x, 2, axis=-1)
            return jnp.concatenate([x1 * cos - x2 * sin, x1 * sin + x2 * cos], axis=-1)
        b, n, _ = tgt.shape
        m = src.shape[1]
        h, hd = (NUM_HEADS, HEAD_DIM)
        q = (tgt @ Wq).reshape(b, n, h, hd).transpose(0, 2, 1, 3)
        kv = (src @ Wkv).reshape(b, m, 2, h, hd)
        k = kv[:, :, 0].transpose(0, 2, 1, 3)
        v = kv[:, :, 1].transpose(0, 2, 1, 3)
        q = rms_norm(q, q_norm_w)
        k = rms_norm(k, k_norm_w)
        q = rope(q, tgt_pos)
        k = rope(k, src_pos)
        scores = jnp.einsum('bhnd,bhmd->bhnm', q, k) / hd ** 0.5
        attn = jax.nn.softmax(scores, axis=-1)
        x = jnp.einsum('bhnm,bhmd->bhnd', attn, v)
        x = x.transpose(0, 2, 1, 3).reshape(b, n, h * hd)
        return x @ Wo

    def _L1_ffn_ref(x, clip_x, clip_down, w_gate, w_up, w_down):
        import jax, jax.numpy as jnp
        import numpy as np
        QMAX = 127.0

        def _ste_round(v):
            return v + jax.lax.stop_gradient(jnp.round(v) - v)

        def _act_fake_quant(x, clip_factor):
            scale = jax.nn.sigmoid(clip_factor) * jnp.max(jnp.abs(x)) / QMAX
            return jnp.clip(_ste_round(x / scale), -QMAX - 1.0, QMAX) * scale

        def _weight_fake_quant(w):
            scale = jnp.max(jnp.abs(w), axis=1, keepdims=True) / QMAX
            return jnp.clip(_ste_round(w / scale), -QMAX - 1.0, QMAX) * scale
        xq = _act_fake_quant(x, clip_x[0])
        gate = jnp.einsum('bsh,ih->bsi', xq, _weight_fake_quant(w_gate))
        up = jnp.einsum('bsh,ih->bsi', xq, _weight_fake_quant(w_up))
        h = _act_fake_quant(jax.nn.silu(gate) * up, clip_down[0])
        return jnp.einsum('bsi,hi->bsh', h, _weight_fake_quant(w_down))
    x = x + _L0_attn_ref(_layernorm(x, axis=-1), L0_attn_Wq, L0_attn_bq, L0_attn_Wk, L0_attn_bk, L0_attn_Wv, L0_attn_bv, L0_attn_Wo, L0_attn_bo, L0_attn_scale)
    x = x + _L0_xattn_ref(_layernorm(x, axis=-1), ctx_1024, ctx_1024, L0_xattn_Wq_w, L0_xattn_Wq_b, L0_xattn_Wk_w, L0_xattn_Wk_b, L0_xattn_Wv_w, L0_xattn_Wv_b)
    x = x + _L0_ffn_ref(_layernorm(x, axis=-1), L0_ffn_router_w, L0_ffn_router_b, L0_ffn_expert_w, L0_ffn_expert_b)
    x = x + _L1_attn_ref(_layernorm(x, axis=-1), L1_attn_W_qkv, L1_attn_W_out)
    x = x + _L1_xattn_ref(_layernorm(x, axis=-1), ctx_1024, fside_BxS2_0, fside_BxS2_0, L1_xattn_Wq, L1_xattn_Wkv, L1_xattn_Wo, L1_xattn_q_norm_w, L1_xattn_k_norm_w)
    x = x + _L1_ffn_ref(_layernorm(x, axis=-1), L1_ffn_clip_x, L1_ffn_clip_down, L1_ffn_w_gate, L1_ffn_w_up, L1_ffn_w_down)
    return x

_drawn_inputs = setup_inputs


def setup_inputs(seed=0):
    import zlib

    import numpy as np

    out = dict(_drawn_inputs(seed))
    spreads = {'L0_ffn_router_b': (0.0, 0.1),
     'L0_ffn_expert_b': (0.0, 0.1),
     'L1_xattn_q_norm_w': (1.0, 0.6),
     'L1_xattn_k_norm_w': (1.0, 0.2)}
    factors = {'L0_attn_Wq': 7.207,
     'L0_attn_bq': 8.0,
     'L0_attn_Wk': 6.152,
     'L0_attn_bk': 22.523,
     'L0_attn_bv': 2.819,
     'L0_xattn_Wq_b': 5.859,
     'L0_xattn_Wk_b': 64.0}
    for name, (base, spread) in spreads.items():
        noise = np.random.default_rng([zlib.crc32(name.encode()), seed]).standard_normal(out[name].shape)
        drawn = base * np.exp(spread * noise) if base else spread * noise
        out[name] = jnp.asarray(drawn.astype(out[name].dtype))
    for name, factor in factors.items():
        out[name] = (out[name] * factor).astype(out[name].dtype)
    return out
```

```python
import numpy as np
import concourse.bass as bass
from concourse import mybir
from contextlib import ExitStack

F32 = mybir.dt.float32
BF16 = mybir.dt.bfloat16
U32 = mybir.dt.uint32
ALU = mybir.AluOpType
ACT = mybir.ActivationFunctionType
AX = mybir.AxisListType

B, S, D = 32, 128, 256
P = 128
KC = D // P
H, HD = 16, 16
HG = 4
E = 8
I = 704
IC = -(-I // P)
EPS = 1e-5
RMS_EPS = float(np.finfo(np.float32).eps)
QMAX = 127.0
ROUND = 1.5 * 2.0 ** 23
TWO_PI = 2.0 * np.pi
NEG = -1e30


def rows(c):
    return min(P, I - c * P)


def waits(eng, sem, value):
    if isinstance(value, int) and value <= 0:
        return
    eng.wait_ge(sem, value)


def pipeline(eng, body, depth, turn=2, count=B):
    last = count + depth - 1
    head = 1 + turn if turn > 2 else 2 * turn
    steady = (count - head) // turn * turn
    for t in range(head):
        body(t, t % turn, lambda s, t=t: 0 <= t - s < count)
    with eng.Fori(head, head + steady - turn + 1, turn) as t:
        for i in range(turn):
            body(t + i, (head + i) % turn, lambda s: True)
    for t in range(head + steady, last):
        body(t, t % turn, lambda s, t=t: 0 <= t - s < count)


def apart(eng, k):
    eng.wait_ge(k.constants_done, 1)


def clear(nc, sems):
    with nc.Block() as block:
        @block.gpsimd
        def _(pool):
            for s in sems:
                pool.sem_clear(s)


def seq(x, b):
    if isinstance(b, int):
        return x[:, b, :]
    return x[:, bass.ds(b, 1), :].rearrange("p a d -> p (a d)")


def head_rows(h):
    return h // 8, h % 8 // 2, h % 2


def group_heads(g):
    return [8 * c + 2 * g + half for c in range(2) for half in range(2)]


class Norm:

    def __init__(self, ctx, nc, name, sem):
        self.stats = ctx.enter_context(nc.sbuf_tensor(f"{name}_stats", [P, 2, 6], F32))
        self.mean_var = ctx.enter_context(nc.sbuf_tensor(f"{name}_mean_var", [P, 2, 2], F32))
        self.var_eps = ctx.enter_context(nc.sbuf_tensor(f"{name}_var_eps", [P, 2, 1], F32))
        self.rstd = ctx.enter_context(nc.sbuf_tensor(f"{name}_rstd", [P, 2, 1], F32))
        self.mean_done = sem("mean_done")
        self.eps_added = sem("eps_added")
        self.rstd_done = sem("rstd_done")


def norm_statistics(dve, n, k, x, b, par):
    waits(dve, n.rstd_done, b - 1)
    dve.bn_stats(n.stats[:, par, :], seq(x, b))
    dve.drain()
    dve.bn_aggr(n.mean_var[:, par, :], n.stats[:, par, :]).then_inc(n.mean_done, 1)


def norm_rstd(pool, n, k, b, par):
    pool.wait_ge(n.mean_done, b + 1)
    pool.tensor_tensor(n.var_eps[:, par, :], n.mean_var[:, par, 1:2], k.eps[:, 0:1], ALU.add).then_inc(n.eps_added, 1)
    pool.wait_ge(n.eps_added, b + 1)
    pool.tensor_tensor(n.rstd[:, par, :], n.var_eps[:, par, :], k.minus_half[:, 0:1],
                       ALU.pow).then_inc(n.rstd_done, 1)


def heads_attention(nc, name, x, k, w_in, w_out, qkv_bias=None, out_bias=None, mask=None,
                    rope=None, batch_rope=None, ctx_t=None, scale=1.0, loads=()):
    with ExitStack() as ctx:
        sems = []
        def sb(n, shape, dt=F32):
            return ctx.enter_context(nc.sbuf_tensor(f"{name}_{n}", shape, dt))

        def bank(n):
            return ctx.enter_context(nc.psum_tensor(f"{name}_{n}", [P, 512], F32))

        def sem(n):
            sems.append(ctx.enter_context(nc.semaphore(f"{name}_{n}")))
            return sems[-1]

        rotated = rope is not None or batch_rope is not None
        norm = Norm(ctx, nc, name, sem)
        xn = sb("xn", [P, 2, D])
        xn_t = sb("xn_t", [P, 2, KC, S])
        if ctx_t is not None:
            c_t = sb("c_t", [P, 2, KC, S])
            c_loaded = [sem(f"c_loaded{i}") for i in range(2)]
        if rotated:
            qk = sb("qk", [P, 2 * D])
            by_cos = sb("by_cos", [P, 2 * D])
            by_sin = sb("by_sin", [P, 2 * D])
            qk_rot = sb("qk_rot", [P, 2, 2 * D])
        if batch_rope is not None:
            squares = sb("squares", [P, 2 * D])
            sum_sq = sb("sum_sq", [P, 2 * H])
            rms = sb("rms", [P, 2 * H])
            squared, summed, rms_eps, rms_done, rms_used = map(
                sem, ("squared", "summed", "rms_eps", "rms_done", "rms_used"))
        q_t = sb("q_t", [P, 2, KC, S])
        k_t = sb("k_t", [P, 2, 2, KC, S])
        v = sb("v", [P, 4, H, 2 * HD])
        neg_max = sb("neg_max", [P, 2, HG, 4])
        total = sb("total", [P, 2, HG, 4])
        share = sb("share", [P, 2, HG, 4])
        probs = sb("probs", [P, 2, HG, 4, S])
        probs_t = sb("probs_t", [P, 2, 4, S])
        o_t = sb("o_t", [P, KC, S])
        xv_bank, qk_bank, oo_bank, qkt_bank = map(bank, ("xv_bank", "qk_bank", "oo_bank", "qkt_bank"))
        score_banks = [bank(f"scores{i}") for i in range(2)]
        pt_banks = [bank(f"pt{i}") for i in range(2)]
        xn_tp, v_p = xv_bank[:, 0:D], xv_bank[:, D:2 * D]
        o_tp, out_p = oo_bank[:, 0:D], oo_bank[:, D:2 * D]

        (v_zeroed, xn_done, xn_tp_done, xn_t_done, qk_p_done, v_p_done, v_done, qk_done, cos_done,
         sin_done, rot_done, qkt_p_done, qk_t_done, scores_done, max_done,
         exp_done, share_done, probs_done, pt_p_done, pt_done, pv_done, o_t_done, out_p_done,
         x_biased, x_done) = map(sem, (
             "v_zeroed", "xn_done", "xn_tp_done", "xn_t_done", "qk_p_done", "v_p_done", "v_done",
             "qk_done", "cos_done", "sin_done", "rot_done", "qkt_p_done", "qk_t_done", "scores_done", "max_done", "exp_done", "share_done", "probs_done",
             "pt_p_done", "pt_done", "pv_done", "o_t_done", "out_p_done", "x_biased", "x_done"))

        blocks = ctx.enter_context(ExitStack())
        block = blocks.enter_context(nc.Block())

        if ctx_t is not None:
            @block.sync
            def _(sp):
                def load(b, par):
                    waits(sp, v_p_done, b - 1)
                    src = ctx_t[b] if isinstance(b, int) else \
                        ctx_t[bass.ds(b, 1)].rearrange("a d t -> (a d) t")
                    sp.dma_start(c_t[:, par, :, :], src.rearrange("(c p) t -> p c t", p=P)
                                 ).then_inc(c_loaded[par], 16)
                load(0, 0)
                load(1, 1)
                with sp.Fori(2, B - 1, 2) as t:
                    load(t, 0)
                    load(t + 1, 1)

        @block.tensor
        def _(pe):
            for s, n in loads:
                pe.wait_ge(s, n)

            def project(b, par):
                pe.wait_ge(xn_t_done, b + 1)
                waits(pe, qk_done if rotated else qk_t_done, b)
                if rotated and ctx_t is None:
                    for c in range(KC):
                        last = pe.matmul(qk_bank[:], xn_t[:, par, c, :], w_in[:, c, 0:2 * D],
                                         start=c == 0, stop=c == KC - 1)
                elif rotated:
                    for c in range(KC):
                        pe.matmul(qk_bank[:, 0:D], xn_t[:, par, c, :], w_in[:, c, 0:D],
                                  start=c == 0, stop=c == KC - 1)
                    pe.wait_ge(c_loaded[par], 8 * (b - par) + 16)
                    for c in range(KC):
                        last = pe.matmul(qk_bank[:, D:2 * D], c_t[:, par, c, :], w_in[:, c, D:2 * D],
                                         start=c == 0, stop=c == KC - 1)
                else:
                    for f in range(2 * KC):
                        for c in range(KC):
                            last = pe.matmul(qk_bank[:, f * S:(f + 1) * S],
                                             w_in[:, c, f * P:(f + 1) * P], xn_t[:, par, c, :],
                                             start=c == 0, stop=c == KC - 1)
                last.then_inc(qk_p_done, 1)
                src = xn_t if ctx_t is None else c_t
                for c in range(KC):
                    last = pe.matmul(v_p, src[:, par, c, :], w_in[:, c, 2 * D:3 * D],
                                     start=c == 0, stop=c == KC - 1)
                last.then_inc(v_p_done, 1)

            def scores(b, par, g):
                ring = score_banks[g % 2]
                waits(pe, exp_done, 4 * b + g - 1)
                if g == 0:
                    pe.wait_ge(qk_t_done, b + 1)
                if mask is not None:
                    pe.matmul(ring[:], k.ident_bf[:], mask[:, None, :].broadcast_to([P, 4, S]),
                              start=True, stop=True)
                for j, h in enumerate(group_heads(g)):
                    c, _, half = head_rows(h)
                    strip = slice(32 * g, 32 * g + 32)
                    last = pe.matmul(ring[:, j * S:(j + 1) * S], q_t[strip, par, c, :],
                                     k_t[strip, par, half, c, :], start=mask is None,
                                     stop=True, skip_group_check=mask is not None)
                last.then_inc(scores_done, 1)

            def probs_transposed(b, par, g):
                pe.wait_ge(probs_done, 4 * b + g + 1)
                waits(pe, pt_done, 4 * b + g - 1)
                for j in range(4):
                    last = pe.transpose(pt_banks[g % 2][:, j * S:(j + 1) * S],
                                        probs[:, par, g, j, :], k.ident[:])
                last.then_inc(pt_p_done, 1)

            def weighted_values(b, vbuf, g):
                pe.wait_ge(pt_done, 4 * b + g + 1)
                if g == 0:
                    waits(pe, x_done, b)
                    pe.wait_ge(v_done, b + 1)
                for j, h in enumerate(group_heads(g)):
                    c, _, half = head_rows(h)
                    last = pe.matmul(o_tp[32 * g:32 * g + 32, c * S:(c + 1) * S], v[:, vbuf, h, :],
                                     probs_t[:, g % 2, j, :], start=half == 0, stop=half == 1,
                                     skip_group_check=True)
                last.then_inc(pv_done, 1)

            def body(t, phase, live):
                par = phase % 2
                other = 1 - par
                if live(2):
                    b = t - 2
                    if rotated:
                        pe.wait_ge(rot_done, b + 1)
                        waits(pe, qk_t_done, b)
                        for f in range(2 * KC):
                            last = pe.transpose(qkt_bank[:, f * S:(f + 1) * S],
                                                qk_rot[:, par, f * P:(f + 1) * P], k.ident[:])
                        last.then_inc(qkt_p_done, 1)
                if live(1):
                    b = t - 1
                    pe.wait_ge(xn_done, b + 1)
                    waits(pe, v_done, b)
                    for c in range(KC):
                        last = pe.transpose(xn_tp[:, c * S:(c + 1) * S],
                                            xn[:, other, c * P:(c + 1) * P], k.ident[:])
                    last.then_inc(xn_tp_done, 1)
                if live(3):
                    probs_transposed(t - 3, other, 0)
                    probs_transposed(t - 3, other, 1)
                if live(2):
                    scores(t - 2, par, 0)
                    scores(t - 2, par, 1)
                if live(1):
                    project(t - 1, other)
                vbuf = (phase - 3) % 4
                for g in range(HG):
                    if live(3):
                        weighted_values(t - 3, vbuf, g)
                        if g < 2:
                            probs_transposed(t - 3, other, g + 2)
                    if live(2) and g < 2:
                        scores(t - 2, par, g + 2)
                if live(3):
                    b = t - 3
                    pe.wait_ge(o_t_done, b + 1)
                    for c in range(KC):
                        last = pe.matmul(out_p, o_t[:, c, :], w_out[:, c, :],
                                         start=c == 0, stop=c == KC - 1)
                    last.then_inc(out_p_done, 1)
            pipeline(pe, body, 4, 4)

        @block.vector
        def _(dve):
            dve.memset(v[:], 0.0).then_inc(v_zeroed, 1)
            dve.wait_ge(v_zeroed, 1)

            def body(t, phase, live):
                par = phase % 2
                other = 1 - par
                def head_max(g):
                    b = t - 2
                    dve.wait_ge(scores_done, 4 * b + g + 1)
                    waits(dve, exp_done, 4 * b + g - 7)
                    dve.tensor_reduce(neg_max[:, par, g, :],
                                      score_banks[g % 2][:].rearrange("p (j s) -> p j s", j=4),
                                      axis=AX.X, op=ALU.max, negate=True).then_inc(max_done, 1)

                def normalise(g):
                    b = t - 2
                    dve.wait_ge(exp_done, 4 * b + g + 1)
                    dve.reciprocal(share[:, par, g, :], total[:, par, g, :]).then_inc(share_done, 1)
                    dve.wait_ge(share_done, 4 * b + g + 1)
                    dve.tensor_tensor(probs[:, par, g, :, :], probs[:, par, g, :, :],
                                      share[:, par, g, :, None].broadcast_to([P, 4, S]),
                                      ALU.mult).then_inc(probs_done, 1)

                def copy_pt(g):
                    b = t - 3
                    dve.wait_ge(pt_p_done, 4 * b + g + 1)
                    waits(dve, pv_done, 4 * b + g - 1)
                    dve.tensor_copy(probs_t[:, g % 2, :, :].rearrange("p j s -> p (j s)"),
                                    pt_banks[g % 2][:]).then_inc(pt_done, 1)

                if live(3):
                    copy_pt(0)
                    copy_pt(1)
                if live(2):
                    head_max(0)
                    head_max(1)
                if live(1):
                    b = t - 1
                    if batch_rope is not None:
                        dve.wait_ge(squared, b + 1)
                        waits(dve, rms_done, b)
                        dve.tensor_reduce(sum_sq[:], squares[:].rearrange("p (h d) -> p h d", d=HD),
                                          axis=AX.X, op=ALU.add).then_inc(summed, 1)
                    dve.wait_ge(v_p_done, b + 1)
                    waits(dve, pv_done, 4 * b - 12)
                    vbuf = (phase - 1) % 4
                    for half in range(2):
                        dst = v[:, vbuf, half:H:2, half * HD:(half + 1) * HD]
                        src = v_p.rearrange("p (h d) -> p h d", d=HD)[:, half:H:2, :]
                        if qkv_bias is None:
                            last = dve.tensor_copy(dst, src)
                        else:
                            bias = qkv_bias[:, 2 * D:3 * D].rearrange("p (h d) -> p h d", d=HD)
                            last = dve.tensor_tensor(dst, src, bias[:, half:H:2, :], ALU.add)
                    last.then_inc(v_done, 1)
                    if rotated:
                        dve.wait_ge(qk_p_done, b + 1)
                        waits(dve, cos_done, b)
                        waits(dve, sin_done, b)
                        if batch_rope is not None:
                            dve.wait_ge(rms_done, b + 1)
                            dve.tensor_tensor(qk[:].rearrange("p (h d) -> p h d", d=HD),
                                              qk_bank[:].rearrange("p (h d) -> p h d", d=HD),
                                              rms[:, :, None].broadcast_to([P, 2 * H, HD]),
                                              ALU.mult).then_inc(qk_done, 1)
                            tab = seq(batch_rope, b)
                        else:
                            dve.tensor_tensor(qk[:], qk_bank[:], qkv_bias[:, 0:2 * D],
                                              ALU.add).then_inc(qk_done, 1)
                            tab = rope
                        dve.wait_ge(qk_done, b + 1)
                        waits(dve, rot_done, b)
                        cos = tab[:, 0:2 * HD].rearrange("p (a d) -> p a d", a=2)
                        dve.tensor_tensor(by_cos[:].rearrange("p (a h d) -> p a h d", a=2, h=H),
                                          qk[:].rearrange("p (a h d) -> p a h d", a=2, h=H),
                                          cos[:, :, None, :].broadcast_to([P, 2, H, HD]),
                                          ALU.mult).then_inc(cos_done, 1)
                if live(2):
                    normalise(0)
                    normalise(1)
                    head_max(2)
                    head_max(3)
                if live(3):
                    copy_pt(2)
                    copy_pt(3)
                if live(0):
                    norm_statistics(dve, norm, k, x, t, par)
                if live(1) and rotated:
                    b = t - 1
                    dve.wait_ge(sin_done, b + 1)
                    dve.wait_ge(cos_done, b + 1)
                    waits(dve, qkt_p_done, b - 1)
                    dve.tensor_tensor(qk_rot[:, other, :], by_cos[:], by_sin[:],
                                      ALU.add).then_inc(rot_done, 1)
                if live(0):
                    dve.wait_ge(norm.rstd_done, t + 1)
                    waits(dve, xn_tp_done, t - 1)
                    dve.tensor_scalar(xn[:, par, :], seq(x, t), norm.mean_var[:, par, 0:1],
                                      norm.rstd[:, par, :], ALU.subtract, ALU.mult
                                      ).then_inc(xn_done, 1)
                if live(2):
                    normalise(2)
                    normalise(3)
                if live(3):
                    b = t - 3
                    dve.wait_ge(out_p_done, b + 1)
                    if out_bias is not None:
                        dve.wait_ge(x_biased, b + 1)
                    dve.tensor_tensor(seq(x, b), out_p, seq(x, b), ALU.add).then_inc(x_done, 1)
            for s, n in k.x_chunks:
                dve.wait_ge(s, n)
            pipeline(dve, body, 4, 4)

        @block.scalar
        def _(act):
            def exps(t, par, g):
                b = t - 2
                act.wait_ge(max_done, 4 * b + g + 1)
                waits(act, probs_done, 4 * b + g - 7)
                if g == 0:
                    waits(act, pt_p_done, 4 * b - 4)
                for j in range(4):
                    last = act.activation(probs[:, par, g, j, :], score_banks[g % 2][:, j * S:(j + 1) * S],
                                          ACT.Exp, bias=neg_max[:, par, g, j:j + 1],
                                          accum_out=total[:, par, g, j:j + 1])
                last.then_inc(exp_done, 1)

            def body(t, phase, live):
                par = phase % 2
                other = 1 - par
                if live(2):
                    b = t - 2
                    src = qkt_bank if rotated else qk_bank
                    if rotated:
                        act.wait_ge(qkt_p_done, b + 1)
                    else:
                        act.wait_ge(qk_p_done, b + 1)
                    waits(act, scores_done, 4 * b - 4)
                    act.activation(q_t[:, par, :, :].rearrange("p c t -> p (c t)"), src[:, 0:2 * S],
                                   ACT.Copy, scale=scale)
                    for half, kept in enumerate((k.even_rows, k.odd_rows)):
                        last = act.activation(k_t[:, par, half, :, :].rearrange("p c t -> p (c t)"),
                                              src[:, 2 * S:4 * S], ACT.Copy, scale=kept[:, 0:1])
                    last.then_inc(qk_t_done, 1)
                if live(1):
                    b = t - 1
                    act.wait_ge(xn_tp_done, b + 1)
                    waits(act, v_p_done, b - 1)
                    act.activation(xn_t[:, other, :, :].rearrange("p c t -> p (c t)"), xn_tp,
                                   ACT.Copy).then_inc(xn_t_done, 1)
                if live(2):
                    exps(t, par, 0)
                    exps(t, par, 1)
                if live(1) and batch_rope is not None:
                    b = t - 1
                    act.wait_ge(qk_p_done, b + 1)
                    waits(act, summed, b)
                    act.activation(squares[:], qk_bank[:], ACT.Square).then_inc(squared, 1)
                if live(2):
                    exps(t, par, 2)
                    exps(t, par, 3)
                if live(3):
                    b = t - 3
                    act.wait_ge(pv_done, 4 * b + 4)
                    waits(act, out_p_done, b)
                    act.activation(o_t[:].rearrange("p c t -> p (c t)"), o_tp,
                                   ACT.Copy).then_inc(o_t_done, 1)
            pipeline(act, body, 4, 4)

        @block.gpsimd
        def _(pool):
            def body(t, phase, live):
                par = phase % 2
                if live(1) and batch_rope is not None:
                    b = t - 1
                    pool.wait_ge(summed, b + 1)
                    waits(pool, qk_done, b)
                    pool.tensor_tensor(sum_sq[:], sum_sq[:], k.rms_eps[:], ALU.add
                                       ).then_inc(rms_eps, 1)
                    pool.wait_ge(rms_eps, b + 1)
                    pool.tensor_tensor(rms[:], sum_sq[:], k.minus_half[:, 0:2 * H],
                                       ALU.pow).then_inc(rms_done, 1)
                if live(1) and rotated:
                    b = t - 1
                    pool.wait_ge(qk_done, b + 1)
                    waits(pool, rot_done, b)
                    tab = rope if batch_rope is None else seq(batch_rope, b)
                    sin = tab[:, 2 * HD:4 * HD].rearrange("p (a f d) -> p a f d", a=2, f=2)
                    dst = by_sin[:].rearrange("p (a h f d) -> p a h f d", a=2, h=H, f=2)
                    src = qk[:].rearrange("p (a h f d) -> p a h f d", a=2, h=H, f=2)
                    for f in range(2):
                        last = pool.tensor_tensor(dst[:, :, :, f, :], src[:, :, :, 1 - f, :],
                                                  sin[:, :, f, :][:, :, None, :].broadcast_to(
                                                      [P, 2, H, HD // 2]), ALU.mult)
                    last.then_inc(sin_done, 1)
                if live(1) and out_bias is not None:
                    b = t - 1
                    pool.wait_ge(xn_done, b + 1)
                    pool.tensor_tensor(seq(x, b), seq(x, b), out_bias[:], ALU.add
                                       ).then_inc(x_biased, 1)
                if live(0):
                    norm_rstd(pool, norm, k, t, par)
            pipeline(pool, body, 4, 4)

        blocks.close()
        clear(nc, sems)


def context_attention(nc, name, x, k, w_in, q_bias, k_bias, v_bias, ctx_t, loads):
    with ExitStack() as ctx:
        sems = []
        def sb(n, shape, dt=F32):
            return ctx.enter_context(nc.sbuf_tensor(f"{name}_{n}", shape, dt))

        def bank(n):
            return ctx.enter_context(nc.psum_tensor(f"{name}_{n}", [P, 512], F32))

        def sem(n):
            sems.append(ctx.enter_context(nc.semaphore(f"{name}_{n}")))
            return sems[-1]

        norm = Norm(ctx, nc, name, sem)
        xn = sb("xn", [P, 2, D])
        xn_t = sb("xn_t", [P, 2, KC, S])
        c_t = sb("c_t", [P, 2, KC, S])
        q_t = sb("q_t", [P, 2, KC, S])
        k_t = sb("k_t", [P, 2, KC, S])
        v = sb("v", [P, 4, D])
        neg_max = sb("neg_max", [P, 2, 1])
        total = sb("total", [P, 2, 1])
        share = sb("share", [P, 4, 1])
        probs = sb("probs", [P, 2, S])
        probs_t = sb("probs_t", [P, 2, S])
        xq_bank, k_bank, v_bank, score_bank, pt_bank, out_bank = map(
            bank, ("xq_bank", "k_bank", "v_bank", "score_bank", "pt_bank", "out_bank"))
        xn_tp, q_p = xq_bank[:, 0:D], xq_bank[:, D:2 * D]
        c_loaded = [sem(f"c_loaded{i}") for i in range(2)]
        (xn_done, xn_tp_done, xn_t_done, q_p_done, k_p_done, v_p_done, v_done, q_t_done, k_t_done,
         scores_done, max_done, exp_done, share_done, pt_p_done, pt_done, out_p_done, x_done) = map(
             sem, ("xn_done", "xn_tp_done", "xn_t_done", "q_p_done", "k_p_done", "v_p_done", "v_done",
                   "q_t_done", "k_t_done", "scores_done", "max_done", "exp_done", "share_done",
                   "pt_p_done", "pt_done", "out_p_done", "x_done"))

        blocks = ctx.enter_context(ExitStack())
        block = blocks.enter_context(nc.Block())

        @block.sync
        def _(sp):
            def load(b, par):
                waits(sp, k_p_done, b - 1)
                src = ctx_t[b] if isinstance(b, int) else \
                    ctx_t[bass.ds(b, 1)].rearrange("a d t -> (a d) t")
                sp.dma_start(c_t[:, par, :, :], src.rearrange("(c p) t -> p c t", p=P)
                             ).then_inc(c_loaded[par], 16)
            load(0, 0)
            load(1, 1)
            with sp.Fori(2, B - 1, 2) as t:
                load(t, 0)
                load(t + 1, 1)

        @block.tensor
        def _(pe):
            for s, n in loads:
                pe.wait_ge(s, n)

            def body(t, phase, live):
                par, other = phase % 2, 1 - phase % 2
                if live(1):
                    b = t - 1
                    pe.wait_ge(xn_done, b + 1)
                    waits(pe, q_t_done, b)
                    for c in range(KC):
                        last = pe.transpose(xn_tp[:, c * S:(c + 1) * S],
                                            xn[:, other, c * P:(c + 1) * P], k.ident[:])
                    last.then_inc(xn_tp_done, 1)
                if live(2):
                    b = t - 2
                    pe.wait_ge(q_t_done, b + 1)
                    pe.wait_ge(k_t_done, b + 1)
                    waits(pe, exp_done, b)
                    for c in range(KC):
                        last = pe.matmul(score_bank[:, 0:S], q_t[:, par, c, :], k_t[:, par, c, :],
                                         start=c == 0, stop=c == KC - 1)
                    last.then_inc(scores_done, 1)
                if live(3):
                    b = t - 3
                    pe.wait_ge(exp_done, b + 1)
                    waits(pe, pt_done, b)
                    pe.transpose(pt_bank[:, 0:S], probs[:, other, :], k.ident[:]).then_inc(pt_p_done, 1)
                if live(1):
                    b = t - 1
                    pe.wait_ge(c_loaded[other], 8 * (b - other) + 16)
                    waits(pe, v_done, b)
                    for c in range(KC):
                        last = pe.matmul(v_bank[:, 0:D], c_t[:, other, c, :], w_in[:, c, 2 * D:3 * D],
                                         start=c == 0, stop=c == KC - 1)
                    last.then_inc(v_p_done, 1)
                    waits(pe, k_t_done, b)
                    for f in range(KC):
                        for c in range(KC):
                            last = pe.matmul(k_bank[:, f * S:(f + 1) * S],
                                             w_in[:, c, D + f * P:D + (f + 1) * P],
                                             c_t[:, other, c, :], start=c == 0, stop=c == KC - 1)
                    last.then_inc(k_p_done, 1)
                    pe.wait_ge(xn_t_done, b + 1)
                    for f in range(KC):
                        for c in range(KC):
                            last = pe.matmul(q_p[:, f * S:(f + 1) * S],
                                             w_in[:, c, f * P:(f + 1) * P], xn_t[:, other, c, :],
                                             start=c == 0, stop=c == KC - 1)
                    last.then_inc(q_p_done, 1)
                if live(3):
                    b = t - 3
                    pe.wait_ge(pt_done, b + 1)
                    pe.wait_ge(v_done, b + 1)
                    waits(pe, x_done, b)
                    pe.matmul(out_bank[:, 0:D], probs_t[:, other, :], v[:, (phase - 3) % 4, :],
                              start=True, stop=True).then_inc(out_p_done, 1)
            pipeline(pe, body, 4, 4)

        @block.vector
        def _(dve):
            def body(t, phase, live):
                par, other = phase % 2, 1 - phase % 2
                if live(2):
                    b = t - 2
                    dve.wait_ge(scores_done, b + 1)
                    waits(dve, exp_done, b - 1)
                    dve.tensor_reduce(neg_max[:, par, :], score_bank[:, 0:S], axis=AX.X, op=ALU.max,
                                      negate=True).then_inc(max_done, 1)
                if live(3):
                    b = t - 3
                    dve.wait_ge(pt_p_done, b + 1)
                    waits(dve, out_p_done, b - 1)
                    dve.tensor_copy(probs_t[:, other, :], pt_bank[:, 0:S]).then_inc(pt_done, 1)
                if live(0):
                    norm_statistics(dve, norm, k, x, t, par)
                if live(1):
                    b = t - 1
                    dve.wait_ge(v_p_done, b + 1)
                    waits(dve, out_p_done, b - 3)
                    dve.tensor_tensor(v[:, (phase - 1) % 4, :], v_bank[:, 0:D], v_bias[:],
                                      ALU.add).then_inc(v_done, 1)
                    dve.wait_ge(q_p_done, b + 1)
                    waits(dve, scores_done, b - 1)
                    for f in range(KC):
                        last = dve.tensor_scalar(q_t[:, other, f, :], q_p[:, f * S:(f + 1) * S],
                                                 q_bias[:, f:f + 1], D ** -0.5, ALU.add, ALU.mult)
                    last.then_inc(q_t_done, 1)
                if live(0):
                    dve.wait_ge(norm.rstd_done, t + 1)
                    waits(dve, xn_tp_done, t - 1)
                    dve.tensor_scalar(xn[:, par, :], seq(x, t), norm.mean_var[:, par, 0:1],
                                      norm.rstd[:, par, :], ALU.subtract, ALU.mult
                                      ).then_inc(xn_done, 1)
                if live(2):
                    b = t - 2
                    dve.wait_ge(exp_done, b + 1)
                    dve.reciprocal(share[:, (phase - 2) % 4, :], total[:, par, :]).then_inc(share_done, 1)
                if live(3):
                    b = t - 3
                    dve.wait_ge(out_p_done, b + 1)
                    dve.wait_ge(share_done, b + 1)
                    dve.scalar_tensor_tensor(seq(x, b), out_bank[:, 0:D], share[:, (phase - 3) % 4, :],
                                             seq(x, b), ALU.mult, ALU.add).then_inc(x_done, 1)
            pipeline(dve, body, 4, 4)

        @block.scalar
        def _(act):
            def body(t, phase, live):
                par, other = phase % 2, 1 - phase % 2
                if live(1):
                    b = t - 1
                    act.wait_ge(xn_tp_done, b + 1)
                    waits(act, q_p_done, b - 1)
                    act.activation(xn_t[:, other, :, :].rearrange("p c t -> p (c t)"),
                                   xn_tp, ACT.Copy).then_inc(xn_t_done, 1)
                if live(2):
                    b = t - 2
                    act.wait_ge(max_done, b + 1)
                    waits(act, pt_p_done, b - 1)
                    waits(act, share_done, b - 1)
                    act.activation(probs[:, par, :], score_bank[:, 0:S], ACT.Exp,
                                   bias=neg_max[:, par, :], accum_out=total[:, par, :]
                                   ).then_inc(exp_done, 1)
                if live(1):
                    b = t - 1
                    act.wait_ge(k_p_done, b + 1)
                    waits(act, scores_done, b - 1)
                    for f in range(KC):
                        last = act.activation(k_t[:, other, f, :], k_bank[:, f * S:(f + 1) * S],
                                              ACT.Identity, bias=k_bias[:, f:f + 1])
                    last.then_inc(k_t_done, 1)
            pipeline(act, body, 4, 4)

        @block.gpsimd
        def _(pool):
            def body(t, phase, live):
                if live(0):
                    norm_rstd(pool, norm, k, t, phase % 2)
            pipeline(pool, body, 4, 4)

        blocks.close()
        clear(nc, sems)


def experts(nc, name, x, k, w_router, router_bias, w_experts, expert_bias, loads):
    with ExitStack() as ctx:
        sems = []
        def sb(n, shape, dt=F32):
            return ctx.enter_context(nc.sbuf_tensor(f"{name}_{n}", shape, dt))

        def bank(n):
            return ctx.enter_context(nc.psum_tensor(f"{name}_{n}", [P, 512], F32))

        def sem(n):
            sems.append(ctx.enter_context(nc.semaphore(f"{name}_{n}")))
            return sems[-1]

        norm = Norm(ctx, nc, name, sem)
        xn = sb("xn", [P, 2, D])
        xn_t = sb("xn_t", [P, 2, KC, S])
        logits = sb("logits", [P, 2, E])
        top = sb("top", [P, 8])
        best = sb("best", [P, 8], U32)
        best_f = sb("best_f", [P, 1])
        neg_max = sb("neg_max", [P, 2, 1])
        powers = sb("powers", [P, 2, E])
        total = sb("total", [P, 2, 1])
        gate = sb("gate", [P, 1])
        weight = sb("weight", [P, 2, E])
        weight_t = sb("weight_t", [E, 2, S])
        xn_bank, router_bank, weight_bank, bias_bank = map(
            bank, ("xn_bank", "router_bank", "weight_bank", "bias_bank"))
        pair_banks = [bank(f"pair{i}") for i in range(4)]
        (xn_done, xn_tp_done, xn_t_done, logits_p_done, logits_done, top_done, best_done, max_done,
         exp_done, best_f_done, gate_done, weight_done, weight_tp_done, weight_t_done, pair_done,
         bias_done, added) = map(sem, (
             "xn_done", "xn_tp_done", "xn_t_done", "logits_p_done", "logits_done", "top_done",
             "best_done", "max_done", "exp_done", "best_f_done", "gate_done", "weight_done",
             "weight_tp_done", "weight_t_done", "pair_done", "bias_done", "added"))

        blocks = ctx.enter_context(ExitStack())
        block = blocks.enter_context(nc.Block())

        @block.tensor
        def _(pe):
            for s, n in loads:
                pe.wait_ge(s, n)

            def body(t, phase, live):
                par, other = phase % 2, 1 - phase % 2
                if live(2):
                    b = t - 2
                    pe.wait_ge(weight_done, b + 1)
                    waits(pe, weight_t_done, b)
                    pe.transpose(weight_bank[0:E, 0:S], weight[:, par, :], k.ident[:]
                                 ).then_inc(weight_tp_done, 1)
                if live(1):
                    b = t - 1
                    pe.wait_ge(xn_done, b + 1)
                    waits(pe, xn_t_done, b)
                    for c in range(KC):
                        last = pe.transpose(xn_bank[:, c * S:(c + 1) * S],
                                            xn[:, other, c * P:(c + 1) * P], k.ident[:])
                    last.then_inc(xn_tp_done, 1)
                if live(2):
                    b = t - 2
                    for i in range(E // 2):
                        waits(pe, added, 9 * b - 9 + 2 * i + 3)
                        for c in range(KC):
                            last = pe.matmul(pair_banks[i][:], xn_t[:, par, c, :],
                                             w_experts[:, c, i * 2 * D:(i + 1) * 2 * D],
                                             start=c == 0, stop=c == KC - 1)
                        last.then_inc(pair_done, 1)
                        if i == 0:
                            pe.wait_ge(weight_t_done, b + 1)
                            waits(pe, added, 9 * b - 8)
                            pe.matmul(bias_bank[:, 0:D], weight_t[:, par, :], expert_bias[:],
                                      start=True, stop=True).then_inc(bias_done, 1)
                if live(1):
                    b = t - 1
                    pe.wait_ge(xn_t_done, b + 1)
                    waits(pe, logits_done, b)
                    for c in range(KC):
                        last = pe.matmul(router_bank[:, 0:E], xn_t[:, other, c, :], w_router[:, c, :],
                                         start=c == 0, stop=c == KC - 1)
                    last.then_inc(logits_p_done, 1)
            pipeline(pe, body, 3, 2)

        @block.vector
        def _(dve):
            def body(t, phase, live):
                par, other = phase % 2, 1 - phase % 2
                if live(0):
                    norm_statistics(dve, norm, k, x, t, par)
                if live(2):
                    b = t - 2
                    dve.wait_ge(weight_tp_done, b + 1)
                    waits(dve, bias_done, b - 1)
                    dve.tensor_copy(weight_t[:, par, :], weight_bank[0:E, 0:S]
                                    ).then_inc(weight_t_done, 1)
                if live(0):
                    dve.wait_ge(norm.rstd_done, t + 1)
                    waits(dve, xn_tp_done, t - 1)
                    dve.tensor_scalar(xn[:, par, :], seq(x, t), norm.mean_var[:, par, 0:1],
                                      norm.rstd[:, par, :], ALU.subtract, ALU.mult
                                      ).then_inc(xn_done, 1)
                if live(2):
                    b = t - 2
                    dve.wait_ge(bias_done, b + 1)
                    dve.tensor_tensor(seq(x, b), bias_bank[:, 0:D], seq(x, b), ALU.add
                                      ).then_inc(added, 1)
                    for e in range(E):
                        if e % 2 == 0:
                            dve.wait_ge(pair_done, 4 * b + e // 2 + 1)
                        dve.wait_ge(added, 9 * b + e + 1)
                        dve.scalar_tensor_tensor(
                            seq(x, b), pair_banks[e // 2][:, e % 2 * D:(e % 2 + 1) * D],
                            weight[:, par, e:e + 1], seq(x, b), ALU.mult, ALU.add
                        ).then_inc(added, 1)
                if live(1):
                    b = t - 1
                    dve.wait_ge(logits_p_done, b + 1)
                    waits(dve, exp_done, b - 1)
                    dve.tensor_tensor(logits[:, other, :], router_bank[:, 0:E], router_bias[:],
                                      ALU.add).then_inc(logits_done, 1)
                    apart(dve, k)
                    dve.wait_ge(logits_done, b + 1)
                    dve.max(top[:], logits[:, other, :]).then_inc(top_done, 1)
                    dve.wait_ge(top_done, b + 1)
                    dve.tensor_scalar(neg_max[:, other, :], top[:, 0:1], -1.0, None, ALU.mult
                                      ).then_inc(max_done, 1)
                    dve.max_index(best[:], top[:], logits[:, other, :]).then_inc(best_done, 1)
                    dve.wait_ge(best_done, b + 1)
                    dve.tensor_copy(best_f[:], best[:, 0:1]).then_inc(best_f_done, 1)
                    dve.wait_ge(exp_done, b + 1)
                    dve.reciprocal(gate[:], total[:, other, :]).then_inc(gate_done, 1)
                    dve.wait_ge(gate_done, b + 1)
                    dve.wait_ge(best_f_done, b + 1)
                    dve.tensor_scalar(weight[:, other, :], k.iota[:], best_f[:], gate[:],
                                      ALU.is_equal, ALU.mult).then_inc(weight_done, 1)
            pipeline(dve, body, 3, 2)

        @block.scalar
        def _(act):
            def body(t, phase, live):
                par, other = phase % 2, 1 - phase % 2
                if live(1):
                    b = t - 1
                    act.wait_ge(xn_tp_done, b + 1)
                    waits(act, pair_done, 4 * b - 4)
                    waits(act, logits_p_done, b - 1)
                    act.activation(xn_t[:, other, :, :].rearrange("p c t -> p (c t)"),
                                   xn_bank[:, 0:D], ACT.Copy).then_inc(xn_t_done, 1)
                    act.wait_ge(max_done, b + 1)
                    waits(act, gate_done, b - 1)
                    act.activation(powers[:, other, :], logits[:, other, :], ACT.Exp,
                                   bias=neg_max[:, other, :], accum_out=total[:, other, :]
                                   ).then_inc(exp_done, 1)
            pipeline(act, body, 3, 2)

        @block.gpsimd
        def _(pool):
            def body(t, phase, live):
                if live(0):
                    norm_rstd(pool, norm, k, t, phase % 2)
            pipeline(pool, body, 3, 2)

        blocks.close()
        clear(nc, sems)


U = 4
UNITS = B // U
UT = U * S


def unit(x, u):
    if isinstance(u, int):
        return x[:, u]
    return x[:, bass.ds(u, 1)].rearrange("p a n -> p (a n)")


def quantised_ffn(nc, name, x, k, w_gate, w_up, w_down, clips, out, loads):
    with ExitStack() as ctx:
        def sb(n, shape, dt=F32, c=ctx):
            return c.enter_context(nc.sbuf_tensor(f"{name}_{n}", shape, dt))

        def bank(n, c, dt=F32):
            return c.enter_context(nc.psum_tensor(f"{name}_{n}", [P, 2048 // (4 if dt == F32 else 2)], dt))

        def sem(n):
            return ctx.enter_context(nc.semaphore(f"{name}_{n}"))

        gate_t = sb("gate_t", [P, KC, I], BF16)
        up_t = sb("up_t", [P, KC, I], BF16)
        down_t = sb("down_t", [P, IC, D], BF16)
        gate_scale = sb("gate_scale", [P, IC])
        up_scale = sb("up_scale", [P, IC])
        down_scale = sb("down_scale", [P, KC])
        down_row = sb("down_row", [P, D])
        sig = sb("sig", [P, 2])
        act_scale = sb("act_scale", [P, 2])
        act_inverse = sb("act_inverse", [P, 2])
        seq_max = sb("seq_max", [P, B])
        row_max = sb("row_max", [P, 2])
        one_max = sb("one_max", [1, 2])
        xn_all = sb("xn_all", [P, UNITS, U * D])

        def whole_max(dve_or_pe, which, src, bank_, maxed, turned, taken, spread):
            if dve_or_pe is nc.vector:
                dve = dve_or_pe
                dve.tensor_reduce(row_max[:, which:which + 1], src, axis=AX.X, op=ALU.max
                                  ).then_inc(maxed, 1)
                dve.wait_ge(turned, 1)
                dve.tensor_reduce(one_max[:, which:which + 1], bank_[0:1, 0:P], axis=AX.X,
                                  op=ALU.max).then_inc(taken, 1)
                dve.wait_ge(spread, 1)
            else:
                pe = dve_or_pe
                pe.wait_ge(maxed, 1)
                pe.transpose(bank_[0:1, 0:P], row_max[:, which:which + 1], k.ident[:]
                             ).then_inc(turned, 1)
                pe.wait_ge(taken, 1)
                pe.matmul(bank_[:, P:P + 1], k.ones[0:1, :], one_max[:, which:which + 1],
                          start=True, stop=True).then_inc(spread, 1)

        with ExitStack() as part:
            norm = Norm(part, nc, name, sem)
            names = ("gate", "up", "down")
            shapes = dict(gate=[P, IC, D], up=[P, IC, D], down=[P, KC, I])
            raw = {n: sb(f"{n}_raw", shapes[n], F32, part) for n in names}
            inverse = {n: sb(f"{n}_inverse", [P, shapes[n][1]], F32, part) for n in names}
            ints = {n: sb(f"{n}_ints", shapes[n], BF16, part) for n in names}
            scale = dict(gate=gate_scale, up=up_scale, down=down_scale)
            diagonal = sb("diagonal", [P, KC, P], F32, part)
            exps = sb("exps", [P, 2], F32, part)
            turn_banks = [bank(f"turn{i}", part, BF16) for i in range(4)]
            row_bank = bank("row_bank", part)
            tails, chain, sig_exp, ints_done, turned, copied, diag_done, row_done, \
                xn_done, xn_maxed, x_maxed, x_turned, x_taken, x_spread = map(sem, (
                    "tails", "chain", "sig_exp", "ints_done", "turned", "copied",
                    "diag_done", "row_done", "xn_done", "xn_maxed", "x_maxed", "x_turned", "x_taken", "x_spread"))
            last_rows = rows(IC - 1)
            block = part.enter_context(nc.Block())
            w_loads = [sem(f"w_loaded{i}") for i in range(5)]

            turns = []
            for n, dst in (("gate", gate_t), ("up", up_t)):
                for c in range(IC):
                    for h in range(KC):
                        turns.append((n, c, h * P, rows(c), P, dst[:, h, c * P:c * P + rows(c)]))
            for c in range(KC):
                for i in range(IC):
                    turns.append(("down", c, i * P, P, rows(i), down_t[0:rows(i), i, c * P:(c + 1) * P]))

            @block.sync
            def _(sp):
                sp.wait_ge(tails, 2)
                for n, src, i in (("gate", w_gate, 0), ("up", w_up, 2)):
                    full = (IC - 1) * P
                    sp.dma_start(raw[n][:, 0:IC - 1, :],
                                 src[0:full, :].rearrange("(c p) h -> p c h", p=P)
                                 ).then_inc(w_loads[i], 16)
                    sp.dma_start(raw[n][0:last_rows, IC - 1, :], src[full:I, :]
                                 ).then_inc(w_loads[i + 1], 16)
                sp.dma_start(raw["down"][:], w_down.rearrange("(c p) i -> p c i", p=P)
                             ).then_inc(w_loads[4], 16)

            @block.gpsimd
            def _(pool):
                for n in ("gate", "up"):
                    pool.memset(raw[n][last_rows:P, IC - 1, :], 1.0).then_inc(tails, 1)

                def body(b, par, live):
                    norm_rstd(pool, norm, k, b, par)
                pipeline(pool, body, 1, 2)

            @block.scalar
            def _(act):
                act.activation(exps[:], clips[:], ACT.Exp, scale=-1.0).then_inc(sig_exp, 1)
                for i, (n, c, at, r, w, dst) in enumerate(turns):
                    act.wait_ge(turned, i + 1)
                    act.activation(dst, turn_banks[i % 4][0:w, 0:r], ACT.Copy).then_inc(copied, 1)

            @block.tensor
            def _(pe):
                for i, (n, c, at, r, w, dst) in enumerate(turns):
                    pe.wait_ge(ints_done, names.index(n) + 1)
                    waits(pe, copied, i - 3)
                    pe.transpose(turn_banks[i % 4][0:w, 0:r], ints[n][0:r, c, at:at + w],
                                 k.ident_bf[0:r, 0:r]).then_inc(turned, 1)
                pe.wait_ge(diag_done, KC)
                for c in range(KC):
                    last = pe.matmul(row_bank[:, c * P:(c + 1) * P], k.ones[:], diagonal[:, c, :],
                                     start=True, stop=True)
                last.then_inc(row_done, 1)
                whole_max(pe, 0, None, row_bank[:, D:2 * D], x_maxed, x_turned, x_taken, x_spread)

            @block.vector
            def _(dve):
                steps = [0]

                def step(instruction):
                    steps[0] += 1
                    instruction.then_inc(chain, 1)
                    dve.wait_ge(chain, steps[0])

                for number, n in enumerate(names):
                    for i in ((0, 1), (2, 3), (4,))[number]:
                        dve.wait_ge(w_loads[i], 16)
                    chunks = shapes[n][1]
                    step(dve.tensor_reduce(scale[n][:], raw[n][:], axis=AX.X, op=ALU.max,
                                           apply_absolute_value=True))
                    step(dve.tensor_scalar(scale[n][:], scale[n][:], 1.0 / QMAX, None, ALU.mult))
                    step(dve.reciprocal(inverse[n][:], scale[n][:]))
                    for c in range(chunks):
                        last = dve.tensor_scalar(raw[n][:, c, :], raw[n][:, c, :],
                                                 inverse[n][:, c:c + 1], ROUND, ALU.mult, ALU.add)
                    step(last)
                    step(dve.tensor_scalar(raw[n][:], raw[n][:], ROUND - QMAX - 1.0, ROUND + QMAX,
                                           ALU.max, ALU.min))
                    dve.tensor_scalar(ints[n][:], raw[n][:], -ROUND, None, ALU.add
                                      ).then_inc(ints_done, 1)
                for c in range(KC):
                    dve.tensor_scalar(diagonal[:, c, :], k.ident[:], down_scale[:, c:c + 1], None,
                                      ALU.mult).then_inc(diag_done, 1)
                dve.wait_ge(sig_exp, 1)
                step(dve.tensor_scalar(exps[:], exps[:], 1.0, None, ALU.add))
                step(dve.reciprocal(sig[:], exps[:]))

                def body(b, par, live):
                    norm_statistics(dve, norm, k, x, b, par)
                    dve.wait_ge(norm.rstd_done, b + 1)
                    flat = xn_all[:].rearrange("p u (s d) -> p (u s) d", d=D)
                    dve.tensor_scalar(seq(flat, b), seq(x, b), norm.mean_var[:, par, 0:1],
                                      norm.rstd[:, par, :], ALU.subtract, ALU.mult
                                      ).then_inc(xn_done, 1)
                    dve.wait_ge(xn_done, b + 1)
                    dst = seq_max[:, b:b + 1] if isinstance(b, int) else seq_max[:, bass.ds(b, 1)]
                    dve.tensor_reduce(dst, seq(flat, b), axis=AX.X, op=ALU.max,
                                      apply_absolute_value=True).then_inc(xn_maxed, 1)
                pipeline(dve, body, 1, 2)
                dve.wait_ge(row_done, 1)
                step(dve.tensor_copy(down_row[:], row_bank[:, 0:D]))
                dve.wait_ge(xn_maxed, B)
                whole_max(dve, 0, seq_max[:], row_bank[:, D:2 * D], x_maxed, x_turned, x_taken,
                          x_spread)
                step(dve.tensor_scalar(act_scale[:, 0:1], row_bank[:, D + P:D + P + 1], sig[:, 0:1],
                                       1.0 / QMAX, ALU.mult, ALU.mult))
                step(dve.reciprocal(act_inverse[:, 0:1], act_scale[:, 0:1]))
                dve.tensor_scalar(gate_scale[:], gate_scale[:], act_scale[:, 0:1], None, ALU.mult)
                step(dve.tensor_scalar(up_scale[:], up_scale[:], act_scale[:, 0:1], None, ALU.mult))
                assert steps[0] < 200

        hidden = sb("hidden", [P, UNITS, IC * UT])
        hidden_max = sb("hidden_max", [P, UNITS * IC])
        rounded = sb("rounded", [P, U * D])

        with ExitStack() as part:
            x_ints = sb("x_ints", [P, 2, U, D], BF16, part)
            x_ints_t = sb("x_ints_t", [P, 2, KC, UT], BF16, part)
            silu = sb("silu", [P, 2, UT], F32, part)
            turn_bank = bank("x_turn", part, BF16)
            gate_banks = [bank(f"gate_bank{i}", part) for i in range(2)]
            up_banks = [bank(f"up_bank{i}", part) for i in range(2)]
            max_bank = bank("max_bank", part)
            (zeroed, scaled, clipped, x_ints_done, x_turned2, x_ints_t_done, gate_done, up_done,
             silu_done, hidden_done, hidden_maxed, h_maxed, h_turned, h_taken, h_spread, sc) = map(
                 sem, ("zeroed", "scaled", "clipped", "x_ints_done", "x_turned2", "x_ints_t_done",
                       "gate_done", "up_done", "silu_done", "hidden_done", "hidden_maxed",
                       "h_maxed", "h_turned", "h_taken", "h_spread", "sc"))
            block = part.enter_context(nc.Block())

            @block.tensor
            def _(pe):
                def body(t, par, live):
                    other = 1 - par
                    if live(1):
                        u = t - 1
                        pe.wait_ge(x_ints_done, u + 1)
                        waits(pe, x_ints_t_done, u)
                        for c in range(KC):
                            for s in range(U):
                                last = pe.transpose(turn_bank[:, c * UT + s * S:c * UT + (s + 1) * S],
                                                    x_ints[:, other, s, c * P:(c + 1) * P],
                                                    k.ident_bf[:])
                        last.then_inc(x_turned2, 1)
                    if live(2):
                        u = t - 2
                        pe.wait_ge(x_ints_t_done, u + 1)
                        for i in range(IC):
                            n = IC * u + i
                            for w_t, banks, freed, done in (
                                    (gate_t, gate_banks, silu_done, gate_done),
                                    (up_t, up_banks, hidden_done, up_done)):
                                waits(pe, freed, n - 1)
                                for c in range(KC):
                                    last = pe.matmul(banks[i % 2][0:rows(i), :],
                                                     w_t[:, c, i * P:i * P + rows(i)],
                                                     x_ints_t[:, par, c, :],
                                                     start=c == 0, stop=c == KC - 1)
                                last.then_inc(done, 1)
                pipeline(pe, body, 3, 2, UNITS)
                whole_max(pe, 1, None, max_bank, h_maxed, h_turned, h_taken, h_spread)

            @block.scalar
            def _(act):
                def body(t, par, live):
                    other = 1 - par
                    if live(1):
                        u = t - 1
                        act.wait_ge(x_turned2, u + 1)
                        waits(act, up_done, IC * (u - 1))
                        act.activation(x_ints_t[:, other, :, :].rearrange("p c t -> p (c t)"),
                                       turn_bank[:], ACT.Copy).then_inc(x_ints_t_done, 1)
                    if live(2):
                        u = t - 2
                        for i in range(IC):
                            n = IC * u + i
                            act.wait_ge(gate_done, n + 1)
                            waits(act, hidden_done, n - 1)
                            act.activation(silu[0:rows(i), i % 2, :], gate_banks[i % 2][0:rows(i), :],
                                           ACT.Silu, scale=gate_scale[0:rows(i), i:i + 1]
                                           ).then_inc(silu_done, 1)
                pipeline(act, body, 3, 2, UNITS)

            @block.vector
            def _(dve):
                dve.memset(hidden_max[:], 0.0).then_inc(zeroed, 1)
                dve.wait_ge(zeroed, 1)

                def body(t, par, live):
                    if live(0):
                        waits(dve, x_ints_done, t)
                        dve.tensor_scalar(rounded[:], unit(xn_all, t), act_inverse[:, 0:1], ROUND,
                                          ALU.mult, ALU.add).then_inc(scaled, 1)
                        dve.wait_ge(scaled, t + 1)
                        dve.tensor_scalar(rounded[:], rounded[:], ROUND - QMAX - 1.0, ROUND + QMAX,
                                          ALU.max, ALU.min).then_inc(clipped, 1)
                        dve.wait_ge(clipped, t + 1)
                        waits(dve, x_turned2, t - 1)
                        dve.tensor_scalar(x_ints[:, par, :, :].rearrange("p s d -> p (s d)"),
                                          rounded[:], -ROUND, None, ALU.add).then_inc(x_ints_done, 1)
                    if live(2):
                        u = t - 2
                        for i in range(IC):
                            n = IC * u + i
                            r = rows(i)
                            if isinstance(u, int):
                                dst = hidden[0:r, u, i * UT:(i + 1) * UT]
                                peak = hidden_max[0:r, n:n + 1]
                            else:
                                dst = hidden[0:r, bass.ds(u, 1), i * UT:(i + 1) * UT].rearrange(
                                    "p a n -> p (a n)")
                                peak = hidden_max[0:r, bass.ds(n, 1)]
                            dve.wait_ge(up_done, n + 1)
                            dve.wait_ge(silu_done, n + 1)
                            dve.scalar_tensor_tensor(dst, up_banks[i % 2][0:r, :],
                                                     up_scale[0:r, i:i + 1], silu[0:r, i % 2, :],
                                                     ALU.mult, ALU.mult).then_inc(hidden_done, 1)
                            dve.wait_ge(hidden_done, n + 1)
                            dve.tensor_reduce(peak, dst, axis=AX.X, op=ALU.max,
                                              apply_absolute_value=True).then_inc(hidden_maxed, 1)
                pipeline(dve, body, 3, 2, UNITS)
                dve.wait_ge(hidden_maxed, UNITS * IC)
                whole_max(dve, 1, hidden_max[:], max_bank, h_maxed, h_turned, h_taken, h_spread)
                dve.tensor_scalar(act_scale[:, 1:2], max_bank[:, P:P + 1], sig[:, 1:2], 1.0 / QMAX,
                                  ALU.mult, ALU.mult).then_inc(sc, 1)
                dve.wait_ge(sc, 1)
                dve.reciprocal(act_inverse[:, 1:2], act_scale[:, 1:2])
                dve.tensor_scalar(down_row[:], down_row[:], act_scale[:, 1:2], None, ALU.mult
                                  ).then_inc(sc, 1)
                dve.wait_ge(sc, 2)

        with ExitStack() as part:
            h_round = sb("h_round", [P, IC * UT], F32, part)
            h_ints = sb("h_ints", [P, 2, IC * UT], BF16, part)
            addend = sb("addend", [P, 2, D], F32, part)
            out_banks = [bank(f"out{i}", part) for i in range(4)]
            h_scaled, h_clipped, h_ints_done, down_done, addend_done, x_done = map(sem, (
                "h_scaled", "h_clipped", "h_ints_done", "down_done", "addend_done", "x_done"))
            stored = [sem(f"stored{i}") for i in range(UNITS)]
            block = part.enter_context(nc.Block())
            full = (IC - 1) * UT
            parts = ((P, 0, full), (rows(IC - 1), full, IC * UT))

            @block.vector
            def _(dve):
                def body(t, par, live):
                    if live(0):
                        waits(dve, h_ints_done, 2 * t)
                        for i, (r, lo, hi) in enumerate(parts):
                            src = hidden[0:r, t, lo:hi] if isinstance(t, int) else \
                                hidden[0:r, bass.ds(t, 1), lo:hi].rearrange("p a n -> p (a n)")
                            dve.tensor_scalar(h_round[0:r, lo:hi], src, act_inverse[0:r, 1:2], ROUND,
                                              ALU.mult, ALU.add).then_inc(h_scaled, 1)
                        for i, (r, lo, hi) in enumerate(parts):
                            dve.wait_ge(h_scaled, 2 * t + i + 1)
                            dve.tensor_scalar(h_round[0:r, lo:hi], h_round[0:r, lo:hi],
                                              ROUND - QMAX - 1.0, ROUND + QMAX, ALU.max, ALU.min
                                              ).then_inc(h_clipped, 1)
                    if live(1):
                        u = t - 1
                        for s in range(U):
                            n = U * u + s
                            dve.wait_ge(down_done, n + 1)
                            waits(dve, x_done, n - 1)
                            dve.tensor_tensor(addend[:, s % 2, :], out_banks[s][:, 0:D], down_row[:],
                                              ALU.mult).then_inc(addend_done, 1)
                pipeline(dve, body, 2, 2, UNITS)

            @block.scalar
            def _(act):
                def body(t, par, live):
                    if live(0):
                        waits(act, down_done, U * (t - 1))
                        for i, (r, lo, hi) in enumerate(parts):
                            act.wait_ge(h_clipped, 2 * t + i + 1)
                            act.activation(h_ints[0:r, par, lo:hi], h_round[0:r, lo:hi], ACT.Copy,
                                           bias=-ROUND).then_inc(h_ints_done, 1)
                pipeline(act, body, 1, 2, UNITS)

            @block.tensor
            def _(pe):
                def body(t, par, live):
                    pe.wait_ge(h_ints_done, 2 * t + 2)
                    for s in range(U):
                        waits(pe, addend_done, U * (t - 1) + s + 1)
                        for i in range(IC):
                            at = i * UT + s * S
                            last = pe.matmul(out_banks[s][:, 0:D], h_ints[0:rows(i), par, at:at + S],
                                             down_t[0:rows(i), i, :], start=i == 0, stop=i == IC - 1)
                        last.then_inc(down_done, 1)
                pipeline(pe, body, 1, 2, UNITS)

            @block.gpsimd
            def _(pool):
                def body(t, par, live):
                    for s in range(U):
                        n = U * t + s
                        pool.wait_ge(addend_done, n + 1)
                        pool.tensor_tensor(seq(x, n), seq(x, n), addend[:, s % 2, :], ALU.add
                                           ).then_inc(x_done, 1)
                pipeline(pool, body, 1, 2, UNITS)

            @block.sync
            def _(sp):
                for u in range(UNITS):
                    sp.wait_ge(x_done, U * (u + 1))
                    sp.dma_start(out[U * u:U * u + U].rearrange("b t d -> t b d"),
                                 x[:, U * u:U * u + U, :]).then_inc(stored[u], 16)
                for u in range(UNITS):
                    sp.wait_ge(stored[u], 16)


class Constants:
    pass


def decoder(nc, a, out):
    with ExitStack() as ctx:
        def sb(n, shape, dt=F32, c=ctx):
            return c.enter_context(nc.sbuf_tensor(n, shape, dt))

        def sem(n):
            return ctx.enter_context(nc.semaphore(n))

        x = sb("x_all", [P, B, D])
        k = Constants()
        k.ident = sb("ident", [P, P])
        k.ident_bf = sb("ident_bf", [P, P], BF16)
        k.ones = sb("ones", [P, P])
        k.minus_half = sb("minus_half", [P, 2 * H])
        k.even_rows = sb("even_rows", [P, 1])
        k.odd_rows = sb("odd_rows", [P, 1])
        k.eps = sb("eps", [P, 1])
        k.rms_eps = sb("rms_eps", [P, 2 * H])
        k.iota = sb("iota", [P, E])
        clips = sb("clips", [P, 2])
        x_loaded = [sem("x_loaded0"), sem("x_loaded1")]
        k.x_chunks = []
        k.constants_done = sem("constants_done")

        with ExitStack() as early:
            def big(n, shape, dt=F32):
                return sb(n, shape, dt, early)

            causal = big("causal", [P, S], BF16)
            window = big("window", [P, S], BF16)
            l0_rope = big("l0_rope", [P, 4 * HD])
            l1_rope = big("l1_rope", [P, B, 4 * HD])
            weights, loaded = {}, {}
            for n, shape in (("L0_attn_w_in", [P, KC, 3 * D]), ("L0_attn_w_out", [P, KC, D]),
                             ("L0_xattn_w_in", [P, KC, 3 * D]), ("L0_router", [P, KC, E]),
                             ("L0_experts", [P, KC, E * D]), ("L1_attn_w_in", [P, KC, 3 * D]),
                             ("L1_attn_w_out", [P, KC, D]), ("L1_xattn_w_in", [P, KC, 3 * D]),
                             ("L1_xattn_w_out", [P, KC, D])):
                weights[n] = big(f"{n}_sb", shape)
                loaded[n] = (sem(f"{n}_loaded"), 16)
            rows_of = {}
            for n, width in (("L0_attn_bias", 3 * D), ("L0_attn_bo", D), ("L0_xattn_bv", D),
                             ("L0_router_b", E)):
                rows_of[n] = big(f"{n}_sb", [P, width])
            l0_xattn_bq = big("l0_xattn_bq", [P, KC])
            l0_xattn_bk = big("l0_xattn_bk", [P, KC])
            expert_bias = big("expert_bias", [E, D])

            with ExitStack() as part:
                causal_f = sb("causal_f", [P, S], F32, part)
                window_f = sb("window_f", [P, S], F32, part)
                scale = sb("l0_scale", [P, 1], F32, part)
                pos = sb("pos", [P, B], F32, part)
                freq = sb("freq", [P, HD // 2], F32, part)
                norm_w = sb("norm_w", [P, 2, HD], F32, part)
                angle = sb("angle", [P, B, HD // 2], F32, part)
                turns = sb("turns", [P, B, HD // 2], F32, part)
                cosine = sb("cosine", [P, B, HD // 2], F32, part)
                sine = sb("sine", [P, B, HD // 2], F32, part)
                minus_sine = sb("minus_sine", [P, B, HD // 2], F32, part)
                small = [sem(f"small{i}") for i in range(17)]
                sin_angle, cos_angle, sin_done, chain = map(sem, ("sin_angle", "cos_angle",
                                                                   "sin_done", "setup_chain"))
                block = part.enter_context(nc.Block())

                def spread(row, width):
                    return row.rearrange("(a n) -> a n", a=1).broadcast_to([P, width])

                smalls = [(k.ident[:], a["ident"]), (causal_f[:], a["causal"]),
                          (window_f[:], a["window"]), (k.even_rows[:], a["even_rows"]),
                          (k.odd_rows[:], a["odd_rows"]), (k.iota[:], a["iota"]),
                          (l0_rope[:], a["l0_rope"]), (freq[:], a["freq"]),
                          (pos[:], a["pos_t"]), (scale[:], spread(a["L0_scale"], 1)),
                          (norm_w[:, 0, :], spread(a["L1_q_norm"], HD)),
                          (norm_w[:, 1, :], spread(a["L1_k_norm"], HD)),
                          (clips[:, 0:1], spread(a["clip_x"], 1)),
                          (clips[:, 1:2], spread(a["clip_down"], 1)),
                          (l0_xattn_bq[:], a["L0_xattn_bq"]),
                          (l0_xattn_bk[:], a["L0_xattn_bk"]),
                          (expert_bias[:], a["L0_expert_b"])]
                row_loads = [sem(f"row{i}") for i in range(4)]

                @block.sync
                def _(sp):
                    for n in ("L0_attn_w_in", "L0_attn_w_out"):
                        sp.dma_start(weights[n][:], a[n].rearrange("(c p) n -> p c n", p=P)
                                     ).then_inc(loaded[n][0], 16)
                    sp.dma_start(x[:, 0:4, :], a["x"][0:4].rearrange("b t d -> t b d")
                                 ).then_inc(x_loaded[0], 16)
                    for i, (n, row) in enumerate(rows_of.items()):
                        sp.dma_start(row[:], spread(a[n], row.shape[1])).then_inc(row_loads[i], 16)
                    sp.dma_start(x[:, 4:B, :], a["x"][4:B].rearrange("b t d -> t b d")
                                 ).then_inc(x_loaded[1], 16)
                    for n in list(weights)[2:]:
                        src = a[n].rearrange("(c p) n -> p c n", p=P)
                        sp.dma_start(weights[n][:], src).then_inc(loaded[n][0], 16)

                @block.scalar
                def _(act):
                    for i, (dst, src) in enumerate(smalls):
                        act.dma_start(dst, src).then_inc(small[i], 16)
                    act.wait_ge(sin_angle, 1)
                    act.activation(sine[:], angle[:], ACT.Sin).then_inc(sin_done, 1)
                    act.wait_ge(cos_angle, 1)
                    act.activation(cosine[:], turns[:], ACT.Sin).then_inc(sin_done, 1)

                @block.vector
                def _(dve):
                    steps = [0]

                    def step(instruction):
                        steps[0] += 1
                        instruction.then_inc(chain, 1)
                        dve.wait_ge(chain, steps[0])

                    dve.memset(k.ones[:], 1.0)
                    dve.memset(k.minus_half[:], -0.5)
                    dve.memset(k.eps[:], EPS)
                    dve.memset(k.rms_eps[:], HD * RMS_EPS)
                    for s in small:
                        dve.wait_ge(s, 16)
                    for s in row_loads:
                        dve.wait_ge(s, 16)
                    dve.tensor_copy(k.ident_bf[:], k.ident[:])
                    dve.tensor_copy(causal[:], causal_f[:])
                    dve.tensor_copy(window[:], window_f[:])
                    for lo in (0, 2 * HD):
                        dve.tensor_scalar(l0_rope[:, lo:lo + HD], l0_rope[:, lo:lo + HD], scale[:],
                                          None, ALU.mult)
                    dve.tensor_scalar(norm_w[:, 1, :], norm_w[:, 1, :], HD ** 0.5, None, ALU.mult)
                    step(dve.tensor_tensor(angle[:], pos[:, :, None].broadcast_to([P, B, HD // 2]),
                                           freq[:, None, :].broadcast_to([P, B, HD // 2]), ALU.mult))
                    step(dve.tensor_scalar(turns[:], angle[:], 1.0 / TWO_PI, ROUND, ALU.mult, ALU.add))
                    step(dve.tensor_scalar(turns[:], turns[:], -ROUND, None, ALU.add))
                    for part_of in PI_PARTS:
                        step(dve.scalar_tensor_tensor(angle[:], turns[:], -part_of, angle[:],
                                                      ALU.mult, ALU.add))
                    dve.tensor_scalar(angle[:], angle[:], -PI_BELOW, PI_BELOW, ALU.max, ALU.min
                                      ).then_inc(sin_angle, 1)
                    dve.wait_ge(sin_angle, 1)
                    step(dve.tensor_scalar(minus_sine[:], angle[:], PI_BELOW / 2, -TWO_PI, ALU.is_gt,
                                           ALU.mult))
                    step(dve.tensor_scalar(turns[:], angle[:], float(np.pi / 2), None, ALU.add))
                    step(dve.tensor_tensor(turns[:], turns[:], minus_sine[:], ALU.add))
                    dve.tensor_scalar(turns[:], turns[:], -PI_BELOW, PI_BELOW, ALU.max, ALU.min
                                      ).then_inc(cos_angle, 1)
                    dve.wait_ge(sin_done, 2)
                    step(dve.tensor_scalar(minus_sine[:], sine[:], -1.0, None, ALU.mult))
                    half = HD // 2
                    for which in range(2):
                        for f in range(2):
                            w = norm_w[:, which, f * half:(f + 1) * half]
                            v = norm_w[:, which, (1 - f) * half:(2 - f) * half]
                            at = which * HD + f * half
                            dve.tensor_tensor(l1_rope[:, :, at:at + half], cosine[:],
                                              w[:, None, :].broadcast_to([P, B, half]), ALU.mult)
                            last = dve.tensor_tensor(
                                l1_rope[:, :, 2 * HD + at:2 * HD + at + half],
                                (minus_sine, sine)[f][:],
                                v[:, None, :].broadcast_to([P, B, half]), ALU.mult)
                    last.then_inc(k.constants_done, 1)

            k.x_chunks = [(s, 16) for s in x_loaded]
            w = weights
            heads_attention(nc, "l0a", x, k, w["L0_attn_w_in"], w["L0_attn_w_out"],
                            qkv_bias=rows_of["L0_attn_bias"], out_bias=rows_of["L0_attn_bo"],
                            mask=causal, rope=l0_rope,
                            loads=[loaded["L0_attn_w_in"], loaded["L0_attn_w_out"]])
            k.x_chunks = []
            context_attention(nc, "l0x", x, k, w["L0_xattn_w_in"], l0_xattn_bq, l0_xattn_bk,
                              rows_of["L0_xattn_bv"], a["ctx_t"], [loaded["L0_xattn_w_in"]])
            experts(nc, "l0f", x, k, w["L0_router"], rows_of["L0_router_b"], w["L0_experts"],
                    expert_bias, [loaded["L0_router"], loaded["L0_experts"]])
            heads_attention(nc, "l1a", x, k, w["L1_attn_w_in"], w["L1_attn_w_out"], mask=window,
                            scale=HD ** -0.5,
                            loads=[loaded["L1_attn_w_in"], loaded["L1_attn_w_out"]])
            heads_attention(nc, "l1x", x, k, w["L1_xattn_w_in"], w["L1_xattn_w_out"],
                            batch_rope=l1_rope, ctx_t=a["ctx_t"],
                            loads=[loaded["L1_xattn_w_in"], loaded["L1_xattn_w_out"]])
        quantised_ffn(nc, "l1f", x, k, a["w_gate"], a["w_up"], a["w_down"], clips, out, [])


PI_PARTS = [6.28125, float(np.float32(0.0019350051879882812)),
            float(TWO_PI - 6.28125 - np.float32(0.0019350051879882812))]
PI_BELOW = float(np.nextafter(np.float32(np.pi), np.float32(0)))


def constants():
    half = HD // 2
    freq = (10000.0 ** (-np.arange(0, HD, 2, dtype=np.float32) / np.float32(HD))).astype(np.float32)
    angle = (np.arange(S, dtype=np.float32)[:, None] * freq).astype(np.float32).astype(np.float64)
    cos, sin = np.cos(angle), np.sin(angle)
    rope = np.concatenate([cos, cos, cos, cos, -sin, sin, -sin, sin], 1).astype(np.float32)
    q, key = np.arange(S)[:, None], np.arange(S)[None, :]
    odd = (np.arange(P) // HD % 2).astype(np.float32)[:, None]
    return {
        "ident": np.eye(P, dtype=np.float32),
        "causal": np.where(key > q, NEG, 0.0).astype(np.float32),
        "window": np.where((key > q) | (key <= q - 64), NEG, 0.0).astype(np.float32),
        "even_rows": np.ascontiguousarray(1 - odd), "odd_rows": np.ascontiguousarray(odd),
        "iota": np.ascontiguousarray(np.broadcast_to(np.arange(E, dtype=np.float32), (P, E))),
        "l0_rope": rope, "freq": np.ascontiguousarray(np.broadcast_to(freq, (P, half))),
    }


def kernel(**inputs):
    import numpy as _np
    import concourse.bacc as _bacc
    from concourse import mybir as _mybir
    from concourse.bass_utils import run_bass_kernel_spmd as _run

    i = {n: _np.asarray(v) for n, v in inputs.items()}
    order = _np.arange(D).reshape(H, HD // 2, 2).transpose(0, 2, 1).reshape(D)
    arrays = {
        "x": i["x"], "ctx_t": i["ctx_1024"].transpose(0, 2, 1), "pos_t": i["fside_BxS2_0"].T,
        "L0_attn_w_in": _np.concatenate([i["L0_attn_Wq"][order].T, i["L0_attn_Wk"][order].T,
                                         i["L0_attn_Wv"].T], 1),
        "L0_attn_w_out": i["L0_attn_Wo"].T,
        "L0_attn_bias": _np.concatenate([i["L0_attn_bq"][order], i["L0_attn_bk"][order],
                                         i["L0_attn_bv"]]),
        "L0_attn_bo": i["L0_attn_bo"], "L0_scale": i["L0_attn_scale"],
        "L0_xattn_w_in": _np.concatenate([i["L0_xattn_Wq_w"].T, i["L0_xattn_Wk_w"].T,
                                          i["L0_xattn_Wv_w"].T], 1),
        "L0_xattn_bq": i["L0_xattn_Wq_b"].reshape(KC, P).T,
        "L0_xattn_bk": i["L0_xattn_Wk_b"].reshape(KC, P).T,
        "L0_xattn_bv": i["L0_xattn_Wv_b"],
        "L0_router": i["L0_ffn_router_w"], "L0_router_b": i["L0_ffn_router_b"],
        "L0_experts": i["L0_ffn_expert_w"].transpose(1, 0, 2).reshape(D, E * D),
        "L0_expert_b": i["L0_ffn_expert_b"],
        "L1_attn_w_in": i["L1_attn_W_qkv"], "L1_attn_w_out": i["L1_attn_W_out"],
        "L1_xattn_w_in": _np.concatenate([i["L1_xattn_Wq"], i["L1_xattn_Wkv"]], 1),
        "L1_xattn_w_out": i["L1_xattn_Wo"],
        "L1_q_norm": i["L1_xattn_q_norm_w"], "L1_k_norm": i["L1_xattn_k_norm_w"],
        "clip_x": i["L1_ffn_clip_x"], "clip_down": i["L1_ffn_clip_down"],
        "w_gate": i["L1_ffn_w_gate"], "w_up": i["L1_ffn_w_up"], "w_down": i["L1_ffn_w_down"],
        **constants(),
    }
    nc = _bacc.Bacc("TRN2", target_bir_lowering=False, num_devices=1)
    launched, aps = {}, {}
    for name, value in arrays.items():
        value = _np.ascontiguousarray(value)
        launched[f"in_{name}"] = value
        aps[name] = nc.dram_tensor(f"in_{name}", value.shape, _mybir.dt.from_np(value.dtype),
                                   kind="ExternalInput").ap()
    out = nc.dram_tensor("out", (B, S, D), _mybir.dt.float32, kind="ExternalOutput").ap()
    decoder(nc, aps, out)
    r = _run(nc, [launched], core_ids=[0])
    return r.results[0]["out"]
```

```python
import numpy as np
import concourse.bass as bass
from concourse import mybir
from contextlib import ExitStack

F32 = mybir.dt.float32
BF16 = mybir.dt.bfloat16
U32 = mybir.dt.uint32
ALU = mybir.AluOpType
ACT = mybir.ActivationFunctionType
AX = mybir.AxisListType

B, S, D = 32, 128, 256
P = 128
KC = D // P
H, HD = 16, 16
HG = 4
E = 8
I = 704
IC = -(-I // P)
EPS = 1e-5
RMS_EPS = float(np.finfo(np.float32).eps)
QMAX = 127.0
ROUND = 1.5 * 2.0 ** 23
TWO_PI = 2.0 * np.pi
NEG = -1e30


def rows(c):
    return min(P, I - c * P)


def waits(eng, sem, value):
    if isinstance(value, int) and value <= 0:
        return
    eng.wait_ge(sem, value)


def pipeline(eng, body, depth, turn=2, count=B):
    last = count + depth - 1
    head = 1 + turn if turn > 2 else 2 * turn
    steady = (count - head) // turn * turn
    for t in range(head):
        body(t, t % turn, lambda s, t=t: 0 <= t - s < count)
    with eng.Fori(head, head + steady - turn + 1, turn) as t:
        for i in range(turn):
            body(t + i, (head + i) % turn, lambda s: True)
    for t in range(head + steady, last):
        body(t, t % turn, lambda s, t=t: 0 <= t - s < count)


def apart(eng, k):
    eng.wait_ge(k.constants_done, 1)


def clear(nc, sems):
    with nc.Block() as block:
        @block.gpsimd
        def _(pool):
            for s in sems:
                pool.sem_clear(s)


def seq(x, b):
    if isinstance(b, int):
        return x[:, b, :]
    return x[:, bass.ds(b, 1), :].rearrange("p a d -> p (a d)")


def head_rows(h):
    return h // 8, h % 8 // 2, h % 2


def group_heads(g):
    return [8 * c + 2 * g + half for c in range(2) for half in range(2)]


class Norm:

    def __init__(self, ctx, nc, name, sem):
        self.stats = ctx.enter_context(nc.sbuf_tensor(f"{name}_stats", [P, 2, 6], F32))
        self.mean_var = ctx.enter_context(nc.sbuf_tensor(f"{name}_mean_var", [P, 2, 2], F32))
        self.var_eps = ctx.enter_context(nc.sbuf_tensor(f"{name}_var_eps", [P, 2, 1], F32))
        self.rstd = ctx.enter_context(nc.sbuf_tensor(f"{name}_rstd", [P, 2, 1], F32))
        self.mean_done = sem("mean_done")
        self.eps_added = sem("eps_added")
        self.rstd_done = sem("rstd_done")


def norm_statistics(dve, n, k, x, b, par):
    waits(dve, n.rstd_done, b - 1)
    dve.bn_stats(n.stats[:, par, :], seq(x, b))
    dve.drain()
    dve.bn_aggr(n.mean_var[:, par, :], n.stats[:, par, :]).then_inc(n.mean_done, 1)


def norm_rstd(pool, n, k, b, par):
    pool.wait_ge(n.mean_done, b + 1)
    pool.tensor_tensor(n.var_eps[:, par, :], n.mean_var[:, par, 1:2], k.eps[:, 0:1], ALU.add).then_inc(n.eps_added, 1)
    pool.wait_ge(n.eps_added, b + 1)
    pool.tensor_tensor(n.rstd[:, par, :], n.var_eps[:, par, :], k.minus_half[:, 0:1],
                       ALU.pow).then_inc(n.rstd_done, 1)


def heads_attention(nc, name, x, k, w_in, w_out, qkv_bias=None, out_bias=None, mask=None,
                    rope=None, batch_rope=None, ctx_t=None, scale=1.0, loads=(),
                    x_arrives={}):
    SC = 2 if rope is None and batch_rope is None else 3
    QT, WV, OUT = SC - 1, SC + 1, SC + 2
    with ExitStack() as ctx:
        sems = []
        def sb(n, shape, dt=F32):
            return ctx.enter_context(nc.sbuf_tensor(f"{name}_{n}", shape, dt))

        def bank(n):
            return ctx.enter_context(nc.psum_tensor(f"{name}_{n}", [P, 512], F32))

        def sem(n):
            sems.append(ctx.enter_context(nc.semaphore(f"{name}_{n}")))
            return sems[-1]

        rotated = rope is not None or batch_rope is not None
        norm = Norm(ctx, nc, name, sem)
        xn = sb("xn", [P, 2, D])
        xn_t = sb("xn_t", [P, 2, KC, S])
        if ctx_t is not None:
            c_t = sb("c_t", [P, 2, KC, S])
            c_loaded = [sem(f"c_loaded{i}") for i in range(2)]
        if rotated:
            qk = sb("qk", [P, 2 * D])
            by_cos = sb("by_cos", [P, 2, 2 * D])
            by_sin = sb("by_sin", [P, 2 * D])
            qk_rot = sb("qk_rot", [P, 2, 2 * D])
        if batch_rope is not None:
            squares = sb("squares", [P, 2 * D])
            sum_sq = sb("sum_sq", [P, 2 * H])
            rms = sb("rms", [P, 2, 2 * H])
            squared, summed, rms_eps, rms_done, turned = map(
                sem, ("squared", "summed", "rms_eps", "rms_done", "turned"))
        q_t = sb("q_t", [P, 2, KC, S])
        k_t = sb("k_t", [P, 2, 2, KC, S])
        v = sb("v", [P, 4, H, 2 * HD])
        neg_max = sb("neg_max", [P, 2, HG, 4])
        total = sb("total", [P, 2, HG, 4])
        share = sb("share", [P, 2, HG, 4])
        probs = sb("probs", [P, 2, HG, 4, S])
        probs_t = sb("probs_t", [P, 2, 4, S])
        o_t = sb("o_t", [P, KC, S])
        xv_bank, qk_bank, oo_bank, qkt_bank = map(bank, ("xv_bank", "qk_bank", "oo_bank", "qkt_bank"))
        score_banks = [bank(f"scores{i}") for i in range(2)]
        pt_banks = [bank(f"pt{i}") for i in range(2)]
        xn_tp, v_p = xv_bank[:, 0:D], xv_bank[:, D:2 * D]
        o_tp, out_p = oo_bank[:, 0:D], oo_bank[:, D:2 * D]

        (v_zeroed, xn_done, xn_tp_done, xn_t_done, qk_p_done, v_p_done, v_done, qk_done, cos_done,
         sin_done, rot_done, qkt_p_done, qk_t_done, scores_done, max_done,
         exp_done, share_done, probs_done, pt_p_done, pt_done, pv_done, o_t_done, out_p_done,
         x_biased, x_done) = map(sem, (
             "v_zeroed", "xn_done", "xn_tp_done", "xn_t_done", "qk_p_done", "v_p_done", "v_done",
             "qk_done", "cos_done", "sin_done", "rot_done", "qkt_p_done", "qk_t_done", "scores_done", "max_done", "exp_done", "share_done", "probs_done",
             "pt_p_done", "pt_done", "pv_done", "o_t_done", "out_p_done", "x_biased", "x_done"))

        copied = (pt_done, sem("pt_done_by_act"))

        def pt_copied(b, g):
            return copied[g % 2], 2 * b + g // 2 + 1

        blocks = ctx.enter_context(ExitStack())
        block = blocks.enter_context(nc.Block())

        if ctx_t is not None:
            @block.sync
            def _(sp):
                def load(b, par):
                    waits(sp, v_p_done, b - 1)
                    src = ctx_t[b] if isinstance(b, int) else \
                        ctx_t[bass.ds(b, 1)].rearrange("a d t -> (a d) t")
                    sp.dma_start(c_t[:, par, :, :], src.rearrange("(c p) t -> p c t", p=P)
                                 ).then_inc(c_loaded[par], 16)
                load(0, 0)
                load(1, 1)
                with sp.Fori(2, B - 1, 2) as t:
                    load(t, 0)
                    load(t + 1, 1)

        @block.tensor
        def _(pe):
            for s, n in loads:
                pe.wait_ge(s, n)

            def project(b, par):
                pe.wait_ge(xn_t_done, b + 1)
                waits(pe, qk_t_done if not rotated else squared if batch_rope is not None else
                      qk_done, b)
                if rotated and ctx_t is None:
                    for c in range(KC):
                        last = pe.matmul(qk_bank[:], xn_t[:, par, c, :], w_in[:, c, 0:2 * D],
                                         start=c == 0, stop=c == KC - 1)
                elif rotated:
                    for c in range(KC):
                        pe.matmul(qk_bank[:, 0:D], xn_t[:, par, c, :], w_in[:, c, 0:D],
                                  start=c == 0, stop=c == KC - 1)
                    pe.wait_ge(c_loaded[par], 8 * (b - par) + 16)
                    for c in range(KC):
                        last = pe.matmul(qk_bank[:, D:2 * D], c_t[:, par, c, :], w_in[:, c, D:2 * D],
                                         start=c == 0, stop=c == KC - 1)
                else:
                    for f in range(2 * KC):
                        for c in range(KC):
                            last = pe.matmul(qk_bank[:, f * S:(f + 1) * S],
                                             w_in[:, c, f * P:(f + 1) * P], xn_t[:, par, c, :],
                                             start=c == 0, stop=c == KC - 1)
                last.then_inc(qk_p_done, 1)
                src = xn_t if ctx_t is None else c_t
                for c in range(KC):
                    last = pe.matmul(v_p, src[:, par, c, :], w_in[:, c, 2 * D:3 * D],
                                     start=c == 0, stop=c == KC - 1)
                last.then_inc(v_p_done, 1)

            def scores(b, par, g):
                ring = score_banks[g % 2]
                waits(pe, exp_done, 4 * b + g - 1)
                if g == 0:
                    pe.wait_ge(qk_t_done, b + 1)
                if mask is not None:
                    pe.matmul(ring[:], k.ident_bf[:], mask[:, None, :].broadcast_to([P, 4, S]),
                              start=True, stop=True)
                for j, h in enumerate(group_heads(g)):
                    c, _, half = head_rows(h)
                    strip = slice(32 * g, 32 * g + 32)
                    last = pe.matmul(ring[:, j * S:(j + 1) * S], q_t[strip, par, c, :],
                                     k_t[strip, par, half, c, :], start=mask is None,
                                     stop=True, skip_group_check=mask is not None)
                last.then_inc(scores_done, 1)

            def probs_transposed(b, par, g):
                pe.wait_ge(probs_done, 4 * b + g + 1)
                waits(pe, *(pt_copied(b, g - 2) if g >= 2 else pt_copied(b - 1, g + 2)))
                for j in range(4):
                    last = pe.transpose(pt_banks[g % 2][:, j * S:(j + 1) * S],
                                        probs[:, par, g, j, :], k.ident[:])
                last.then_inc(pt_p_done, 1)

            def weighted_values(b, vbuf, g):
                pe.wait_ge(*pt_copied(b, g))
                if g == 0:
                    waits(pe, x_done, b)
                    pe.wait_ge(v_done, b + 1)
                for j, h in enumerate(group_heads(g)):
                    c, _, half = head_rows(h)
                    last = pe.matmul(o_tp[32 * g:32 * g + 32, c * S:(c + 1) * S], v[:, vbuf, h, :],
                                     probs_t[:, g % 2, j, :], start=half == 0, stop=half == 1,
                                     skip_group_check=True)
                last.then_inc(pv_done, 1)

            def body(t, phase, live):
                par, other, sc, wv = phase % 2, (phase - 1) % 2, (phase - SC) % 2, (phase - WV) % 2
                qt = (phase - QT) % 2
                if live(1):
                    b = t - 1
                    pe.wait_ge(xn_done, b + 1)
                    waits(pe, v_done, b)
                    for c in range(KC):
                        last = pe.transpose(xn_tp[:, c * S:(c + 1) * S],
                                            xn[:, other, c * P:(c + 1) * P], k.ident[:])
                    last.then_inc(xn_tp_done, 1)
                if live(WV):
                    probs_transposed(t - WV, wv, 0)
                    probs_transposed(t - WV, wv, 1)
                if live(SC):
                    scores(t - SC, sc, 0)
                    scores(t - SC, sc, 1)
                if live(OUT):
                    b = t - OUT
                    pe.wait_ge(o_t_done, b + 1)
                    for c in range(KC):
                        last = pe.matmul(out_p, o_t[:, c, :], w_out[:, c, :],
                                         start=c == 0, stop=c == KC - 1)
                    last.then_inc(out_p_done, 1)
                if live(1):
                    project(t - 1, other)
                if live(QT) and rotated:
                    b = t - QT
                    pe.wait_ge(rot_done, b + 1)
                    waits(pe, qk_t_done, b)
                    for f in range(2 * KC):
                        last = pe.transpose(qkt_bank[:, f * S:(f + 1) * S],
                                            qk_rot[:, qt, f * P:(f + 1) * P], k.ident[:])
                    last.then_inc(qkt_p_done, 1)
                vbuf = (phase - WV) % 4
                for g in range(HG):
                    if live(WV):
                        weighted_values(t - WV, vbuf, g)
                        if g < 2:
                            probs_transposed(t - WV, wv, g + 2)
                    if live(SC) and g < 2:
                        scores(t - SC, sc, g + 2)
            pipeline(pe, body, OUT + 1, 4)

        @block.vector
        def _(dve):
            dve.memset(v[:], 0.0).then_inc(v_zeroed, 1)
            dve.wait_ge(v_zeroed, 1)

            def body(t, phase, live):
                par, other, sc, wv = phase % 2, (phase - 1) % 2, (phase - SC) % 2, (phase - WV) % 2
                qt = (phase - QT) % 2
                def head_max(g):
                    b = t - SC
                    dve.wait_ge(scores_done, 4 * b + g + 1)
                    waits(dve, exp_done, 4 * b + g - 7)
                    dve.tensor_reduce(neg_max[:, sc, g, :],
                                      score_banks[g % 2][:].rearrange("p (j s) -> p j s", j=4),
                                      axis=AX.X, op=ALU.max, negate=True).then_inc(max_done, 1)

                def normalise(b, sc, g):
                    dve.wait_ge(exp_done, 4 * b + g + 1)
                    dve.reciprocal(share[:, sc, g, :], total[:, sc, g, :]).then_inc(share_done, 1)
                    dve.wait_ge(share_done, 4 * b + g + 1)
                    dve.tensor_tensor(probs[:, sc, g, :, :], probs[:, sc, g, :, :],
                                      share[:, sc, g, :, None].broadcast_to([P, 4, S]),
                                      ALU.mult).then_inc(probs_done, 1)

                def copy_pt(g):
                    b = t - WV
                    dve.wait_ge(pt_p_done, 4 * b + g + 1)
                    waits(dve, pv_done, 4 * b + g - 1)
                    dve.tensor_copy(probs_t[:, g % 2, :, :].rearrange("p j s -> p (j s)"),
                                    pt_banks[g % 2][:]).then_inc(pt_done, 1)

                if live(WV):
                    copy_pt(0)
                if live(WV):
                    normalise(t - WV, wv, 2)
                if live(SC):
                    head_max(0)
                if live(WV):
                    normalise(t - WV, wv, 3)
                if live(SC):
                    head_max(1)
                if live(OUT):
                    b = t - OUT
                    dve.wait_ge(out_p_done, b + 1)
                    if out_bias is not None:
                        dve.wait_ge(x_biased, b + 1)
                    dve.tensor_tensor(seq(x, b), out_p, seq(x, b), ALU.add).then_inc(x_done, 1)
                if live(2) and batch_rope is not None:
                    b = t - 2
                    dve.wait_ge(rms_done, b + 1)
                    dve.wait_ge(turned, b + 1)
                    waits(dve, qkt_p_done, b - 1)
                    dve.tensor_tensor(qk_rot[:, par, :].rearrange("p (h d) -> p h d", d=HD),
                                      by_cos[:, par, :].rearrange("p (h d) -> p h d", d=HD),
                                      rms[:, par, :, None].broadcast_to([P, 2 * H, HD]),
                                      ALU.mult).then_inc(rot_done, 1)
                if live(SC):
                    normalise(t - SC, sc, 0)
                    normalise(t - SC, sc, 1)
                if live(0):
                    if isinstance(t, int) and t in x_arrives:
                        dve.wait_ge(x_arrives[t], 16)
                    norm_statistics(dve, norm, k, x, t, par)
                if live(1):
                    b = t - 1
                    if qkv_bias is not None:
                        dve.wait_ge(v_p_done, b + 1)
                        waits(dve, pv_done, 4 * b - 12)
                        bias = qkv_bias[:, 2 * D:3 * D].rearrange("p (h d) -> p h d", d=HD)
                        for half in range(2):
                            last = dve.tensor_tensor(
                                v[:, (phase - 1) % 4, half:H:2, half * HD:(half + 1) * HD],
                                v_p.rearrange("p (h d) -> p h d", d=HD)[:, half:H:2, :],
                                bias[:, half:H:2, :], ALU.add)
                        last.then_inc(v_done, 1)
                if live(1) and rotated:
                    b = t - 1
                    if batch_rope is None:
                        dve.wait_ge(qk_p_done, b + 1)
                        waits(dve, sin_done, b)
                        dve.tensor_tensor(qk[:], qk_bank[:], qkv_bias[:, 0:2 * D],
                                          ALU.add).then_inc(qk_done, 1)
                    tab = rope if batch_rope is None else seq(batch_rope, b)
                    dve.wait_ge(qk_done, b + 1)
                    cos = tab[:, 0:2 * HD].rearrange("p (a d) -> p a d", a=2)
                    dve.tensor_tensor(by_cos[:, other, :].rearrange("p (a h d) -> p a h d", a=2, h=H),
                                      qk[:].rearrange("p (a h d) -> p a h d", a=2, h=H),
                                      cos[:, :, None, :].broadcast_to([P, 2, H, HD]),
                                      ALU.mult).then_inc(cos_done, 1)
                    if batch_rope is not None:
                        dve.wait_ge(squared, b + 1)
                        waits(dve, rms_done, b)
                        dve.tensor_reduce(sum_sq[:], squares[:].rearrange("p (h d) -> p h d", d=HD),
                                          axis=AX.X, op=ALU.add).then_inc(summed, 1)
                if live(WV):
                    copy_pt(2)
                if live(SC):
                    head_max(2)
                if live(0):
                    dve.wait_ge(norm.rstd_done, t + 1)
                    waits(dve, xn_tp_done, t - 1)
                    dve.tensor_scalar(xn[:, par, :], seq(x, t), norm.mean_var[:, par, 0:1],
                                      norm.rstd[:, par, :], ALU.subtract, ALU.mult
                                      ).then_inc(xn_done, 1)
                if live(1) and rotated:
                    b = t - 1
                    dve.wait_ge(sin_done, b + 1)
                    dve.wait_ge(cos_done, b + 1)
                    if batch_rope is None:
                        waits(dve, qkt_p_done, b - 1)
                        dve.tensor_tensor(qk_rot[:, other, :], by_cos[:, other, :], by_sin[:],
                                          ALU.add).then_inc(rot_done, 1)
                    else:
                        dve.tensor_tensor(by_cos[:, other, :], by_cos[:, other, :], by_sin[:], ALU.add
                                          ).then_inc(turned, 1)
                if live(SC):
                    head_max(3)
            pipeline(dve, body, OUT + 1, 4)

        @block.scalar
        def _(act):
            def copy_pt(b, g):
                act.wait_ge(pt_p_done, 4 * b + g + 1)
                waits(act, pv_done, 4 * b + g - 1)
                act.activation(probs_t[:, 1, :, :].rearrange("p j s -> p (j s)"), pt_banks[1][:],
                               ACT.Copy).then_inc(copied[1], 1)

            def exps(t, par, g):
                b = t - SC
                act.wait_ge(max_done, 4 * b + g + 1)
                waits(act, probs_done, 4 * b + g - 7)
                if g == 0:
                    waits(act, pt_p_done, 4 * b - 4)
                for j in range(4):
                    last = act.activation(probs[:, par, g, j, :], score_banks[g % 2][:, j * S:(j + 1) * S],
                                          ACT.Exp, bias=neg_max[:, par, g, j:j + 1],
                                          accum_out=total[:, par, g, j:j + 1])
                last.then_inc(exp_done, 1)

            def body(t, phase, live):
                par, other, sc, wv = phase % 2, (phase - 1) % 2, (phase - SC) % 2, (phase - WV) % 2
                qt = (phase - QT) % 2
                if live(1):
                    b = t - 1
                    act.wait_ge(xn_tp_done, b + 1)
                    waits(act, v_p_done, b - 1)
                    act.activation(xn_t[:, other, :, :].rearrange("p c t -> p (c t)"), xn_tp,
                                   ACT.Copy).then_inc(xn_t_done, 1)
                if live(WV):
                    copy_pt(t - WV, 1)
                if live(SC):
                    exps(t, sc, 0)
                    exps(t, sc, 1)
                if live(1) and batch_rope is not None:
                    b = t - 1
                    act.wait_ge(qk_p_done, b + 1)
                    waits(act, sin_done, b)
                    waits(act, cos_done, b)
                    act.activation(qk[:], qk_bank[:], ACT.Copy).then_inc(qk_done, 1)
                    waits(act, summed, b)
                    act.activation(squares[:], qk_bank[:], ACT.Square).then_inc(squared, 1)
                if live(1) and qkv_bias is None:
                    b = t - 1
                    act.wait_ge(v_p_done, b + 1)
                    waits(act, pv_done, 4 * b - 12)
                    for half in range(2):
                        last = act.activation(
                            v[:, (phase - 1) % 4, half:H:2, half * HD:(half + 1) * HD],
                            v_p.rearrange("p (h d) -> p h d", d=HD)[:, half:H:2, :], ACT.Copy)
                    last.then_inc(v_done, 1)
                if live(QT):
                    b = t - QT
                    src = qkt_bank if rotated else qk_bank
                    if rotated:
                        act.wait_ge(qkt_p_done, b + 1)
                    else:
                        act.wait_ge(qk_p_done, b + 1)
                    waits(act, scores_done, 4 * b - 4)
                    act.activation(q_t[:, qt, :, :].rearrange("p c t -> p (c t)"), src[:, 0:2 * S],
                                   ACT.Copy, scale=scale)
                    for half, kept in enumerate((k.even_rows, k.odd_rows)):
                        last = act.activation(k_t[:, qt, half, :, :].rearrange("p c t -> p (c t)"),
                                              src[:, 2 * S:4 * S], ACT.Copy, scale=kept[:, 0:1])
                    last.then_inc(qk_t_done, 1)
                if live(WV):
                    copy_pt(t - WV, 3)
                if live(SC):
                    exps(t, sc, 2)
                if live(SC):
                    exps(t, sc, 3)
                if live(WV):
                    b = t - WV
                    act.wait_ge(pv_done, 4 * b + 4)
                    waits(act, out_p_done, b)
                    act.activation(o_t[:].rearrange("p c t -> p (c t)"), o_tp,
                                   ACT.Copy).then_inc(o_t_done, 1)
            pipeline(act, body, OUT + 1, 4)

        @block.gpsimd
        def _(pool):
            def body(t, phase, live):
                par, other, sc, wv = phase % 2, (phase - 1) % 2, (phase - SC) % 2, (phase - WV) % 2
                qt = (phase - QT) % 2
                if live(0):
                    norm_rstd(pool, norm, k, t, par)
                if live(1) and rotated:
                    b = t - 1
                    pool.wait_ge(qk_done, b + 1)
                    waits(pool, rot_done if batch_rope is None else turned, b)
                    tab = rope if batch_rope is None else seq(batch_rope, b)
                    sin = tab[:, 2 * HD:4 * HD].rearrange("p (a f d) -> p a f d", a=2, f=2)
                    dst = by_sin[:].rearrange("p (a h f d) -> p a h f d", a=2, h=H, f=2)
                    src = qk[:].rearrange("p (a h f d) -> p a h f d", a=2, h=H, f=2)
                    for f in range(2):
                        last = pool.tensor_tensor(dst[:, :, :, f, :], src[:, :, :, 1 - f, :],
                                                  sin[:, :, f, :][:, :, None, :].broadcast_to(
                                                      [P, 2, H, HD // 2]), ALU.mult)
                    last.then_inc(sin_done, 1)
                if live(1) and out_bias is not None:
                    b = t - 1
                    pool.wait_ge(xn_done, b + 1)
                    pool.tensor_tensor(seq(x, b), seq(x, b), out_bias[:], ALU.add
                                       ).then_inc(x_biased, 1)
                if live(1) and batch_rope is not None:
                    b = t - 1
                    pool.wait_ge(summed, b + 1)
                    waits(pool, rot_done, b - 1)
                    pool.tensor_tensor(sum_sq[:], sum_sq[:], k.rms_eps[:], ALU.add
                                       ).then_inc(rms_eps, 1)
                    pool.wait_ge(rms_eps, b + 1)
                    pool.tensor_tensor(rms[:, other, :], sum_sq[:], k.minus_half[:, 0:2 * H],
                                       ALU.pow).then_inc(rms_done, 1)
            pipeline(pool, body, OUT + 1, 4)

        blocks.close()
        clear(nc, sems)


def context_attention(nc, name, x, k, w_in, q_bias, k_bias, v_bias, ctx_t, loads):
    with ExitStack() as ctx:
        sems = []
        def sb(n, shape, dt=F32):
            return ctx.enter_context(nc.sbuf_tensor(f"{name}_{n}", shape, dt))

        def bank(n):
            return ctx.enter_context(nc.psum_tensor(f"{name}_{n}", [P, 512], F32))

        def sem(n):
            sems.append(ctx.enter_context(nc.semaphore(f"{name}_{n}")))
            return sems[-1]

        norm = Norm(ctx, nc, name, sem)
        xn = sb("xn", [P, 2, D])
        xn_t = sb("xn_t", [P, 2, KC, S])
        c_t = sb("c_t", [P, 2, KC, S])
        q_t = sb("q_t", [P, 2, KC, S])
        k_t = sb("k_t", [P, 2, KC, S])
        v = sb("v", [P, 4, D])
        neg_max = sb("neg_max", [P, 2, 1])
        total = sb("total", [P, 2, 1])
        share = sb("share", [P, 4, 1])
        probs = sb("probs", [P, 2, S])
        probs_t = sb("probs_t", [P, 2, S])
        xq_bank, k_bank, v_bank, score_bank, pt_bank, out_bank = map(
            bank, ("xq_bank", "k_bank", "v_bank", "score_bank", "pt_bank", "out_bank"))
        xn_tp, q_p = xq_bank[:, 0:D], xq_bank[:, D:2 * D]
        c_loaded = [sem(f"c_loaded{i}") for i in range(2)]
        (xn_done, xn_tp_done, xn_t_done, q_p_done, k_p_done, v_p_done, v_done, q_t_done, k_t_done,
         scores_done, max_done, exp_done, share_done, pt_p_done, pt_done, out_p_done, x_done) = map(
             sem, ("xn_done", "xn_tp_done", "xn_t_done", "q_p_done", "k_p_done", "v_p_done", "v_done",
                   "q_t_done", "k_t_done", "scores_done", "max_done", "exp_done", "share_done",
                   "pt_p_done", "pt_done", "out_p_done", "x_done"))

        blocks = ctx.enter_context(ExitStack())
        block = blocks.enter_context(nc.Block())

        @block.sync
        def _(sp):
            def load(b, par):
                waits(sp, k_p_done, b - 1)
                src = ctx_t[b] if isinstance(b, int) else \
                    ctx_t[bass.ds(b, 1)].rearrange("a d t -> (a d) t")
                sp.dma_start(c_t[:, par, :, :], src.rearrange("(c p) t -> p c t", p=P)
                             ).then_inc(c_loaded[par], 16)
            load(0, 0)
            load(1, 1)
            with sp.Fori(2, B - 1, 2) as t:
                load(t, 0)
                load(t + 1, 1)

        @block.tensor
        def _(pe):
            for s, n in loads:
                pe.wait_ge(s, n)

            def body(t, phase, live):
                par, other = phase % 2, 1 - phase % 2
                if live(1):
                    b = t - 1
                    pe.wait_ge(xn_done, b + 1)
                    waits(pe, q_t_done, b)
                    for c in range(KC):
                        last = pe.transpose(xn_tp[:, c * S:(c + 1) * S],
                                            xn[:, other, c * P:(c + 1) * P], k.ident[:])
                    last.then_inc(xn_tp_done, 1)
                if live(2):
                    b = t - 2
                    pe.wait_ge(q_t_done, b + 1)
                    pe.wait_ge(k_t_done, b + 1)
                    waits(pe, exp_done, b)
                    for c in range(KC):
                        last = pe.matmul(score_bank[:, 0:S], q_t[:, par, c, :], k_t[:, par, c, :],
                                         start=c == 0, stop=c == KC - 1)
                    last.then_inc(scores_done, 1)
                if live(3):
                    b = t - 3
                    pe.wait_ge(exp_done, b + 1)
                    waits(pe, pt_done, b)
                    pe.transpose(pt_bank[:, 0:S], probs[:, other, :], k.ident[:]).then_inc(pt_p_done, 1)
                if live(1):
                    b = t - 1
                    pe.wait_ge(c_loaded[other], 8 * (b - other) + 16)
                    waits(pe, v_done, b)
                    for c in range(KC):
                        last = pe.matmul(v_bank[:, 0:D], c_t[:, other, c, :], w_in[:, c, 2 * D:3 * D],
                                         start=c == 0, stop=c == KC - 1)
                    last.then_inc(v_p_done, 1)
                    waits(pe, k_t_done, b)
                    for f in range(KC):
                        for c in range(KC):
                            last = pe.matmul(k_bank[:, f * S:(f + 1) * S],
                                             w_in[:, c, D + f * P:D + (f + 1) * P],
                                             c_t[:, other, c, :], start=c == 0, stop=c == KC - 1)
                    last.then_inc(k_p_done, 1)
                    pe.wait_ge(xn_t_done, b + 1)
                    for f in range(KC):
                        for c in range(KC):
                            last = pe.matmul(q_p[:, f * S:(f + 1) * S],
                                             w_in[:, c, f * P:(f + 1) * P], xn_t[:, other, c, :],
                                             start=c == 0, stop=c == KC - 1)
                    last.then_inc(q_p_done, 1)
                if live(3):
                    b = t - 3
                    pe.wait_ge(pt_done, b + 1)
                    pe.wait_ge(v_done, b + 1)
                    waits(pe, x_done, b)
                    pe.matmul(out_bank[:, 0:D], probs_t[:, other, :], v[:, (phase - 3) % 4, :],
                              start=True, stop=True).then_inc(out_p_done, 1)
            pipeline(pe, body, 4, 4)

        @block.vector
        def _(dve):
            def body(t, phase, live):
                par, other = phase % 2, 1 - phase % 2
                if live(2):
                    b = t - 2
                    dve.wait_ge(scores_done, b + 1)
                    waits(dve, exp_done, b - 1)
                    dve.tensor_reduce(neg_max[:, par, :], score_bank[:, 0:S], axis=AX.X, op=ALU.max,
                                      negate=True).then_inc(max_done, 1)
                if live(3):
                    b = t - 3
                    dve.wait_ge(pt_p_done, b + 1)
                    waits(dve, out_p_done, b - 1)
                    dve.tensor_copy(probs_t[:, other, :], pt_bank[:, 0:S]).then_inc(pt_done, 1)
                if live(0):
                    norm_statistics(dve, norm, k, x, t, par)
                if live(1):
                    b = t - 1
                    dve.wait_ge(v_p_done, b + 1)
                    waits(dve, out_p_done, b - 3)
                    dve.tensor_tensor(v[:, (phase - 1) % 4, :], v_bank[:, 0:D], v_bias[:],
                                      ALU.add).then_inc(v_done, 1)
                    dve.wait_ge(q_p_done, b + 1)
                    waits(dve, scores_done, b - 1)
                    for f in range(KC):
                        last = dve.tensor_scalar(q_t[:, other, f, :], q_p[:, f * S:(f + 1) * S],
                                                 q_bias[:, f:f + 1], D ** -0.5, ALU.add, ALU.mult)
                    last.then_inc(q_t_done, 1)
                if live(0):
                    dve.wait_ge(norm.rstd_done, t + 1)
                    waits(dve, xn_tp_done, t - 1)
                    dve.tensor_scalar(xn[:, par, :], seq(x, t), norm.mean_var[:, par, 0:1],
                                      norm.rstd[:, par, :], ALU.subtract, ALU.mult
                                      ).then_inc(xn_done, 1)
                if live(2):
                    b = t - 2
                    dve.wait_ge(exp_done, b + 1)
                    dve.reciprocal(share[:, (phase - 2) % 4, :], total[:, par, :]).then_inc(share_done, 1)
                if live(3):
                    b = t - 3
                    dve.wait_ge(out_p_done, b + 1)
                    dve.wait_ge(share_done, b + 1)
                    dve.scalar_tensor_tensor(seq(x, b), out_bank[:, 0:D], share[:, (phase - 3) % 4, :],
                                             seq(x, b), ALU.mult, ALU.add).then_inc(x_done, 1)
            pipeline(dve, body, 4, 4)

        @block.scalar
        def _(act):
            def body(t, phase, live):
                par, other = phase % 2, 1 - phase % 2
                if live(1):
                    b = t - 1
                    act.wait_ge(xn_tp_done, b + 1)
                    waits(act, q_p_done, b - 1)
                    act.activation(xn_t[:, other, :, :].rearrange("p c t -> p (c t)"),
                                   xn_tp, ACT.Copy).then_inc(xn_t_done, 1)
                if live(2):
                    b = t - 2
                    act.wait_ge(max_done, b + 1)
                    waits(act, pt_p_done, b - 1)
                    waits(act, share_done, b - 1)
                    act.activation(probs[:, par, :], score_bank[:, 0:S], ACT.Exp,
                                   bias=neg_max[:, par, :], accum_out=total[:, par, :]
                                   ).then_inc(exp_done, 1)
                if live(1):
                    b = t - 1
                    act.wait_ge(k_p_done, b + 1)
                    waits(act, scores_done, b - 1)
                    for f in range(KC):
                        last = act.activation(k_t[:, other, f, :], k_bank[:, f * S:(f + 1) * S],
                                              ACT.Identity, bias=k_bias[:, f:f + 1])
                    last.then_inc(k_t_done, 1)
            pipeline(act, body, 4, 4)

        @block.gpsimd
        def _(pool):
            def body(t, phase, live):
                if live(0):
                    norm_rstd(pool, norm, k, t, phase % 2)
            pipeline(pool, body, 4, 4)

        blocks.close()
        clear(nc, sems)


def experts(nc, name, x, k, w_router, router_bias, w_experts, expert_bias, loads):
    with ExitStack() as ctx:
        sems = []
        def sb(n, shape, dt=F32):
            return ctx.enter_context(nc.sbuf_tensor(f"{name}_{n}", shape, dt))

        def bank(n):
            return ctx.enter_context(nc.psum_tensor(f"{name}_{n}", [P, 512], F32))

        def sem(n):
            sems.append(ctx.enter_context(nc.semaphore(f"{name}_{n}")))
            return sems[-1]

        norm = Norm(ctx, nc, name, sem)
        xn = sb("xn", [P, 2, D])
        xn_t = sb("xn_t", [P, 2, KC, S])
        logits = sb("logits", [P, 2, E])
        top = sb("top", [P, 8])
        best = sb("best", [P, 8], U32)
        best_f = sb("best_f", [P, 1])
        neg_max = sb("neg_max", [P, 2, 1])
        powers = sb("powers", [P, 2, E])
        total = sb("total", [P, 2, 1])
        gate = sb("gate", [P, 1])
        weight = sb("weight", [P, 2, E])
        weight_t = sb("weight_t", [E, 2, S])
        xn_bank, router_bank, weight_bank, bias_bank = map(
            bank, ("xn_bank", "router_bank", "weight_bank", "bias_bank"))
        pair_banks = [bank(f"pair{i}") for i in range(4)]
        (xn_done, xn_tp_done, xn_t_done, logits_p_done, logits_done, top_done, best_done, max_done,
         exp_done, best_f_done, gate_done, weight_done, weight_tp_done, weight_t_done, pair_done,
         bias_done, added) = map(sem, (
             "xn_done", "xn_tp_done", "xn_t_done", "logits_p_done", "logits_done", "top_done",
             "best_done", "max_done", "exp_done", "best_f_done", "gate_done", "weight_done",
             "weight_tp_done", "weight_t_done", "pair_done", "bias_done", "added"))

        blocks = ctx.enter_context(ExitStack())
        block = blocks.enter_context(nc.Block())

        @block.tensor
        def _(pe):
            for s, n in loads:
                pe.wait_ge(s, n)

            def body(t, phase, live):
                par, other = phase % 2, 1 - phase % 2
                if live(2):
                    b = t - 2
                    pe.wait_ge(weight_done, b + 1)
                    waits(pe, weight_t_done, b)
                    pe.transpose(weight_bank[0:E, 0:S], weight[:, par, :], k.ident[:]
                                 ).then_inc(weight_tp_done, 1)
                if live(1):
                    b = t - 1
                    pe.wait_ge(xn_done, b + 1)
                    waits(pe, xn_t_done, b)
                    for c in range(KC):
                        last = pe.transpose(xn_bank[:, c * S:(c + 1) * S],
                                            xn[:, other, c * P:(c + 1) * P], k.ident[:])
                    last.then_inc(xn_tp_done, 1)
                def pair(b, i):
                    waits(pe, added, 9 * b - 9 + 2 * i + 3)
                    for c in range(KC):
                        last = pe.matmul(pair_banks[i][:], xn_t[:, par, c, :],
                                         w_experts[:, c, i * 2 * D:(i + 1) * 2 * D],
                                         start=c == 0, stop=c == KC - 1)
                    last.then_inc(pair_done, 1)

                if live(2):
                    b = t - 2
                    pair(b, 0)
                    pe.wait_ge(weight_t_done, b + 1)
                    waits(pe, added, 9 * b - 8)
                    pe.matmul(bias_bank[:, 0:D], weight_t[:, par, :], expert_bias[:],
                              start=True, stop=True).then_inc(bias_done, 1)
                if live(1):
                    b = t - 1
                    pe.wait_ge(xn_t_done, b + 1)
                    waits(pe, logits_done, b)
                    for c in range(KC):
                        last = pe.matmul(router_bank[:, 0:E], xn_t[:, other, c, :], w_router[:, c, :],
                                         start=c == 0, stop=c == KC - 1)
                    last.then_inc(logits_p_done, 1)
                if live(2):
                    for i in range(1, E // 2):
                        pair(t - 2, i)
            pipeline(pe, body, 3, 2)

        @block.vector
        def _(dve):
            def body(t, phase, live):
                par, other = phase % 2, 1 - phase % 2

                def add_experts(b, first, last):
                    for e in range(first, last):
                        if e % 2 == 0:
                            dve.wait_ge(pair_done, 4 * b + e // 2 + 1)
                        dve.wait_ge(added, 9 * b + e + 1)
                        dve.scalar_tensor_tensor(
                            seq(x, b), pair_banks[e // 2][:, e % 2 * D:(e % 2 + 1) * D],
                            weight[:, par, e:e + 1], seq(x, b), ALU.mult, ALU.add
                        ).then_inc(added, 1)

                if live(0):
                    norm_statistics(dve, norm, k, x, t, par)
                if live(2):
                    b = t - 2
                    dve.wait_ge(weight_tp_done, b + 1)
                    waits(dve, bias_done, b - 1)
                    dve.tensor_copy(weight_t[:, par, :], weight_bank[0:E, 0:S]
                                    ).then_inc(weight_t_done, 1)
                if live(0):
                    dve.wait_ge(norm.rstd_done, t + 1)
                    waits(dve, xn_tp_done, t - 1)
                    dve.tensor_scalar(xn[:, par, :], seq(x, t), norm.mean_var[:, par, 0:1],
                                      norm.rstd[:, par, :], ALU.subtract, ALU.mult
                                      ).then_inc(xn_done, 1)
                if live(2):
                    b = t - 2
                    dve.wait_ge(bias_done, b + 1)
                    dve.tensor_tensor(seq(x, b), bias_bank[:, 0:D], seq(x, b), ALU.add
                                      ).then_inc(added, 1)
                    add_experts(b, 0, 2)
                if live(1):
                    b = t - 1
                    dve.wait_ge(logits_p_done, b + 1)
                    waits(dve, exp_done, b - 1)
                    dve.tensor_tensor(logits[:, other, :], router_bank[:, 0:E], router_bias[:],
                                      ALU.add).then_inc(logits_done, 1)
                    apart(dve, k)
                    dve.wait_ge(logits_done, b + 1)
                    dve.max(top[:], logits[:, other, :]).then_inc(top_done, 1)
                    dve.wait_ge(top_done, b + 1)
                    dve.tensor_scalar(neg_max[:, other, :], top[:, 0:1], -1.0, None, ALU.mult
                                      ).then_inc(max_done, 1)
                    dve.max_index(best[:], top[:], logits[:, other, :]).then_inc(best_done, 1)
                    dve.wait_ge(best_done, b + 1)
                    dve.tensor_copy(best_f[:], best[:, 0:1]).then_inc(best_f_done, 1)
                    dve.wait_ge(exp_done, b + 1)
                    dve.reciprocal(gate[:], total[:, other, :]).then_inc(gate_done, 1)
                    dve.wait_ge(gate_done, b + 1)
                    dve.wait_ge(best_f_done, b + 1)
                    dve.tensor_scalar(weight[:, other, :], k.iota[:], best_f[:], gate[:],
                                      ALU.is_equal, ALU.mult).then_inc(weight_done, 1)
                if live(2):
                    add_experts(t - 2, 2, E)
            pipeline(dve, body, 3, 2)

        @block.scalar
        def _(act):
            def body(t, phase, live):
                par, other = phase % 2, 1 - phase % 2
                if live(1):
                    b = t - 1
                    act.wait_ge(xn_tp_done, b + 1)
                    waits(act, pair_done, 4 * b - 4)
                    waits(act, logits_p_done, b - 1)
                    act.activation(xn_t[:, other, :, :].rearrange("p c t -> p (c t)"),
                                   xn_bank[:, 0:D], ACT.Copy).then_inc(xn_t_done, 1)
                    act.wait_ge(max_done, b + 1)
                    waits(act, gate_done, b - 1)
                    act.activation(powers[:, other, :], logits[:, other, :], ACT.Exp,
                                   bias=neg_max[:, other, :], accum_out=total[:, other, :]
                                   ).then_inc(exp_done, 1)
            pipeline(act, body, 3, 2)

        @block.gpsimd
        def _(pool):
            def body(t, phase, live):
                if live(0):
                    norm_rstd(pool, norm, k, t, phase % 2)
            pipeline(pool, body, 3, 2)

        blocks.close()
        clear(nc, sems)


U = 4
UNITS = B // U
UT = U * S


def unit(x, u):
    if isinstance(u, int):
        return x[:, u]
    return x[:, bass.ds(u, 1)].rearrange("p a n -> p (a n)")


def quantised_ffn(nc, name, x, k, w_gate, w_up, w_down, clips, out, loads):
    with ExitStack() as ctx:
        def sb(n, shape, dt=F32, c=ctx):
            return c.enter_context(nc.sbuf_tensor(f"{name}_{n}", shape, dt))

        def bank(n, c, dt=F32):
            return c.enter_context(nc.psum_tensor(f"{name}_{n}", [P, 2048 // (4 if dt == F32 else 2)], dt))

        def sem(n):
            return ctx.enter_context(nc.semaphore(f"{name}_{n}"))

        gate_t = sb("gate_t", [P, KC, I], BF16)
        up_t = sb("up_t", [P, KC, I], BF16)
        down_t = sb("down_t", [P, IC, D], BF16)
        gate_scale = sb("gate_scale", [P, IC])
        up_scale = sb("up_scale", [P, IC])
        down_scale = sb("down_scale", [P, KC])
        down_row = sb("down_row", [P, D])
        sig = sb("sig", [P, 2])
        act_scale = sb("act_scale", [P, 2])
        act_inverse = sb("act_inverse", [P, 2])
        seq_max = sb("seq_max", [P, B])
        row_max = sb("row_max", [P, 2])
        one_max = sb("one_max", [1, 2])
        xn_all = sb("xn_all", [P, UNITS, U * D])

        def whole_max(dve_or_pe, which, src, bank_, maxed, turned, taken, spread):
            if dve_or_pe is nc.vector:
                dve = dve_or_pe
                dve.tensor_reduce(row_max[:, which:which + 1], src, axis=AX.X, op=ALU.max
                                  ).then_inc(maxed, 1)
                dve.wait_ge(turned, 1)
                dve.tensor_reduce(one_max[:, which:which + 1], bank_[0:1, 0:P], axis=AX.X,
                                  op=ALU.max).then_inc(taken, 1)
                dve.wait_ge(spread, 1)
            else:
                pe = dve_or_pe
                pe.wait_ge(maxed, 1)
                pe.transpose(bank_[0:1, 0:P], row_max[:, which:which + 1], k.ident[:]
                             ).then_inc(turned, 1)
                pe.wait_ge(taken, 1)
                pe.matmul(bank_[:, P:P + 1], k.ones[0:1, :], one_max[:, which:which + 1],
                          start=True, stop=True).then_inc(spread, 1)

        with ExitStack() as part:
            norm = Norm(part, nc, name, sem)
            names = ("gate", "up", "down")
            shapes = dict(gate=[P, IC, D], up=[P, IC, D], down=[P, KC, I])
            raw = {n: sb(f"{n}_raw", shapes[n], F32, part) for n in names}
            inverse = {n: sb(f"{n}_inverse", [P, shapes[n][1]], F32, part) for n in names}
            ints = {n: sb(f"{n}_ints", shapes[n], BF16, part) for n in names}
            scale = dict(gate=gate_scale, up=up_scale, down=down_scale)
            diagonal = sb("diagonal", [P, KC, P], F32, part)
            exps = sb("exps", [P, 2], F32, part)
            turn_banks = [bank(f"turn{i}", part, BF16) for i in range(4)]
            row_bank = bank("row_bank", part)
            tails, chain, sig_exp, ints_done, turned, copied, diag_done, row_done, \
                xn_done, xn_maxed, x_maxed, x_turned, x_taken, x_spread = map(sem, (
                    "tails", "chain", "sig_exp", "ints_done", "turned", "copied",
                    "diag_done", "row_done", "xn_done", "xn_maxed", "x_maxed", "x_turned", "x_taken", "x_spread"))
            last_rows = rows(IC - 1)
            block = part.enter_context(nc.Block())
            w_loads = [sem(f"w_loaded{i}") for i in range(5)]

            turns = []
            for n, dst in (("gate", gate_t), ("up", up_t)):
                for c in range(IC):
                    for h in range(KC):
                        turns.append((n, c, h * P, rows(c), P, dst[:, h, c * P:c * P + rows(c)]))
            for c in range(KC):
                for i in range(IC):
                    turns.append(("down", c, i * P, P, rows(i), down_t[0:rows(i), i, c * P:(c + 1) * P]))

            @block.sync
            def _(sp):
                sp.wait_ge(tails, 2)
                for n, src, i in (("gate", w_gate, 0), ("up", w_up, 2)):
                    full = (IC - 1) * P
                    sp.dma_start(raw[n][:, 0:IC - 1, :],
                                 src[0:full, :].rearrange("(c p) h -> p c h", p=P)
                                 ).then_inc(w_loads[i], 16)
                    sp.dma_start(raw[n][0:last_rows, IC - 1, :], src[full:I, :]
                                 ).then_inc(w_loads[i + 1], 16)
                sp.dma_start(raw["down"][:], w_down.rearrange("(c p) i -> p c i", p=P)
                             ).then_inc(w_loads[4], 16)

            @block.gpsimd
            def _(pool):
                for n in ("gate", "up"):
                    pool.memset(raw[n][last_rows:P, IC - 1, :], 1.0).then_inc(tails, 1)

                def body(b, par, live):
                    norm_rstd(pool, norm, k, b, par)
                pipeline(pool, body, 1, 2)

            @block.scalar
            def _(act):
                act.activation(exps[:], clips[:], ACT.Exp, scale=-1.0).then_inc(sig_exp, 1)
                for i, (n, c, at, r, w, dst) in enumerate(turns):
                    act.wait_ge(turned, i + 1)
                    act.activation(dst, turn_banks[i % 4][0:w, 0:r], ACT.Copy).then_inc(copied, 1)

            @block.tensor
            def _(pe):
                for i, (n, c, at, r, w, dst) in enumerate(turns):
                    pe.wait_ge(ints_done, names.index(n) + 1)
                    waits(pe, copied, i - 3)
                    pe.transpose(turn_banks[i % 4][0:w, 0:r], ints[n][0:r, c, at:at + w],
                                 k.ident_bf[0:r, 0:r]).then_inc(turned, 1)
                pe.wait_ge(diag_done, KC)
                for c in range(KC):
                    last = pe.matmul(row_bank[:, c * P:(c + 1) * P], k.ones[:], diagonal[:, c, :],
                                     start=True, stop=True)
                last.then_inc(row_done, 1)
                whole_max(pe, 0, None, row_bank[:, D:2 * D], x_maxed, x_turned, x_taken, x_spread)

            @block.vector
            def _(dve):
                steps = [0]

                def step(instruction):
                    steps[0] += 1
                    instruction.then_inc(chain, 1)
                    dve.wait_ge(chain, steps[0])

                for number, n in enumerate(names):
                    for i in ((0, 1), (2, 3), (4,))[number]:
                        dve.wait_ge(w_loads[i], 16)
                    chunks = shapes[n][1]
                    step(dve.tensor_reduce(scale[n][:], raw[n][:], axis=AX.X, op=ALU.max,
                                           apply_absolute_value=True))
                    step(dve.tensor_scalar(scale[n][:], scale[n][:], 1.0 / QMAX, None, ALU.mult))
                    step(dve.reciprocal(inverse[n][:], scale[n][:]))
                    for c in range(chunks):
                        last = dve.tensor_scalar(raw[n][:, c, :], raw[n][:, c, :],
                                                 inverse[n][:, c:c + 1], ROUND, ALU.mult, ALU.add)
                    step(last)
                    step(dve.tensor_scalar(raw[n][:], raw[n][:], ROUND - QMAX - 1.0, ROUND + QMAX,
                                           ALU.max, ALU.min))
                    dve.tensor_scalar(ints[n][:], raw[n][:], -ROUND, None, ALU.add
                                      ).then_inc(ints_done, 1)
                for c in range(KC):
                    dve.tensor_scalar(diagonal[:, c, :], k.ident[:], down_scale[:, c:c + 1], None,
                                      ALU.mult).then_inc(diag_done, 1)
                dve.wait_ge(sig_exp, 1)
                step(dve.tensor_scalar(exps[:], exps[:], 1.0, None, ALU.add))
                step(dve.reciprocal(sig[:], exps[:]))

                flat = xn_all[:].rearrange("p u (s d) -> p (u s) d", d=D)

                def body(t, par, live):
                    if live(0):
                        norm_statistics(dve, norm, k, x, t, par)
                    if live(1):
                        b = t - 1
                        dve.wait_ge(norm.rstd_done, b + 1)
                        dve.tensor_scalar(seq(flat, b), seq(x, b), norm.mean_var[:, 1 - par, 0:1],
                                          norm.rstd[:, 1 - par, :], ALU.subtract, ALU.mult
                                          ).then_inc(xn_done, 1)
                    if live(2):
                        b = t - 2
                        dve.wait_ge(xn_done, b + 1)
                        dst = seq_max[:, b:b + 1] if isinstance(b, int) else seq_max[:, bass.ds(b, 1)]
                        dve.tensor_reduce(dst, seq(flat, b), axis=AX.X, op=ALU.max,
                                          apply_absolute_value=True).then_inc(xn_maxed, 1)
                pipeline(dve, body, 3, 2)
                dve.wait_ge(row_done, 1)
                step(dve.tensor_copy(down_row[:], row_bank[:, 0:D]))
                dve.wait_ge(xn_maxed, B)
                whole_max(dve, 0, seq_max[:], row_bank[:, D:2 * D], x_maxed, x_turned, x_taken,
                          x_spread)
                step(dve.tensor_scalar(act_scale[:, 0:1], row_bank[:, D + P:D + P + 1], sig[:, 0:1],
                                       1.0 / QMAX, ALU.mult, ALU.mult))
                step(dve.reciprocal(act_inverse[:, 0:1], act_scale[:, 0:1]))
                dve.tensor_scalar(gate_scale[:], gate_scale[:], act_scale[:, 0:1], None, ALU.mult)
                step(dve.tensor_scalar(up_scale[:], up_scale[:], act_scale[:, 0:1], None, ALU.mult))
                assert steps[0] < 200

        hidden = sb("hidden", [P, UNITS, IC * UT])
        hidden_max = sb("hidden_max", [P, UNITS * IC])
        rounded = sb("rounded", [P, U * D])

        with ExitStack() as part:
            x_ints = sb("x_ints", [P, 2, U, D], BF16, part)
            x_ints_t = sb("x_ints_t", [P, 2, KC, UT], BF16, part)
            silu = sb("silu", [P, 2, UT], F32, part)
            turn_bank = bank("x_turn", part, BF16)
            gate_banks = [bank(f"gate_bank{i}", part) for i in range(2)]
            up_banks = [bank(f"up_bank{i}", part) for i in range(2)]
            max_bank = bank("max_bank", part)
            (zeroed, scaled, clipped, x_ints_done, x_turned2, x_ints_t_done, gate_done, up_done,
             silu_done, hidden_done, hidden_maxed, h_maxed, h_turned, h_taken, h_spread, sc) = map(
                 sem, ("zeroed", "scaled", "clipped", "x_ints_done", "x_turned2", "x_ints_t_done",
                       "gate_done", "up_done", "silu_done", "hidden_done", "hidden_maxed",
                       "h_maxed", "h_turned", "h_taken", "h_spread", "sc"))
            block = part.enter_context(nc.Block())

            @block.tensor
            def _(pe):
                def body(t, par, live):
                    other = 1 - par
                    if live(1):
                        u = t - 1
                        pe.wait_ge(x_ints_done, u + 1)
                        waits(pe, x_ints_t_done, u)
                        for c in range(KC):
                            for s in range(U):
                                last = pe.transpose(turn_bank[:, c * UT + s * S:c * UT + (s + 1) * S],
                                                    x_ints[:, other, s, c * P:(c + 1) * P],
                                                    k.ident_bf[:])
                        last.then_inc(x_turned2, 1)
                    if live(2):
                        u = t - 2
                        pe.wait_ge(x_ints_t_done, u + 1)
                        for i in range(IC):
                            n = IC * u + i
                            for w_t, banks, freed, done in (
                                    (gate_t, gate_banks, silu_done, gate_done),
                                    (up_t, up_banks, hidden_done, up_done)):
                                waits(pe, freed, n - 1)
                                for c in range(KC):
                                    last = pe.matmul(banks[i % 2][0:rows(i), :],
                                                     w_t[:, c, i * P:i * P + rows(i)],
                                                     x_ints_t[:, par, c, :],
                                                     start=c == 0, stop=c == KC - 1)
                                last.then_inc(done, 1)
                pipeline(pe, body, 3, 2, UNITS)
                whole_max(pe, 1, None, max_bank, h_maxed, h_turned, h_taken, h_spread)

            @block.scalar
            def _(act):
                def body(t, par, live):
                    other = 1 - par
                    if live(1):
                        u = t - 1
                        act.wait_ge(x_turned2, u + 1)
                        waits(act, up_done, IC * (u - 1))
                        act.activation(x_ints_t[:, other, :, :].rearrange("p c t -> p (c t)"),
                                       turn_bank[:], ACT.Copy).then_inc(x_ints_t_done, 1)
                    if live(2):
                        u = t - 2
                        for i in range(IC):
                            n = IC * u + i
                            act.wait_ge(gate_done, n + 1)
                            waits(act, hidden_done, n - 1)
                            act.activation(silu[0:rows(i), i % 2, :], gate_banks[i % 2][0:rows(i), :],
                                           ACT.Silu, scale=gate_scale[0:rows(i), i:i + 1]
                                           ).then_inc(silu_done, 1)
                pipeline(act, body, 3, 2, UNITS)

            @block.vector
            def _(dve):
                dve.memset(hidden_max[:], 0.0).then_inc(zeroed, 1)
                dve.wait_ge(zeroed, 1)

                def body(t, par, live):
                    if live(0):
                        waits(dve, x_ints_done, t)
                        dve.tensor_scalar(rounded[:], unit(xn_all, t), act_inverse[:, 0:1], ROUND,
                                          ALU.mult, ALU.add).then_inc(scaled, 1)
                        dve.wait_ge(scaled, t + 1)
                        dve.tensor_scalar(rounded[:], rounded[:], ROUND - QMAX - 1.0, ROUND + QMAX,
                                          ALU.max, ALU.min).then_inc(clipped, 1)
                        dve.wait_ge(clipped, t + 1)
                        waits(dve, x_turned2, t - 1)
                        dve.tensor_scalar(x_ints[:, par, :, :].rearrange("p s d -> p (s d)"),
                                          rounded[:], -ROUND, None, ALU.add).then_inc(x_ints_done, 1)
                    if live(2):
                        u = t - 2
                        for i in range(IC):
                            n = IC * u + i
                            r = rows(i)
                            if isinstance(u, int):
                                dst = hidden[0:r, u, i * UT:(i + 1) * UT]
                                peak = hidden_max[0:r, n:n + 1]
                            else:
                                dst = hidden[0:r, bass.ds(u, 1), i * UT:(i + 1) * UT].rearrange(
                                    "p a n -> p (a n)")
                                peak = hidden_max[0:r, bass.ds(n, 1)]
                            dve.wait_ge(up_done, n + 1)
                            dve.wait_ge(silu_done, n + 1)
                            dve.scalar_tensor_tensor(dst, up_banks[i % 2][0:r, :],
                                                     up_scale[0:r, i:i + 1], silu[0:r, i % 2, :],
                                                     ALU.mult, ALU.mult).then_inc(hidden_done, 1)
                            dve.wait_ge(hidden_done, n + 1)
                            dve.tensor_reduce(peak, dst, axis=AX.X, op=ALU.max,
                                              apply_absolute_value=True).then_inc(hidden_maxed, 1)
                pipeline(dve, body, 3, 2, UNITS)
                dve.wait_ge(hidden_maxed, UNITS * IC)
                whole_max(dve, 1, hidden_max[:], max_bank, h_maxed, h_turned, h_taken, h_spread)
                dve.tensor_scalar(act_scale[:, 1:2], max_bank[:, P:P + 1], sig[:, 1:2], 1.0 / QMAX,
                                  ALU.mult, ALU.mult).then_inc(sc, 1)
                dve.wait_ge(sc, 1)
                dve.reciprocal(act_inverse[:, 1:2], act_scale[:, 1:2])
                dve.tensor_scalar(down_row[:], down_row[:], act_scale[:, 1:2], None, ALU.mult
                                  ).then_inc(sc, 1)
                dve.wait_ge(sc, 2)

        with ExitStack() as part:
            h_round = sb("h_round", [P, IC * UT], F32, part)
            h_ints = sb("h_ints", [P, 2, IC * UT], BF16, part)
            addend = sb("addend", [P, 2, D], F32, part)
            out_banks = [bank(f"out{i}", part) for i in range(4)]
            h_scaled, h_clipped, h_ints_done, down_done, addend_done, x_done = map(sem, (
                "h_scaled", "h_clipped", "h_ints_done", "down_done", "addend_done", "x_done"))
            stored = [sem(f"stored{i}") for i in range(UNITS)]
            block = part.enter_context(nc.Block())
            full = (IC - 1) * UT
            parts = ((P, 0, full), (rows(IC - 1), full, IC * UT))

            @block.vector
            def _(dve):
                def body(t, par, live):
                    if live(0):
                        waits(dve, h_ints_done, 2 * t)
                        for i, (r, lo, hi) in enumerate(parts):
                            src = hidden[0:r, t, lo:hi] if isinstance(t, int) else \
                                hidden[0:r, bass.ds(t, 1), lo:hi].rearrange("p a n -> p (a n)")
                            dve.tensor_scalar(h_round[0:r, lo:hi], src, act_inverse[0:r, 1:2], ROUND,
                                              ALU.mult, ALU.add).then_inc(h_scaled, 1)
                        for i, (r, lo, hi) in enumerate(parts):
                            dve.wait_ge(h_scaled, 2 * t + i + 1)
                            dve.tensor_scalar(h_round[0:r, lo:hi], h_round[0:r, lo:hi],
                                              ROUND - QMAX - 1.0, ROUND + QMAX, ALU.max, ALU.min
                                              ).then_inc(h_clipped, 1)
                    if live(1):
                        u = t - 1
                        for s in range(U):
                            n = U * u + s
                            dve.wait_ge(down_done, n + 1)
                            waits(dve, x_done, n - 1)
                            dve.tensor_tensor(addend[:, s % 2, :], out_banks[s][:, 0:D], down_row[:],
                                              ALU.mult).then_inc(addend_done, 1)
                pipeline(dve, body, 2, 2, UNITS)

            @block.scalar
            def _(act):
                def body(t, par, live):
                    if live(0):
                        waits(act, down_done, U * (t - 1))
                        for i, (r, lo, hi) in enumerate(parts):
                            act.wait_ge(h_clipped, 2 * t + i + 1)
                            act.activation(h_ints[0:r, par, lo:hi], h_round[0:r, lo:hi], ACT.Copy,
                                           bias=-ROUND).then_inc(h_ints_done, 1)
                pipeline(act, body, 1, 2, UNITS)

            @block.tensor
            def _(pe):
                def body(t, par, live):
                    pe.wait_ge(h_ints_done, 2 * t + 2)
                    for s in range(U):
                        waits(pe, addend_done, U * (t - 1) + s + 1)
                        for i in range(IC):
                            at = i * UT + s * S
                            last = pe.matmul(out_banks[s][:, 0:D], h_ints[0:rows(i), par, at:at + S],
                                             down_t[0:rows(i), i, :], start=i == 0, stop=i == IC - 1)
                        last.then_inc(down_done, 1)
                pipeline(pe, body, 1, 2, UNITS)

            @block.gpsimd
            def _(pool):
                def body(t, par, live):
                    for s in range(U):
                        n = U * t + s
                        pool.wait_ge(addend_done, n + 1)
                        pool.tensor_tensor(seq(x, n), seq(x, n), addend[:, s % 2, :], ALU.add
                                           ).then_inc(x_done, 1)
                pipeline(pool, body, 1, 2, UNITS)

            @block.sync
            def _(sp):
                for u in range(UNITS):
                    sp.wait_ge(x_done, U * (u + 1))
                    sp.dma_start(out[U * u:U * u + U].rearrange("b t d -> t b d"),
                                 x[:, U * u:U * u + U, :]).then_inc(stored[u], 16)
                for u in range(UNITS):
                    sp.wait_ge(stored[u], 16)


class Constants:
    pass


def decoder(nc, a, out):
    with ExitStack() as ctx:
        def sb(n, shape, dt=F32, c=ctx):
            return c.enter_context(nc.sbuf_tensor(n, shape, dt))

        def sem(n):
            return ctx.enter_context(nc.semaphore(n))

        x = sb("x_all", [P, B, D])
        k = Constants()
        at, widths = 0, (("ident", P), ("causal", S), ("window", S), ("even_rows", 1),
                         ("odd_rows", 1), ("iota", E), ("l0_rope", 4 * HD), ("freq", HD // 2))
        tables = sb("tables", [P, sum(w for _, w in widths)])
        table = {}
        for n, w in widths:
            table[n] = tables[:, at:at + w]
            at += w
        k.ident, k.even_rows, k.odd_rows, k.iota = (
            table[n] for n in ("ident", "even_rows", "odd_rows", "iota"))
        k.ident_bf = sb("ident_bf", [P, P], BF16)
        k.ones = sb("ones", [P, P])
        k.minus_half = sb("minus_half", [P, 2 * H])
        k.eps = sb("eps", [P, 1])
        k.rms_eps = sb("rms_eps", [P, 2 * H])
        clips = sb("clips", [P, 2])
        x_loaded = [sem("x_loaded0"), sem("x_loaded1")]
        k.constants_done = sem("constants_done")

        with ExitStack() as early:
            def big(n, shape, dt=F32):
                return sb(n, shape, dt, early)

            causal = big("causal", [P, S], BF16)
            window = big("window", [P, S], BF16)
            l0_rope = table["l0_rope"]
            l1_rope = big("l1_rope", [P, B, 4 * HD])
            weights, loaded = {}, {}
            for n, shape in (("L0_attn_w_in", [P, KC, 3 * D]), ("L0_attn_w_out", [P, KC, D]),
                             ("L0_xattn_w_in", [P, KC, 3 * D]), ("L0_router", [P, KC, E]),
                             ("L0_experts", [P, KC, E * D]), ("L1_attn_w_in", [P, KC, 3 * D]),
                             ("L1_attn_w_out", [P, KC, D]), ("L1_xattn_w_in", [P, KC, 3 * D]),
                             ("L1_xattn_w_out", [P, KC, D])):
                weights[n] = big(f"{n}_sb", shape)
                loaded[n] = (sem(f"{n}_loaded"), 16)
            rows_of = {}
            for n, width in (("L0_attn_bias", 3 * D), ("L0_attn_bo", D), ("L0_xattn_bv", D),
                             ("L0_router_b", E)):
                rows_of[n] = big(f"{n}_sb", [P, width])
            l0_xattn_bq = big("l0_xattn_bq", [P, KC])
            l0_xattn_bk = big("l0_xattn_bk", [P, KC])
            expert_bias = big("expert_bias", [E, D])

            with ExitStack() as part:
                scale = sb("l0_scale", [P, 1], F32, part)
                pos = sb("pos", [P, B], F32, part)
                norm_w = sb("norm_w", [P, 2, HD], F32, part)
                angle = sb("angle", [P, B, HD // 2], F32, part)
                turns = sb("turns", [P, B, HD // 2], F32, part)
                cosine = sb("cosine", [P, B, HD // 2], F32, part)
                sine = sb("sine", [P, B, HD // 2], F32, part)
                minus_sine = sb("minus_sine", [P, B, HD // 2], F32, part)
                small = [sem(f"small{i}") for i in range(10)]
                sin_angle, cos_angle, sin_done, chain = map(sem, ("sin_angle", "cos_angle",
                                                                   "sin_done", "setup_chain"))
                block = part.enter_context(nc.Block())

                def spread(row, width):
                    return row.rearrange("(a n) -> a n", a=1).broadcast_to([P, width])

                smalls = [(tables[:], a["tables"]), (pos[:], a["pos_t"]),
                          (scale[:], spread(a["L0_scale"], 1)),
                          (norm_w[:, 0, :], spread(a["L1_q_norm"], HD)),
                          (norm_w[:, 1, :], spread(a["L1_k_norm"], HD)),
                          (clips[:, 0:1], spread(a["clip_x"], 1)),
                          (clips[:, 1:2], spread(a["clip_down"], 1)),
                          (l0_xattn_bq[:], a["L0_xattn_bq"]),
                          (l0_xattn_bk[:], a["L0_xattn_bk"]),
                          (expert_bias[:], a["L0_expert_b"])]
                row_loads = [sem(f"row{i}") for i in range(4)]

                @block.sync
                def _(sp):
                    for n in ("L0_attn_w_in", "L0_attn_w_out"):
                        sp.dma_start(weights[n][:], a[n].rearrange("(c p) n -> p c n", p=P)
                                     ).then_inc(loaded[n][0], 16)
                    sp.dma_start(x[:, 0:4, :], a["x"][0:4].rearrange("b t d -> t b d")
                                 ).then_inc(x_loaded[0], 16)
                    for i, (n, row) in enumerate(rows_of.items()):
                        sp.dma_start(row[:], spread(a[n], row.shape[1])).then_inc(row_loads[i], 16)
                    for s in (row_loads[-1], small[-1]):
                        sp.wait_ge(s, 16)
                    sp.dma_start(x[:, 4:B, :], a["x"][4:B].rearrange("b t d -> t b d")
                                 ).then_inc(x_loaded[1], 16)
                    for n in list(weights)[2:]:
                        src = a[n].rearrange("(c p) n -> p c n", p=P)
                        sp.dma_start(weights[n][:], src).then_inc(loaded[n][0], 16)

                @block.scalar
                def _(act):
                    for i, (dst, src) in enumerate(smalls):
                        act.dma_start(dst, src).then_inc(small[i], 16)
                    act.wait_ge(sin_angle, 1)
                    act.activation(sine[:], angle[:], ACT.Sin).then_inc(sin_done, 1)
                    act.wait_ge(cos_angle, 1)
                    act.activation(cosine[:], turns[:], ACT.Sin).then_inc(sin_done, 1)

                @block.vector
                def _(dve):
                    steps = [0]

                    def step(instruction):
                        steps[0] += 1
                        instruction.then_inc(chain, 1)
                        dve.wait_ge(chain, steps[0])

                    dve.memset(k.ones[:], 1.0)
                    dve.memset(k.minus_half[:], -0.5)
                    dve.memset(k.eps[:], EPS)
                    dve.memset(k.rms_eps[:], HD * RMS_EPS)
                    for s in small[0:5]:
                        dve.wait_ge(s, 16)
                    dve.tensor_copy(k.ident_bf[:], k.ident[:])
                    dve.tensor_copy(causal[:], table["causal"])
                    dve.tensor_copy(window[:], table["window"])
                    for lo in (0, 2 * HD):
                        dve.tensor_scalar(l0_rope[:, lo:lo + HD], l0_rope[:, lo:lo + HD], scale[:],
                                          None, ALU.mult)
                    dve.tensor_scalar(norm_w[:, 1, :], norm_w[:, 1, :], HD ** 0.5, None, ALU.mult)
                    step(dve.tensor_tensor(angle[:], pos[:, :, None].broadcast_to([P, B, HD // 2]),
                                           table["freq"][:, None, :].broadcast_to([P, B, HD // 2]), ALU.mult))
                    step(dve.tensor_scalar(turns[:], angle[:], 1.0 / TWO_PI, ROUND, ALU.mult, ALU.add))
                    step(dve.tensor_scalar(turns[:], turns[:], -ROUND, None, ALU.add))
                    for part_of in PI_PARTS:
                        step(dve.scalar_tensor_tensor(angle[:], turns[:], -part_of, angle[:],
                                                      ALU.mult, ALU.add))
                    dve.tensor_scalar(angle[:], angle[:], -PI_BELOW, PI_BELOW, ALU.max, ALU.min
                                      ).then_inc(sin_angle, 1)
                    dve.wait_ge(sin_angle, 1)
                    step(dve.tensor_scalar(minus_sine[:], angle[:], PI_BELOW / 2, -TWO_PI, ALU.is_gt,
                                           ALU.mult))
                    step(dve.tensor_scalar(turns[:], angle[:], float(np.pi / 2), None, ALU.add))
                    step(dve.tensor_tensor(turns[:], turns[:], minus_sine[:], ALU.add))
                    dve.tensor_scalar(turns[:], turns[:], -PI_BELOW, PI_BELOW, ALU.max, ALU.min
                                      ).then_inc(cos_angle, 1)
                    dve.wait_ge(sin_done, 2)
                    step(dve.tensor_scalar(minus_sine[:], sine[:], -1.0, None, ALU.mult))
                    for s in small[5:] + row_loads:
                        dve.wait_ge(s, 16)
                    half = HD // 2
                    for which in range(2):
                        for f in range(2):
                            w = norm_w[:, which, f * half:(f + 1) * half]
                            v = norm_w[:, which, (1 - f) * half:(2 - f) * half]
                            at = which * HD + f * half
                            dve.tensor_tensor(l1_rope[:, :, at:at + half], cosine[:],
                                              w[:, None, :].broadcast_to([P, B, half]), ALU.mult)
                            last = dve.tensor_tensor(
                                l1_rope[:, :, 2 * HD + at:2 * HD + at + half],
                                (minus_sine, sine)[f][:],
                                v[:, None, :].broadcast_to([P, B, half]), ALU.mult)
                    last.then_inc(k.constants_done, 1)

            w = weights
            heads_attention(nc, "l0a", x, k, w["L0_attn_w_in"], w["L0_attn_w_out"],
                            qkv_bias=rows_of["L0_attn_bias"], out_bias=rows_of["L0_attn_bo"],
                            mask=causal, rope=l0_rope,
                            loads=[loaded["L0_attn_w_in"], loaded["L0_attn_w_out"]],
                            x_arrives={0: x_loaded[0], 4: x_loaded[1]})
            context_attention(nc, "l0x", x, k, w["L0_xattn_w_in"], l0_xattn_bq, l0_xattn_bk,
                              rows_of["L0_xattn_bv"], a["ctx_t"], [loaded["L0_xattn_w_in"]])
            experts(nc, "l0f", x, k, w["L0_router"], rows_of["L0_router_b"], w["L0_experts"],
                    expert_bias, [loaded["L0_router"], loaded["L0_experts"]])
            heads_attention(nc, "l1a", x, k, w["L1_attn_w_in"], w["L1_attn_w_out"], mask=window,
                            scale=HD ** -0.5,
                            loads=[loaded["L1_attn_w_in"], loaded["L1_attn_w_out"]])
            heads_attention(nc, "l1x", x, k, w["L1_xattn_w_in"], w["L1_xattn_w_out"],
                            batch_rope=l1_rope, ctx_t=a["ctx_t"],
                            loads=[loaded["L1_xattn_w_in"], loaded["L1_xattn_w_out"]])
        quantised_ffn(nc, "l1f", x, k, a["w_gate"], a["w_up"], a["w_down"], clips, out, [])


PI_PARTS = [6.28125, float(np.float32(0.0019350051879882812)),
            float(TWO_PI - 6.28125 - np.float32(0.0019350051879882812))]
PI_BELOW = float(np.nextafter(np.float32(np.pi), np.float32(0)))


def constants():
    half = HD // 2
    freq = (10000.0 ** (-np.arange(0, HD, 2, dtype=np.float32) / np.float32(HD))).astype(np.float32)
    angle = (np.arange(S, dtype=np.float32)[:, None] * freq).astype(np.float32).astype(np.float64)
    cos, sin = np.cos(angle), np.sin(angle)
    rope = np.concatenate([cos, cos, cos, cos, -sin, sin, -sin, sin], 1).astype(np.float32)
    q, key = np.arange(S)[:, None], np.arange(S)[None, :]
    odd = (np.arange(P) // HD % 2).astype(np.float32)[:, None]
    return {"tables": np.concatenate([
        np.eye(P), np.where(key > q, NEG, 0.0), np.where((key > q) | (key <= q - 64), NEG, 0.0),
        1 - odd, odd, np.broadcast_to(np.arange(E), (P, E)), rope,
        np.broadcast_to(freq, (P, half))], 1).astype(np.float32)}


def kernel(**inputs):
    import numpy as _np
    import concourse.bacc as _bacc
    from concourse import mybir as _mybir
    from concourse.bass_utils import run_bass_kernel_spmd as _run

    i = {n: _np.asarray(v) for n, v in inputs.items()}
    order = _np.arange(D).reshape(H, HD // 2, 2).transpose(0, 2, 1).reshape(D)
    arrays = {
        "x": i["x"], "ctx_t": i["ctx_1024"].transpose(0, 2, 1), "pos_t": i["fside_BxS2_0"].T,
        "L0_attn_w_in": _np.concatenate([i["L0_attn_Wq"][order].T, i["L0_attn_Wk"][order].T,
                                         i["L0_attn_Wv"].T], 1),
        "L0_attn_w_out": i["L0_attn_Wo"].T,
        "L0_attn_bias": _np.concatenate([i["L0_attn_bq"][order], i["L0_attn_bk"][order],
                                         i["L0_attn_bv"]]),
        "L0_attn_bo": i["L0_attn_bo"], "L0_scale": i["L0_attn_scale"],
        "L0_xattn_w_in": _np.concatenate([i["L0_xattn_Wq_w"].T, i["L0_xattn_Wk_w"].T,
                                          i["L0_xattn_Wv_w"].T], 1),
        "L0_xattn_bq": i["L0_xattn_Wq_b"].reshape(KC, P).T,
        "L0_xattn_bk": i["L0_xattn_Wk_b"].reshape(KC, P).T,
        "L0_xattn_bv": i["L0_xattn_Wv_b"],
        "L0_router": i["L0_ffn_router_w"], "L0_router_b": i["L0_ffn_router_b"],
        "L0_experts": i["L0_ffn_expert_w"].transpose(1, 0, 2).reshape(D, E * D),
        "L0_expert_b": i["L0_ffn_expert_b"],
        "L1_attn_w_in": i["L1_attn_W_qkv"], "L1_attn_w_out": i["L1_attn_W_out"],
        "L1_xattn_w_in": _np.concatenate([i["L1_xattn_Wq"], i["L1_xattn_Wkv"]], 1),
        "L1_xattn_w_out": i["L1_xattn_Wo"],
        "L1_q_norm": i["L1_xattn_q_norm_w"], "L1_k_norm": i["L1_xattn_k_norm_w"],
        "clip_x": i["L1_ffn_clip_x"], "clip_down": i["L1_ffn_clip_down"],
        "w_gate": i["L1_ffn_w_gate"], "w_up": i["L1_ffn_w_up"], "w_down": i["L1_ffn_w_down"],
        **constants(),
    }
    nc = _bacc.Bacc("TRN2", target_bir_lowering=False, num_devices=1)
    launched, aps = {}, {}
    for name, value in arrays.items():
        value = _np.ascontiguousarray(value)
        launched[f"in_{name}"] = value
        aps[name] = nc.dram_tensor(f"in_{name}", value.shape, _mybir.dt.from_np(value.dtype),
                                   kind="ExternalInput").ap()
    out = nc.dram_tensor("out", (B, S, D), _mybir.dt.float32, kind="ExternalOutput").ap()
    decoder(nc, aps, out)
    r = _run(nc, [launched], core_ids=[0])
    return r.results[0]["out"]
```

```python
import numpy as np
import concourse.bass as bass
from concourse import mybir
from contextlib import ExitStack

F32 = mybir.dt.float32
BF16 = mybir.dt.bfloat16
F32R = mybir.dt.float32r
U32 = mybir.dt.uint32
ALU = mybir.AluOpType
ACT = mybir.ActivationFunctionType
AX = mybir.AxisListType

B, S, D = 32, 128, 256
P = 128
KC = D // P
H, HD = 16, 16
HG = 4
E = 8
I = 704
IC = -(-I // P)
EPS = 1e-5
RMS_EPS = float(np.finfo(np.float32).eps)
QMAX = 127.0
ROUND = 1.5 * 2.0 ** 23
TWO_PI = 2.0 * np.pi
NEG = -1e30


def rows(c):
    return min(P, I - c * P)


def waits(eng, sem, value):
    if isinstance(value, int) and value <= 0:
        return
    eng.wait_ge(sem, value)


def pipeline(eng, body, depth, turn=2, count=B):
    last = count + depth - 1
    head = 1 + turn if turn > 2 else 2 * turn
    steady = (count - head) // turn * turn
    for t in range(head):
        body(t, t % turn, lambda s, t=t: 0 <= t - s < count)
    with eng.Fori(head, head + steady - turn + 1, turn) as t:
        for i in range(turn):
            body(t + i, (head + i) % turn, lambda s: True)
    for t in range(head + steady, last):
        body(t, t % turn, lambda s, t=t: 0 <= t - s < count)


def apart(eng, k):
    eng.wait_ge(k.constants_done, 1)


def clear(nc, sems):
    with nc.Block() as block:
        @block.gpsimd
        def _(pool):
            for s in sems:
                pool.sem_clear(s)


def seq(x, b):
    if isinstance(b, int):
        return x[:, b, :]
    return x[:, bass.ds(b, 1), :].rearrange("p a d -> p (a d)")


def head_rows(h):
    return h // 8, h % 8 // 2, h % 2


def group_heads(g):
    return [8 * c + 2 * g + half for c in range(2) for half in range(2)]


class Norm:

    def __init__(self, ctx, nc, name, sem):
        self.stats = ctx.enter_context(nc.sbuf_tensor(f"{name}_stats", [P, 2, 6], F32))
        self.mean_var = ctx.enter_context(nc.sbuf_tensor(f"{name}_mean_var", [P, 2, 2], F32))
        self.var_eps = ctx.enter_context(nc.sbuf_tensor(f"{name}_var_eps", [P, 2, 1], F32))
        self.rstd = ctx.enter_context(nc.sbuf_tensor(f"{name}_rstd", [P, 2, 1], F32))
        self.mean_done = sem("mean_done")
        self.eps_added = sem("eps_added")
        self.rstd_done = sem("rstd_done")


def norm_statistics(dve, n, k, x, b, par):
    waits(dve, n.rstd_done, b - 1)
    dve.bn_stats(n.stats[:, par, :], seq(x, b))
    dve.drain()
    dve.bn_aggr(n.mean_var[:, par, :], n.stats[:, par, :]).then_inc(n.mean_done, 1)


def norm_rstd(pool, n, k, b, par):
    pool.wait_ge(n.mean_done, b + 1)
    pool.tensor_tensor(n.var_eps[:, par, :], n.mean_var[:, par, 1:2], k.eps[:, 0:1], ALU.add).then_inc(n.eps_added, 1)
    pool.wait_ge(n.eps_added, b + 1)
    pool.tensor_tensor(n.rstd[:, par, :], n.var_eps[:, par, :], k.minus_half[:, 0:1],
                       ALU.pow).then_inc(n.rstd_done, 1)


def heads_attention(nc, name, x, k, w_in, w_out, qkv_bias=None, out_bias=None, mask=None,
                    rope=None, batch_rope=None, ctx_t=None, scale=1.0, loads=(),
                    x_arrives={}, pool_after=None):
    SC = 2 if rope is None and batch_rope is None else 3
    QT, WV, OUT = SC - 1, SC + 1, SC + 2
    with ExitStack() as ctx:
        sems = []
        def sb(n, shape, dt=F32):
            return ctx.enter_context(nc.sbuf_tensor(f"{name}_{n}", shape, dt))

        def bank(n):
            return ctx.enter_context(nc.psum_tensor(f"{name}_{n}", [P, 512], F32))

        def sem(n):
            sems.append(ctx.enter_context(nc.semaphore(f"{name}_{n}")))
            return sems[-1]

        split = isinstance(w_in, tuple)
        rotated = rope is not None or batch_rope is not None
        norm = Norm(ctx, nc, name, sem)
        xn = sb("xn", [P, 2, D])
        xn_t = sb("xn_t", [P, 2, KC, S], F32R if split else F32)
        if split:
            xn_low = sb("xn_low", [P, 2, KC, S], F32R)
            xn_low_done = sem("xn_low_done")
        if ctx_t is not None:
            c_t = sb("c_t", [P, 2, KC, S])
            c_loaded = [sem(f"c_loaded{i}") for i in range(2)]
        if rotated:
            qk = sb("qk", [P, 2 * D])
            by_cos = sb("by_cos", [P, 2, 2 * D])
            by_sin = sb("by_sin", [P, 2 * D])
            qk_rot = sb("qk_rot", [P, 2, 2 * D])
        if batch_rope is not None:
            squares = sb("squares", [P, 2 * D])
            sum_sq = sb("sum_sq", [P, 2 * H])
            rms = sb("rms", [P, 2, 2 * H])
            squared, summed, rms_eps, rms_done, turned = map(
                sem, ("squared", "summed", "rms_eps", "rms_done", "turned"))
        q_t = sb("q_t", [P, 2, KC, S])
        k_t = sb("k_t", [P, 2, 2, KC, S])
        v = sb("v", [P, 4, H, 2 * HD])
        neg_max = sb("neg_max", [P, 2, HG, 4])
        total = sb("total", [P, 2, HG, 4])
        share = sb("share", [P, 2, HG, 4])
        probs = sb("probs", [P, 2, HG, 4, S])
        probs_t = sb("probs_t", [P, 2, 4, S])
        o_t = sb("o_t", [P, KC, S])
        xv_bank, qk_bank, oo_bank, qkt_bank = map(bank, ("xv_bank", "qk_bank", "oo_bank", "qkt_bank"))
        score_banks = [bank(f"scores{i}") for i in range(2)]
        pt_banks = [bank(f"pt{i}") for i in range(2)]
        xn_tp, v_p = xv_bank[:, 0:D], xv_bank[:, D:2 * D]
        o_tp, out_p = oo_bank[:, 0:D], oo_bank[:, D:2 * D]

        (v_zeroed, xn_done, xn_tp_done, xn_t_done, qk_p_done, v_p_done, v_done, qk_done, cos_done,
         sin_done, rot_done, qkt_p_done, qk_t_done, scores_done, max_done,
         exp_done, share_done, probs_done, pt_p_done, pt_done, pv_done, o_t_done, out_p_done,
         x_biased, x_done) = map(sem, (
             "v_zeroed", "xn_done", "xn_tp_done", "xn_t_done", "qk_p_done", "v_p_done", "v_done",
             "qk_done", "cos_done", "sin_done", "rot_done", "qkt_p_done", "qk_t_done", "scores_done", "max_done", "exp_done", "share_done", "probs_done",
             "pt_p_done", "pt_done", "pv_done", "o_t_done", "out_p_done", "x_biased", "x_done"))

        act_copies = (1, 2, 3) if split else (1, 3)
        pt_done_by_act = sem("pt_done_by_act")

        def pt_copied(b, g):
            mine = act_copies if g in act_copies else [i for i in range(HG) if i not in act_copies]
            return (pt_done_by_act if g in act_copies else pt_done,
                    len(mine) * b + mine.index(g) + 1)

        blocks = ctx.enter_context(ExitStack())
        block = blocks.enter_context(nc.Block())

        if ctx_t is not None:
            @block.sync
            def _(sp):
                def load(b, par):
                    waits(sp, v_p_done, b - 1)
                    src = ctx_t[b] if isinstance(b, int) else \
                        ctx_t[bass.ds(b, 1)].rearrange("a d t -> (a d) t")
                    sp.dma_start(c_t[:, par, :, :], src.rearrange("(c p) t -> p c t", p=P)
                                 ).then_inc(c_loaded[par], 16)
                load(0, 0)
                load(1, 1)
                with sp.Fori(2, B - 1, 2) as t:
                    load(t, 0)
                    load(t + 1, 1)

        @block.tensor
        def _(pe):
            for s, n in loads:
                pe.wait_ge(s, n)

            def project(b, par):
                pe.wait_ge(xn_t_done, b + 1)
                waits(pe, qk_t_done if not rotated else squared if batch_rope is not None else
                      qk_done, b)
                if split:
                    w_high, w_low = w_in
                    terms = ((xn_t, w_high), (xn_t, w_low), (xn_low, w_high))
                    for n, (left, right) in enumerate(terms):
                        if n == 2:
                            pe.wait_ge(xn_low_done, b + 1)
                        for c in range(KC):
                            last = pe.matmul(qk_bank[:], left[:, par, c, :], right[:, c, 0:2 * D],
                                             start=n == c == 0, stop=n == 2 and c == KC - 1)
                elif rotated and ctx_t is None:
                    for c in range(KC):
                        last = pe.matmul(qk_bank[:], xn_t[:, par, c, :], w_in[:, c, 0:2 * D],
                                         start=c == 0, stop=c == KC - 1)
                elif rotated:
                    for c in range(KC):
                        pe.matmul(qk_bank[:, 0:D], xn_t[:, par, c, :], w_in[:, c, 0:D],
                                  start=c == 0, stop=c == KC - 1)
                    pe.wait_ge(c_loaded[par], 8 * (b - par) + 16)
                    for c in range(KC):
                        last = pe.matmul(qk_bank[:, D:2 * D], c_t[:, par, c, :], w_in[:, c, D:2 * D],
                                         start=c == 0, stop=c == KC - 1)
                else:
                    for f in range(2 * KC):
                        for c in range(KC):
                            last = pe.matmul(qk_bank[:, f * S:(f + 1) * S],
                                             w_in[:, c, f * P:(f + 1) * P], xn_t[:, par, c, :],
                                             start=c == 0, stop=c == KC - 1)
                last.then_inc(qk_p_done, 1)
                if not split:
                    terms = ((xn_t if ctx_t is None else c_t, w_in),)
                for n, (left, right) in enumerate(terms):
                    for c in range(KC):
                        last = pe.matmul(v_p, left[:, par, c, :], right[:, c, 2 * D:3 * D],
                                         start=n == c == 0, stop=n == len(terms) - 1 and c == KC - 1)
                last.then_inc(v_p_done, 1)

            def scores(b, par, g):
                ring = score_banks[g % 2]
                waits(pe, exp_done, 4 * b + g - 1)
                if g == 0:
                    pe.wait_ge(qk_t_done, b + 1)
                if mask is not None:
                    pe.matmul(ring[:], k.ident_bf[:], mask[:, None, :].broadcast_to([P, 4, S]),
                              start=True, stop=True)
                for j, h in enumerate(group_heads(g)):
                    c, _, half = head_rows(h)
                    strip = slice(32 * g, 32 * g + 32)
                    last = pe.matmul(ring[:, j * S:(j + 1) * S], q_t[strip, par, c, :],
                                     k_t[strip, par, half, c, :], start=mask is None,
                                     stop=True, skip_group_check=mask is not None)
                last.then_inc(scores_done, 1)

            def probs_transposed(b, par, g):
                pe.wait_ge(probs_done, 4 * b + g + 1)
                waits(pe, *(pt_copied(b, g - 2) if g >= 2 else pt_copied(b - 1, g + 2)))
                for j in range(4):
                    last = pe.transpose(pt_banks[g % 2][:, j * S:(j + 1) * S],
                                        probs[:, par, g, j, :], k.ident[:])
                last.then_inc(pt_p_done, 1)

            def weighted_values(b, vbuf, g):
                pe.wait_ge(*pt_copied(b, g))
                if g == 0:
                    waits(pe, x_done, b)
                    pe.wait_ge(v_done, b + 1)
                for j, h in enumerate(group_heads(g)):
                    c, _, half = head_rows(h)
                    last = pe.matmul(o_tp[32 * g:32 * g + 32, c * S:(c + 1) * S], v[:, vbuf, h, :],
                                     probs_t[:, g % 2, j, :], start=half == 0, stop=half == 1,
                                     skip_group_check=True)
                last.then_inc(pv_done, 1)

            def body(t, phase, live):
                par, other, sc, wv = phase % 2, (phase - 1) % 2, (phase - SC) % 2, (phase - WV) % 2
                qt = (phase - QT) % 2
                if live(1):
                    b = t - 1
                    pe.wait_ge(xn_done, b + 1)
                    waits(pe, v_done, b)
                    for c in range(KC):
                        last = pe.transpose(xn_tp[:, c * S:(c + 1) * S],
                                            xn[:, other, c * P:(c + 1) * P], k.ident[:])
                    last.then_inc(xn_tp_done, 1)
                if live(WV):
                    probs_transposed(t - WV, wv, 0)
                    probs_transposed(t - WV, wv, 1)
                if live(SC):
                    scores(t - SC, sc, 0)
                    scores(t - SC, sc, 1)
                if live(OUT):
                    b = t - OUT
                    pe.wait_ge(o_t_done, b + 1)
                    for c in range(KC):
                        last = pe.matmul(out_p, o_t[:, c, :], w_out[:, c, :],
                                         start=c == 0, stop=c == KC - 1)
                    last.then_inc(out_p_done, 1)
                if live(1):
                    project(t - 1, other)
                if live(QT) and rotated:
                    b = t - QT
                    pe.wait_ge(rot_done, b + 1)
                    waits(pe, qk_t_done, b)
                    for f in range(2 * KC):
                        last = pe.transpose(qkt_bank[:, f * S:(f + 1) * S],
                                            qk_rot[:, qt, f * P:(f + 1) * P], k.ident[:])
                    last.then_inc(qkt_p_done, 1)
                vbuf = (phase - WV) % 4
                for g in range(HG):
                    if live(WV):
                        weighted_values(t - WV, vbuf, g)
                        if g < 2:
                            probs_transposed(t - WV, wv, g + 2)
                    if live(SC) and g < 2:
                        scores(t - SC, sc, g + 2)
            pipeline(pe, body, OUT + 1, 4)

        @block.vector
        def _(dve):
            def body(t, phase, live):
                par, other, sc, wv = phase % 2, (phase - 1) % 2, (phase - SC) % 2, (phase - WV) % 2
                qt = (phase - QT) % 2
                def head_max(g):
                    b = t - SC
                    dve.wait_ge(scores_done, 4 * b + g + 1)
                    waits(dve, exp_done, 4 * b + g - 7)
                    dve.tensor_reduce(neg_max[:, sc, g, :],
                                      score_banks[g % 2][:].rearrange("p (j s) -> p j s", j=4),
                                      axis=AX.X, op=ALU.max, negate=True).then_inc(max_done, 1)

                def normalise(b, sc, g):
                    dve.wait_ge(exp_done, 4 * b + g + 1)
                    dve.reciprocal(share[:, sc, g, :], total[:, sc, g, :]).then_inc(share_done, 1)
                    dve.wait_ge(share_done, 4 * b + g + 1)
                    dve.tensor_tensor(probs[:, sc, g, :, :], probs[:, sc, g, :, :],
                                      share[:, sc, g, :, None].broadcast_to([P, 4, S]),
                                      ALU.mult).then_inc(probs_done, 1)

                def copy_pt(g):
                    b = t - WV
                    dve.wait_ge(pt_p_done, 4 * b + g + 1)
                    waits(dve, pv_done, 4 * b + g - 1)
                    dve.tensor_copy(probs_t[:, g % 2, :, :].rearrange("p j s -> p (j s)"),
                                    pt_banks[g % 2][:]).then_inc(pt_done, 1)

                if live(WV):
                    copy_pt(0)
                if live(WV):
                    normalise(t - WV, wv, 2)
                if live(SC):
                    head_max(0)
                if live(WV):
                    normalise(t - WV, wv, 3)
                if live(SC):
                    head_max(1)
                if live(1) and split:
                    dve.wait_ge(xn_t_done, t)
                    waits(dve, v_p_done, t - 2)
                    dve.tensor_tensor(xn_low[:, other, :, :].rearrange("p c t -> p (c t)"), xn_tp,
                                      xn_t[:, other, :, :].rearrange("p c t -> p (c t)").bitcast(F32),
                                      ALU.subtract).then_inc(xn_low_done, 1)
                if live(OUT):
                    b = t - OUT
                    dve.wait_ge(out_p_done, b + 1)
                    if out_bias is not None:
                        dve.wait_ge(x_biased, b + 1)
                    dve.tensor_tensor(seq(x, b), out_p, seq(x, b), ALU.add).then_inc(x_done, 1)
                if live(2) and batch_rope is not None:
                    b = t - 2
                    dve.wait_ge(rms_done, b + 1)
                    dve.wait_ge(turned, b + 1)
                    waits(dve, qkt_p_done, b - 1)
                    dve.tensor_tensor(qk_rot[:, par, :].rearrange("p (h d) -> p h d", d=HD),
                                      by_cos[:, par, :].rearrange("p (h d) -> p h d", d=HD),
                                      rms[:, par, :, None].broadcast_to([P, 2 * H, HD]),
                                      ALU.mult).then_inc(rot_done, 1)
                if live(SC):
                    normalise(t - SC, sc, 0)
                    normalise(t - SC, sc, 1)
                if live(0):
                    if isinstance(t, int) and t in x_arrives:
                        dve.wait_ge(x_arrives[t], 16)
                    norm_statistics(dve, norm, k, x, t, par)
                if live(1):
                    b = t - 1
                    if qkv_bias is not None:
                        if isinstance(t, int) and t == 1:
                            dve.wait_ge(v_zeroed, 1)
                        dve.wait_ge(v_p_done, b + 1)
                        waits(dve, pv_done, 4 * b - 12)
                        bias = qkv_bias[:, 2 * D:3 * D].rearrange("p (h d) -> p h d", d=HD)
                        for half in range(2):
                            last = dve.tensor_tensor(
                                v[:, (phase - 1) % 4, half:H:2, half * HD:(half + 1) * HD],
                                v_p.rearrange("p (h d) -> p h d", d=HD)[:, half:H:2, :],
                                bias[:, half:H:2, :], ALU.add)
                        last.then_inc(v_done, 1)
                if live(1) and rotated:
                    b = t - 1
                    if batch_rope is None:
                        dve.wait_ge(qk_p_done, b + 1)
                        waits(dve, sin_done, b)
                        dve.tensor_tensor(qk[:], qk_bank[:], qkv_bias[:, 0:2 * D],
                                          ALU.add).then_inc(qk_done, 1)
                    tab = rope if batch_rope is None else seq(batch_rope, b)
                    dve.wait_ge(qk_done, b + 1)
                    cos = tab[:, 0:2 * HD].rearrange("p (a d) -> p a d", a=2)
                    dve.tensor_tensor(by_cos[:, other, :].rearrange("p (a h d) -> p a h d", a=2, h=H),
                                      qk[:].rearrange("p (a h d) -> p a h d", a=2, h=H),
                                      cos[:, :, None, :].broadcast_to([P, 2, H, HD]),
                                      ALU.mult).then_inc(cos_done, 1)
                    if batch_rope is not None:
                        dve.wait_ge(squared, b + 1)
                        waits(dve, rms_done, b)
                        dve.tensor_reduce(sum_sq[:], squares[:].rearrange("p (h d) -> p h d", d=HD),
                                          axis=AX.X, op=ALU.add).then_inc(summed, 1)
                if live(WV) and 2 not in act_copies:
                    copy_pt(2)
                if live(SC):
                    head_max(2)
                if live(0):
                    dve.wait_ge(norm.rstd_done, t + 1)
                    waits(dve, xn_tp_done, t - 1)
                    dve.tensor_scalar(xn[:, par, :], seq(x, t), norm.mean_var[:, par, 0:1],
                                      norm.rstd[:, par, :], ALU.subtract, ALU.mult
                                      ).then_inc(xn_done, 1)
                if isinstance(t, int) and t == 0:
                    dve.memset(v[:], 0.0).then_inc(v_zeroed, 1)
                if live(1) and rotated:
                    b = t - 1
                    dve.wait_ge(sin_done, b + 1)
                    dve.wait_ge(cos_done, b + 1)
                    if batch_rope is None:
                        waits(dve, qkt_p_done, b - 1)
                        dve.tensor_tensor(qk_rot[:, other, :], by_cos[:, other, :], by_sin[:],
                                          ALU.add).then_inc(rot_done, 1)
                    else:
                        dve.tensor_tensor(by_cos[:, other, :], by_cos[:, other, :], by_sin[:], ALU.add
                                          ).then_inc(turned, 1)
                if live(SC):
                    head_max(3)
            pipeline(dve, body, OUT + 1, 4)

        @block.scalar
        def _(act):
            def copy_pt(b, g):
                act.wait_ge(pt_p_done, 4 * b + g + 1)
                waits(act, pv_done, 4 * b + g - 1)
                act.activation(probs_t[:, g % 2, :, :].rearrange("p j s -> p (j s)"),
                               pt_banks[g % 2][:], ACT.Copy).then_inc(pt_done_by_act, 1)

            def exps(t, par, g):
                b = t - SC
                act.wait_ge(max_done, 4 * b + g + 1)
                waits(act, probs_done, 4 * b + g - 7)
                if g == 0:
                    waits(act, pt_p_done, 4 * b - 4)
                for j in range(4):
                    last = act.activation(probs[:, par, g, j, :], score_banks[g % 2][:, j * S:(j + 1) * S],
                                          ACT.Exp, bias=neg_max[:, par, g, j:j + 1],
                                          accum_out=total[:, par, g, j:j + 1])
                last.then_inc(exp_done, 1)

            def body(t, phase, live):
                par, other, sc, wv = phase % 2, (phase - 1) % 2, (phase - SC) % 2, (phase - WV) % 2
                qt = (phase - QT) % 2
                if live(1):
                    b = t - 1
                    act.wait_ge(xn_tp_done, b + 1)
                    waits(act, v_p_done, b - 1)
                    act.activation(xn_t[:, other, :, :].rearrange("p c t -> p (c t)"), xn_tp,
                                   ACT.Copy).then_inc(xn_t_done, 1)
                if live(WV):
                    copy_pt(t - WV, 1)
                if live(SC):
                    exps(t, sc, 0)
                    exps(t, sc, 1)
                if live(1) and batch_rope is not None:
                    b = t - 1
                    act.wait_ge(qk_p_done, b + 1)
                    waits(act, sin_done, b)
                    waits(act, cos_done, b)
                    act.activation(qk[:], qk_bank[:], ACT.Copy).then_inc(qk_done, 1)
                    waits(act, summed, b)
                    act.activation(squares[:], qk_bank[:], ACT.Square).then_inc(squared, 1)
                if live(1) and qkv_bias is None:
                    b = t - 1
                    if isinstance(t, int) and t == 1:
                        act.wait_ge(v_zeroed, 1)
                    act.wait_ge(v_p_done, b + 1)
                    waits(act, pv_done, 4 * b - 12)
                    for half in range(2):
                        last = act.activation(
                            v[:, (phase - 1) % 4, half:H:2, half * HD:(half + 1) * HD],
                            v_p.rearrange("p (h d) -> p h d", d=HD)[:, half:H:2, :], ACT.Copy)
                    last.then_inc(v_done, 1)
                if live(QT):
                    b = t - QT
                    src = qkt_bank if rotated else qk_bank
                    if rotated:
                        act.wait_ge(qkt_p_done, b + 1)
                    else:
                        act.wait_ge(qk_p_done, b + 1)
                    waits(act, scores_done, 4 * b - 4)
                    act.activation(q_t[:, qt, :, :].rearrange("p c t -> p (c t)"), src[:, 0:2 * S],
                                   ACT.Copy, scale=scale)
                    for half, kept in enumerate((k.even_rows, k.odd_rows)):
                        last = act.activation(k_t[:, qt, half, :, :].rearrange("p c t -> p (c t)"),
                                              src[:, 2 * S:4 * S], ACT.Copy, scale=kept[:, 0:1])
                    last.then_inc(qk_t_done, 1)
                if live(WV):
                    if 2 in act_copies:
                        copy_pt(t - WV, 2)
                    copy_pt(t - WV, 3)
                if live(SC):
                    exps(t, sc, 2)
                if live(SC):
                    exps(t, sc, 3)
                if live(WV):
                    b = t - WV
                    act.wait_ge(pv_done, 4 * b + 4)
                    waits(act, out_p_done, b)
                    act.activation(o_t[:].rearrange("p c t -> p (c t)"), o_tp,
                                   ACT.Copy).then_inc(o_t_done, 1)
            pipeline(act, body, OUT + 1, 4)

        @block.gpsimd
        def _(pool):
            def body(t, phase, live):
                par, other, sc, wv = phase % 2, (phase - 1) % 2, (phase - SC) % 2, (phase - WV) % 2
                qt = (phase - QT) % 2
                if live(0):
                    norm_rstd(pool, norm, k, t, par)
                if live(1) and rotated:
                    b = t - 1
                    pool.wait_ge(qk_done, b + 1)
                    waits(pool, rot_done if batch_rope is None else turned, b)
                    tab = rope if batch_rope is None else seq(batch_rope, b)
                    sin = tab[:, 2 * HD:4 * HD].rearrange("p (a f d) -> p a f d", a=2, f=2)
                    dst = by_sin[:].rearrange("p (a h f d) -> p a h f d", a=2, h=H, f=2)
                    src = qk[:].rearrange("p (a h f d) -> p a h f d", a=2, h=H, f=2)
                    for f in range(2):
                        last = pool.tensor_tensor(dst[:, :, :, f, :], src[:, :, :, 1 - f, :],
                                                  sin[:, :, f, :][:, :, None, :].broadcast_to(
                                                      [P, 2, H, HD // 2]), ALU.mult)
                    last.then_inc(sin_done, 1)
                if live(1) and out_bias is not None:
                    b = t - 1
                    pool.wait_ge(xn_done, b + 1)
                    pool.tensor_tensor(seq(x, b), seq(x, b), out_bias[:], ALU.add
                                       ).then_inc(x_biased, 1)
                if live(1) and batch_rope is not None:
                    b = t - 1
                    pool.wait_ge(summed, b + 1)
                    waits(pool, rot_done, b - 1)
                    pool.tensor_tensor(sum_sq[:], sum_sq[:], k.rms_eps[:], ALU.add
                                       ).then_inc(rms_eps, 1)
                    pool.wait_ge(rms_eps, b + 1)
                    pool.tensor_tensor(rms[:, other, :], sum_sq[:], k.minus_half[:, 0:2 * H],
                                       ALU.pow).then_inc(rms_done, 1)
            pipeline(pool, body, OUT + 1, 4)
            if pool_after is not None:
                pool_after(pool)

        blocks.close()
        clear(nc, sems)


def context_attention(nc, name, x, k, w_in, q_bias, k_bias, v_bias, ctx_t, loads):
    with ExitStack() as ctx:
        sems = []
        def sb(n, shape, dt=F32):
            return ctx.enter_context(nc.sbuf_tensor(f"{name}_{n}", shape, dt))

        def bank(n):
            return ctx.enter_context(nc.psum_tensor(f"{name}_{n}", [P, 512], F32))

        def sem(n):
            sems.append(ctx.enter_context(nc.semaphore(f"{name}_{n}")))
            return sems[-1]

        norm = Norm(ctx, nc, name, sem)
        xn = sb("xn", [P, 2, D])
        xn_t = sb("xn_t", [P, 2, KC, S])
        c_t = sb("c_t", [P, 2, KC, S])
        q_t = sb("q_t", [P, 2, KC, S])
        k_t = sb("k_t", [P, 2, KC, S])
        v = sb("v", [P, 4, D])
        neg_max = sb("neg_max", [P, 2, 1])
        total = sb("total", [P, 2, 1])
        share = sb("share", [P, 4, 1])
        probs = sb("probs", [P, 2, S])
        probs_t = sb("probs_t", [P, 2, S])
        xn_bank, q_bank, k_bank, v_bank, score_bank, pt_bank, out_bank = map(
            bank, ("xn_bank", "q_bank", "k_bank", "v_bank", "score_bank", "pt_bank", "out_bank"))
        xn_tp, q_p = xn_bank[:, 0:D], q_bank[:, 0:D]
        c_loaded = [sem(f"c_loaded{i}") for i in range(2)]
        (xn_done, xn_tp_done, xn_t_done, q_p_done, k_p_done, v_p_done, v_done, q_t_done, k_t_done,
         scores_done, max_done, exp_done, share_done, pt_p_done, pt_done, out_p_done, x_done) = map(
             sem, ("xn_done", "xn_tp_done", "xn_t_done", "q_p_done", "k_p_done", "v_p_done", "v_done",
                   "q_t_done", "k_t_done", "scores_done", "max_done", "exp_done", "share_done",
                   "pt_p_done", "pt_done", "out_p_done", "x_done"))

        blocks = ctx.enter_context(ExitStack())
        block = blocks.enter_context(nc.Block())

        @block.sync
        def _(sp):
            def load(b, par):
                waits(sp, k_p_done, b - 1)
                src = ctx_t[b] if isinstance(b, int) else \
                    ctx_t[bass.ds(b, 1)].rearrange("a d t -> (a d) t")
                sp.dma_start(c_t[:, par, :, :], src.rearrange("(c p) t -> p c t", p=P)
                             ).then_inc(c_loaded[par], 16)
            load(0, 0)
            load(1, 1)
            with sp.Fori(2, B - 1, 2) as t:
                load(t, 0)
                load(t + 1, 1)

        @block.tensor
        def _(pe):
            for s, n in loads:
                pe.wait_ge(s, n)

            def body(t, phase, live):
                par, other = phase % 2, 1 - phase % 2
                if live(1):
                    b = t - 1
                    pe.wait_ge(xn_done, b + 1)
                    waits(pe, xn_t_done, b)
                    for c in range(KC):
                        last = pe.transpose(xn_tp[:, c * S:(c + 1) * S],
                                            xn[:, other, c * P:(c + 1) * P], k.ident[:])
                    last.then_inc(xn_tp_done, 1)
                if live(3):
                    b = t - 3
                    pe.wait_ge(exp_done, b + 1)
                    waits(pe, pt_done, b)
                    pe.transpose(pt_bank[:, 0:S], probs[:, other, :], k.ident[:]).then_inc(pt_p_done, 1)
                if live(2):
                    b = t - 2
                    pe.wait_ge(q_t_done, b + 1)
                    pe.wait_ge(k_t_done, b + 1)
                    waits(pe, exp_done, b)
                    for c in range(KC):
                        last = pe.matmul(score_bank[:, 0:S], q_t[:, par, c, :], k_t[:, par, c, :],
                                         start=c == 0, stop=c == KC - 1)
                    last.then_inc(scores_done, 1)
                if live(1):
                    b = t - 1
                    pe.wait_ge(c_loaded[other], 8 * (b - other) + 16)
                    waits(pe, v_done, b)
                    for c in range(KC):
                        last = pe.matmul(v_bank[:, 0:D], c_t[:, other, c, :], w_in[:, c, 2 * D:3 * D],
                                         start=c == 0, stop=c == KC - 1)
                    last.then_inc(v_p_done, 1)
                    waits(pe, k_t_done, b)
                    for f in range(KC):
                        for c in range(KC):
                            last = pe.matmul(k_bank[:, f * S:(f + 1) * S],
                                             w_in[:, c, D + f * P:D + (f + 1) * P],
                                             c_t[:, other, c, :], start=c == 0, stop=c == KC - 1)
                    last.then_inc(k_p_done, 1)
                    pe.wait_ge(xn_t_done, b + 1)
                    waits(pe, q_t_done, b)
                    for f in range(KC):
                        for c in range(KC):
                            last = pe.matmul(q_p[:, f * S:(f + 1) * S],
                                             w_in[:, c, f * P:(f + 1) * P], xn_t[:, other, c, :],
                                             start=c == 0, stop=c == KC - 1)
                    last.then_inc(q_p_done, 1)
                if live(3):
                    b = t - 3
                    pe.wait_ge(pt_done, b + 1)
                    pe.wait_ge(v_done, b + 1)
                    waits(pe, x_done, b)
                    pe.matmul(out_bank[:, 0:D], probs_t[:, other, :], v[:, (phase - 3) % 4, :],
                              start=True, stop=True).then_inc(out_p_done, 1)
            pipeline(pe, body, 4, 4)

        @block.vector
        def _(dve):
            def body(t, phase, live):
                par, other = phase % 2, 1 - phase % 2
                if live(3):
                    b = t - 3
                    dve.wait_ge(pt_p_done, b + 1)
                    waits(dve, out_p_done, b - 1)
                    dve.tensor_copy(probs_t[:, other, :], pt_bank[:, 0:S]).then_inc(pt_done, 1)
                if live(2):
                    b = t - 2
                    dve.wait_ge(scores_done, b + 1)
                    waits(dve, exp_done, b - 1)
                    dve.tensor_reduce(neg_max[:, par, :], score_bank[:, 0:S], axis=AX.X, op=ALU.max,
                                      negate=True).then_inc(max_done, 1)
                if live(0):
                    norm_statistics(dve, norm, k, x, t, par)
                if live(1):
                    b = t - 1
                    dve.wait_ge(v_p_done, b + 1)
                    waits(dve, out_p_done, b - 3)
                    dve.tensor_tensor(v[:, (phase - 1) % 4, :], v_bank[:, 0:D], v_bias[:],
                                      ALU.add).then_inc(v_done, 1)
                if live(0):
                    dve.wait_ge(norm.rstd_done, t + 1)
                    waits(dve, xn_tp_done, t - 1)
                    dve.tensor_scalar(xn[:, par, :], seq(x, t), norm.mean_var[:, par, 0:1],
                                      norm.rstd[:, par, :], ALU.subtract, ALU.mult
                                      ).then_inc(xn_done, 1)
                if live(1):
                    dve.wait_ge(q_p_done, b + 1)
                    waits(dve, scores_done, b - 1)
                    for f in range(KC):
                        last = dve.tensor_scalar(q_t[:, other, f, :], q_p[:, f * S:(f + 1) * S],
                                                 q_bias[:, f:f + 1], D ** -0.5, ALU.add, ALU.mult)
                    last.then_inc(q_t_done, 1)
                if live(2):
                    b = t - 2
                    dve.wait_ge(exp_done, b + 1)
                    dve.reciprocal(share[:, (phase - 2) % 4, :], total[:, par, :]).then_inc(share_done, 1)
                if live(3):
                    b = t - 3
                    dve.wait_ge(out_p_done, b + 1)
                    dve.wait_ge(share_done, b + 1)
                    dve.scalar_tensor_tensor(seq(x, b), out_bank[:, 0:D], share[:, (phase - 3) % 4, :],
                                             seq(x, b), ALU.mult, ALU.add).then_inc(x_done, 1)
            pipeline(dve, body, 4, 4)

        @block.scalar
        def _(act):
            def body(t, phase, live):
                par, other = phase % 2, 1 - phase % 2
                if live(1):
                    b = t - 1
                    act.wait_ge(xn_tp_done, b + 1)
                    waits(act, q_p_done, b - 1)
                    act.activation(xn_t[:, other, :, :].rearrange("p c t -> p (c t)"),
                                   xn_tp, ACT.Copy).then_inc(xn_t_done, 1)
                if live(2):
                    b = t - 2
                    act.wait_ge(max_done, b + 1)
                    waits(act, pt_p_done, b - 1)
                    waits(act, share_done, b - 1)
                    act.activation(probs[:, par, :], score_bank[:, 0:S], ACT.Exp,
                                   bias=neg_max[:, par, :], accum_out=total[:, par, :]
                                   ).then_inc(exp_done, 1)
                if live(1):
                    b = t - 1
                    act.wait_ge(k_p_done, b + 1)
                    waits(act, scores_done, b - 1)
                    for f in range(KC):
                        last = act.activation(k_t[:, other, f, :], k_bank[:, f * S:(f + 1) * S],
                                              ACT.Identity, bias=k_bias[:, f:f + 1])
                    last.then_inc(k_t_done, 1)
            pipeline(act, body, 4, 4)

        @block.gpsimd
        def _(pool):
            def body(t, phase, live):
                if live(0):
                    norm_rstd(pool, norm, k, t, phase % 2)
            pipeline(pool, body, 4, 4)

        blocks.close()
        clear(nc, sems)


def experts(nc, name, x, k, w_router, router_bias, w_experts, expert_bias, loads):
    with ExitStack() as ctx:
        sems = []
        def sb(n, shape, dt=F32):
            return ctx.enter_context(nc.sbuf_tensor(f"{name}_{n}", shape, dt))

        def bank(n):
            return ctx.enter_context(nc.psum_tensor(f"{name}_{n}", [P, 512], F32))

        def sem(n):
            sems.append(ctx.enter_context(nc.semaphore(f"{name}_{n}")))
            return sems[-1]

        norm = Norm(ctx, nc, name, sem)
        xn = sb("xn", [P, 2, D])
        xn_t = sb("xn_t", [P, 2, KC, S])
        xn_high = sb("xn_high", [P, 2, KC, S], F32R)
        xn_low = sb("xn_low", [P, 2, KC, S], F32R)
        logits = sb("logits", [P, 2, E])
        top = sb("top", [P, 8])
        best = sb("best", [P, 8], U32)
        best_f = sb("best_f", [P, 1])
        neg_max = sb("neg_max", [P, 2, 1])
        powers = sb("powers", [P, 2, E])
        total = sb("total", [P, 2, 1])
        gate = sb("gate", [P, 1])
        weight = sb("weight", [P, 2, E])
        weight_t = sb("weight_t", [E, 2, S])
        xn_bank, router_bank, weight_bank, bias_bank = map(
            bank, ("xn_bank", "router_bank", "weight_bank", "bias_bank"))
        pair_banks = [bank(f"pair{i}") for i in range(4)]
        (xn_done, xn_tp_done, xn_t_done, logits_p_done, logits_done, top_done, best_done, max_done,
         exp_done, best_f_done, gate_done, weight_done, weight_tp_done, weight_t_done, pair_done,
         bias_done, added, xn_high_done, xn_low_done) = map(sem, (
             "xn_done", "xn_tp_done", "xn_t_done", "logits_p_done", "logits_done", "top_done",
             "best_done", "max_done", "exp_done", "best_f_done", "gate_done", "weight_done",
             "weight_tp_done", "weight_t_done", "pair_done", "bias_done", "added",
             "xn_high_done", "xn_low_done"))

        blocks = ctx.enter_context(ExitStack())
        block = blocks.enter_context(nc.Block())

        @block.tensor
        def _(pe):
            for s, n in loads:
                pe.wait_ge(s, n)

            def body(t, phase, live):
                par, other = phase % 2, 1 - phase % 2
                if live(2):
                    b = t - 2
                    pe.wait_ge(weight_done, b + 1)
                    waits(pe, weight_t_done, b)
                    pe.transpose(weight_bank[0:E, 0:S], weight[:, par, :], k.ident[:]
                                 ).then_inc(weight_tp_done, 1)
                if live(1):
                    b = t - 1
                    pe.wait_ge(xn_done, b + 1)
                    waits(pe, xn_t_done, b)
                    for c in range(KC):
                        last = pe.transpose(xn_bank[:, c * S:(c + 1) * S],
                                            xn[:, other, c * P:(c + 1) * P], k.ident[:])
                    last.then_inc(xn_tp_done, 1)
                def pair(b, i):
                    waits(pe, added, 9 * b - 9 + 2 * i + 2 + (i >= E // 4))
                    for n, (xn_part, w_part) in enumerate(((xn_high, 0), (xn_high, 1), (xn_low, 0))):
                        for c in range(KC):
                            last = pe.matmul(pair_banks[i][:], xn_part[:, par, c, :],
                                             w_experts[w_part][:, c, i * 2 * D:(i + 1) * 2 * D],
                                             start=n == c == 0, stop=n == 2 and c == KC - 1)
                    last.then_inc(pair_done, 1)

                if live(2):
                    b = t - 2
                    pe.wait_ge(xn_low_done, b + 1)
                    pair(b, 0)
                if live(1):
                    b = t - 1
                    pe.wait_ge(xn_t_done, b + 1)
                    waits(pe, logits_done, b)
                    for c in range(KC):
                        last = pe.matmul(router_bank[:, 0:E], xn_t[:, other, c, :], w_router[:, c, :],
                                         start=c == 0, stop=c == KC - 1)
                    last.then_inc(logits_p_done, 1)
                if live(2):
                    b = t - 2
                    pair(b, 1)
                    pe.wait_ge(weight_t_done, b + 1)
                    waits(pe, added, 9 * b - 4)
                    pe.matmul(bias_bank[:, 0:D], weight_t[:, par, :], expert_bias[:],
                              start=True, stop=True).then_inc(bias_done, 1)
                    for i in range(2, E // 2):
                        pair(b, i)
            pipeline(pe, body, 3, 2)

        @block.vector
        def _(dve):
            def add_expert(b, par, e):
                if e % 2 == 0:
                    dve.wait_ge(pair_done, 4 * b + e // 2 + 1)
                dve.wait_ge(added, 9 * b + e + (e >= E // 2))
                dve.scalar_tensor_tensor(
                    seq(x, b), pair_banks[e // 2][:, e % 2 * D:(e % 2 + 1) * D],
                    weight[:, par, e:e + 1], seq(x, b), ALU.mult, ALU.add).then_inc(added, 1)

            def body(t, phase, live):
                par, other = phase % 2, 1 - phase % 2
                if live(2):
                    b = t - 2
                    dve.wait_ge(weight_tp_done, b + 1)
                    waits(dve, bias_done, b - 1)
                    dve.tensor_copy(weight_t[:, par, :], weight_bank[0:E, 0:S]
                                    ).then_inc(weight_t_done, 1)
                if live(0):
                    norm_statistics(dve, norm, k, x, t, par)
                if live(2):
                    add_expert(b, par, 0)
                if live(1):
                    dve.wait_ge(logits_p_done, t)
                    waits(dve, exp_done, t - 2)
                    dve.tensor_tensor(logits[:, other, :], router_bank[:, 0:E], router_bias[:],
                                      ALU.add).then_inc(logits_done, 1)
                if live(2):
                    add_expert(b, par, 1)
                if live(1):
                    apart(dve, k)
                    dve.wait_ge(logits_done, t)
                    dve.max(top[:], logits[:, other, :]).then_inc(top_done, 1)
                if live(0):
                    dve.wait_ge(norm.rstd_done, t + 1)
                    waits(dve, xn_tp_done, t - 1)
                    dve.tensor_scalar(xn[:, par, :], seq(x, t), norm.mean_var[:, par, 0:1],
                                      norm.rstd[:, par, :], ALU.subtract, ALU.mult
                                      ).then_inc(xn_done, 1)
                if live(1):
                    dve.wait_ge(top_done, t)
                    dve.tensor_scalar(neg_max[:, other, :], top[:, 0:1], -1.0, None, ALU.mult
                                      ).then_inc(max_done, 1)
                    dve.max_index(best[:], top[:], logits[:, other, :]).then_inc(best_done, 1)
                if live(2):
                    add_expert(b, par, 2)
                if live(1):
                    dve.wait_ge(best_done, t)
                    dve.tensor_copy(best_f[:], best[:, 0:1]).then_inc(best_f_done, 1)
                    dve.wait_ge(exp_done, t)
                    dve.reciprocal(gate[:], total[:, other, :]).then_inc(gate_done, 1)
                if live(2):
                    add_expert(b, par, 3)
                if live(1):
                    dve.wait_ge(gate_done, t)
                    dve.wait_ge(best_f_done, t)
                    dve.tensor_scalar(weight[:, other, :], k.iota[:], best_f[:], gate[:],
                                      ALU.is_equal, ALU.mult).then_inc(weight_done, 1)
                if live(2):
                    dve.wait_ge(bias_done, b + 1)
                    dve.wait_ge(added, 9 * b + E // 2)
                    dve.tensor_tensor(seq(x, b), bias_bank[:, 0:D], seq(x, b), ALU.add
                                      ).then_inc(added, 1)
                if live(1):
                    dve.wait_ge(xn_high_done, t)
                    waits(dve, pair_done, 4 * (t - 1) - 4)
                    dve.tensor_tensor(xn_low[:, other, :, :].rearrange("p c t -> p (c t)"),
                                      xn_t[:, other, :, :].rearrange("p c t -> p (c t)"),
                                      xn_high[:, other, :, :].rearrange("p c t -> p (c t)").bitcast(F32),
                                      ALU.subtract).then_inc(xn_low_done, 1)
                if live(2):
                    for e in range(E // 2, E):
                        add_expert(b, par, e)
            pipeline(dve, body, 3, 2)

        @block.scalar
        def _(act):
            def body(t, phase, live):
                par, other = phase % 2, 1 - phase % 2
                if live(1):
                    b = t - 1
                    act.wait_ge(xn_tp_done, b + 1)
                    waits(act, pair_done, 4 * b - 4)
                    waits(act, logits_p_done, b - 1)
                    act.activation(xn_t[:, other, :, :].rearrange("p c t -> p (c t)"),
                                   xn_bank[:, 0:D], ACT.Copy).then_inc(xn_t_done, 1)
                    act.wait_ge(xn_t_done, b + 1)
                    waits(act, xn_low_done, b - 1)
                    act.activation(xn_high[:, other, :, :].rearrange("p c t -> p (c t)"),
                                   xn_t[:, other, :, :].rearrange("p c t -> p (c t)"), ACT.Copy
                                   ).then_inc(xn_high_done, 1)
                    act.wait_ge(max_done, b + 1)
                    waits(act, gate_done, b - 1)
                    act.activation(powers[:, other, :], logits[:, other, :], ACT.Exp,
                                   bias=neg_max[:, other, :], accum_out=total[:, other, :]
                                   ).then_inc(exp_done, 1)
            pipeline(act, body, 3, 2)

        @block.gpsimd
        def _(pool):
            def body(t, phase, live):
                if live(0):
                    norm_rstd(pool, norm, k, t, phase % 2)
            pipeline(pool, body, 3, 2)

        blocks.close()
        clear(nc, sems)


U = 4
UNITS = B // U
UT = U * S


def unit(x, u):
    if isinstance(u, int):
        return x[:, u]
    return x[:, bass.ds(u, 1)].rearrange("p a n -> p (a n)")


def quantised_ffn(nc, name, x, k, w_gate, w_up, w_down, clips, out, loads):
    with ExitStack() as ctx:
        def sb(n, shape, dt=F32, c=ctx):
            return c.enter_context(nc.sbuf_tensor(f"{name}_{n}", shape, dt))

        def bank(n, c, dt=F32):
            return c.enter_context(nc.psum_tensor(f"{name}_{n}", [P, 2048 // (4 if dt == F32 else 2)], dt))

        def sem(n):
            return ctx.enter_context(nc.semaphore(f"{name}_{n}"))

        gate_t = sb("gate_t", [P, KC, I], BF16)
        up_t = sb("up_t", [P, KC, I], BF16)
        down_t = sb("down_t", [P, IC, D], BF16)
        gate_scale = sb("gate_scale", [P, IC])
        up_scale = sb("up_scale", [P, IC])
        down_scale = sb("down_scale", [P, KC])
        down_row = sb("down_row", [P, D])
        sig = sb("sig", [P, 2])
        act_scale = sb("act_scale", [P, 2])
        act_inverse = sb("act_inverse", [P, 2])
        seq_max = sb("seq_max", [P, B])
        row_max = sb("row_max", [P, 2])
        one_max = sb("one_max", [1, 2])
        xn_all = sb("xn_all", [P, UNITS, U * D])

        def whole_max(dve_or_pe, which, src, bank_, maxed, turned, taken, spread):
            if dve_or_pe is nc.vector:
                dve = dve_or_pe
                dve.tensor_reduce(row_max[:, which:which + 1], src, axis=AX.X, op=ALU.max
                                  ).then_inc(maxed, 1)
                dve.wait_ge(turned, 1)
                dve.tensor_reduce(one_max[:, which:which + 1], bank_[0:1, 0:P], axis=AX.X,
                                  op=ALU.max).then_inc(taken, 1)
                dve.wait_ge(spread, 1)
            else:
                pe = dve_or_pe
                pe.wait_ge(maxed, 1)
                pe.transpose(bank_[0:1, 0:P], row_max[:, which:which + 1], k.ident[:]
                             ).then_inc(turned, 1)
                pe.wait_ge(taken, 1)
                pe.matmul(bank_[:, P:P + 1], k.ones[0:1, :], one_max[:, which:which + 1],
                          start=True, stop=True).then_inc(spread, 1)

        with ExitStack() as part:
            norm = Norm(part, nc, name, sem)
            names = ("gate", "up", "down")
            shapes = dict(gate=[P, IC, D], up=[P, IC, D], down=[P, KC, I])
            raw = {n: sb(f"{n}_raw", shapes[n], F32, part) for n in names}
            inverse = {n: sb(f"{n}_inverse", [P, shapes[n][1]], F32, part) for n in names}
            ints = {n: sb(f"{n}_ints", shapes[n], BF16, part) for n in names}
            scale = dict(gate=gate_scale, up=up_scale, down=down_scale)
            diagonal = sb("diagonal", [P, KC, P], F32, part)
            exps = sb("exps", [P, 2], F32, part)
            turn_banks = [bank(f"turn{i}", part, BF16) for i in range(4)]
            row_bank = bank("row_bank", part)
            (tails, chain, sig_exp, inverted, w_scaled, clipped_w, ints_done, turned, copied,
             diag_done, row_done, xn_done, xn_maxed, x_maxed, x_turned, x_taken, x_spread) = map(
                 sem, ("tails", "chain", "sig_exp", "inverted", "w_scaled", "clipped_w",
                       "ints_done", "turned", "copied", "diag_done", "row_done", "xn_done",
                       "xn_maxed", "x_maxed", "x_turned", "x_taken", "x_spread"))
            before = 9
            halves = ((0, before), (before, B - before))
            last_rows = rows(IC - 1)
            block = part.enter_context(nc.Block())
            w_loads = [sem(f"w_loaded{i}") for i in range(5)]

            turns = []
            for n, dst in (("gate", gate_t), ("up", up_t)):
                for h in range(KC):
                    turns.append(([(n, c, h * P, rows(c), P, c * P) for c in range(IC)],
                                  dst[:, h, :], P, I))
            for first, last in ((0, 4), (4, 5), (5, 6)):
                r = rows(first)
                turns.append(([("down", c, i * P, P, r, (i - first) * D + c * P)
                               for i in range(first, last) for c in range(KC)],
                              down_t[0:r, first:last, :].rearrange("p i d -> p (i d)"),
                              r, (last - first) * D))

            @block.sync
            def _(sp):
                sp.wait_ge(tails, 2)
                for n, src, i in (("gate", w_gate, 0), ("up", w_up, 2)):
                    full = (IC - 1) * P
                    sp.dma_start(raw[n][:, 0:IC - 1, :],
                                 src[0:full, :].rearrange("(c p) h -> p c h", p=P)
                                 ).then_inc(w_loads[i], 16)
                    sp.dma_start(raw[n][0:last_rows, IC - 1, :], src[full:I, :]
                                 ).then_inc(w_loads[i + 1], 16)
                sp.dma_start(raw["down"][:], w_down.rearrange("(c p) i -> p c i", p=P)
                             ).then_inc(w_loads[4], 16)

            @block.gpsimd
            def _(pool):
                for n in ("gate", "up"):
                    pool.memset(raw[n][last_rows:P, IC - 1, :], 1.0).then_inc(tails, 1)
                pool.wait_ge(tails, 2)

                def body(b, par, live):
                    norm_rstd(pool, norm, k, b, par)
                for start, count in halves:
                    pipeline(pool, lambda t, phase, live: body(start + t, (start + phase) % 2, live),
                             1, 4, count)

            @block.scalar
            def _(act):
                act.activation(exps[:], clips[:], ACT.Exp, scale=-1.0).then_inc(sig_exp, 1)
                for number, n in enumerate(names):
                    act.wait_ge(inverted, number + 1)
                    for c in range(shapes[n][1]):
                        last = act.activation(raw[n][:, c, :], raw[n][:, c, :], ACT.Copy, bias=ROUND,
                                              scale=inverse[n][:, c:c + 1])
                    last.then_inc(w_scaled, 1)
                for number, n in enumerate(names):
                    act.wait_ge(clipped_w, number + 1)
                    act.activation(ints[n][:], raw[n][:], ACT.Copy, bias=-ROUND
                                   ).then_inc(ints_done, 1)
                for i, (_, dst, r, w) in enumerate(turns):
                    act.wait_ge(turned, i + 1)
                    act.activation(dst, turn_banks[i % 4][0:r, 0:w], ACT.Copy).then_inc(copied, 1)

            @block.tensor
            def _(pe):
                for i, (blocks, _, _, _) in enumerate(turns):
                    pe.wait_ge(ints_done, names.index(blocks[0][0]) + 1)
                    waits(pe, copied, i - 3)
                    for n, c, at, r, w, to in blocks:
                        last = pe.transpose(turn_banks[i % 4][0:w, to:to + r],
                                            ints[n][0:r, c, at:at + w], k.ident_bf[0:r, 0:r])
                    last.then_inc(turned, 1)
                pe.wait_ge(diag_done, KC)
                for c in range(KC):
                    last = pe.matmul(row_bank[:, c * P:(c + 1) * P], k.ones[:], diagonal[:, c, :],
                                     start=True, stop=True)
                last.then_inc(row_done, 1)
                whole_max(pe, 0, None, row_bank[:, D:2 * D], x_maxed, x_turned, x_taken, x_spread)

            @block.vector
            def _(dve):
                steps = [0]

                def step(instruction):
                    steps[0] += 1
                    instruction.then_inc(chain, 1)
                    dve.wait_ge(chain, steps[0])

                flat = xn_all[:].rearrange("p u (s d) -> p (u s) d", d=D)

                def body(t, par, live):
                    if live(0):
                        norm_statistics(dve, norm, k, x, t, par)
                    if live(1):
                        b = t - 1
                        dve.wait_ge(norm.rstd_done, b + 1)
                        dve.tensor_scalar(seq(flat, b), seq(x, b), norm.mean_var[:, 1 - par, 0:1],
                                          norm.rstd[:, 1 - par, :], ALU.subtract, ALU.mult
                                          ).then_inc(xn_done, 1)
                    if live(2):
                        b = t - 2
                        dve.wait_ge(xn_done, b + 1)
                        dst = seq_max[:, b:b + 1] if isinstance(b, int) else seq_max[:, bass.ds(b, 1)]
                        dve.tensor_reduce(dst, seq(flat, b), axis=AX.X, op=ALU.max,
                                          apply_absolute_value=True).then_inc(xn_maxed, 1)

                def norms(start, count):
                    pipeline(dve, lambda t, phase, live: body(start + t, (start + phase) % 2, live),
                             3, 4, count)

                norms(*halves[0])
                for number, n in enumerate(names):
                    for i in ((0, 1), (2, 3), (4,))[number]:
                        dve.wait_ge(w_loads[i], 16)
                    step(dve.tensor_reduce(scale[n][:], raw[n][:], axis=AX.X, op=ALU.max,
                                           apply_absolute_value=True))
                    step(dve.tensor_scalar(scale[n][:], scale[n][:], 1.0 / QMAX, None, ALU.mult))
                    dve.reciprocal(inverse[n][:], scale[n][:]).then_inc(inverted, 1)
                for c in range(KC):
                    dve.tensor_scalar(diagonal[:, c, :], k.ident[:], down_scale[:, c:c + 1], None,
                                      ALU.mult).then_inc(diag_done, 1)
                dve.wait_ge(sig_exp, 1)
                step(dve.tensor_scalar(exps[:], exps[:], 1.0, None, ALU.add))
                step(dve.reciprocal(sig[:], exps[:]))
                for number, n in enumerate(names):
                    dve.wait_ge(w_scaled, number + 1)
                    dve.tensor_scalar(raw[n][:], raw[n][:], ROUND - QMAX - 1.0, ROUND + QMAX,
                                      ALU.max, ALU.min).then_inc(clipped_w, 1)
                norms(*halves[1])
                dve.wait_ge(row_done, 1)
                step(dve.tensor_copy(down_row[:], row_bank[:, 0:D]))
                dve.wait_ge(xn_maxed, B)
                whole_max(dve, 0, seq_max[:], row_bank[:, D:2 * D], x_maxed, x_turned, x_taken,
                          x_spread)
                step(dve.tensor_scalar(act_scale[:, 0:1], row_bank[:, D + P:D + P + 1], sig[:, 0:1],
                                       1.0 / QMAX, ALU.mult, ALU.mult))
                step(dve.reciprocal(act_inverse[:, 0:1], act_scale[:, 0:1]))
                dve.tensor_scalar(gate_scale[:], gate_scale[:], act_scale[:, 0:1], None, ALU.mult)
                step(dve.tensor_scalar(up_scale[:], up_scale[:], act_scale[:, 0:1], None, ALU.mult))
                assert steps[0] < 200

        hidden = sb("hidden", [P, UNITS, IC * UT])
        hidden_max = sb("hidden_max", [P, UNITS * IC])

        with ExitStack() as part:
            x_ints = sb("x_ints", [P, 2, U, D], BF16, part)
            x_ints_t = sb("x_ints_t", [P, 2, KC, UT], BF16, part)
            silu = sb("silu", [P, 3, UT], F32, part)
            turn_bank = bank("x_turn", part, BF16)
            gate_banks = [bank(f"gate_bank{i}", part) for i in range(3)]
            up_banks = [bank(f"up_bank{i}", part) for i in range(3)]
            max_bank = bank("max_bank", part)
            (zeroed, scaled, clipped, x_ints_done, x_turned2, x_ints_t_done, gate_done, up_done,
             silu_done, hidden_done, hidden_maxed, h_maxed, h_turned, h_taken, h_spread, sc) = map(
                 sem, ("zeroed", "scaled", "clipped", "x_ints_done", "x_turned2", "x_ints_t_done",
                       "gate_done", "up_done", "silu_done", "hidden_done", "hidden_maxed",
                       "h_maxed", "h_turned", "h_taken", "h_spread", "sc"))
            block = part.enter_context(nc.Block())

            @block.tensor
            def _(pe):
                def body(t, par, live):
                    other = 1 - par
                    if live(2):
                        u = t - 2
                        pe.wait_ge(x_ints_done, u + 1)
                        waits(pe, x_ints_t_done, u)
                        for c in range(KC):
                            for s in range(U):
                                last = pe.transpose(turn_bank[:, c * UT + s * S:c * UT + (s + 1) * S],
                                                    x_ints[:, par, s, c * P:(c + 1) * P],
                                                    k.ident_bf[:])
                        last.then_inc(x_turned2, 1)
                    if live(3):
                        u = t - 3
                        pe.wait_ge(x_ints_t_done, u + 1)
                        for i in range(IC):
                            n = IC * u + i
                            for w_t, banks, freed, done in (
                                    (gate_t, gate_banks, silu_done, gate_done),
                                    (up_t, up_banks, hidden_done, up_done)):
                                waits(pe, freed, n - 2)
                                for c in range(KC):
                                    last = pe.matmul(banks[i % 3][0:rows(i), :],
                                                     w_t[:, c, i * P:i * P + rows(i)],
                                                     x_ints_t[:, other, c, :],
                                                     start=c == 0, stop=c == KC - 1)
                                last.then_inc(done, 1)
                pipeline(pe, body, 4, 2, UNITS)
                whole_max(pe, 1, None, max_bank, h_maxed, h_turned, h_taken, h_spread)

            @block.scalar
            def _(act):
                def body(t, par, live):
                    other = 1 - par

                    def silus(first, last):
                        u = t - 3
                        for i in range(first, last):
                            n = IC * u + i
                            act.wait_ge(gate_done, n + 1)
                            waits(act, hidden_done, n - 2)
                            act.activation(silu[0:rows(i), i % 3, :], gate_banks[i % 3][0:rows(i), :],
                                           ACT.Silu, scale=gate_scale[0:rows(i), i:i + 1]
                                           ).then_inc(silu_done, 1)

                    if live(3):
                        silus(0, 2)
                    if live(2):
                        u = t - 2
                        act.wait_ge(x_turned2, u + 1)
                        waits(act, up_done, IC * (u - 1))
                        act.activation(x_ints_t[:, par, :, :].rearrange("p c t -> p (c t)"),
                                       turn_bank[:], ACT.Copy).then_inc(x_ints_t_done, 1)
                    if live(3):
                        silus(2, 4)
                    if live(0):
                        act.activation(unit(xn_all, t), unit(xn_all, t), ACT.Copy, bias=ROUND,
                                       scale=act_inverse[:, 0:1]).then_inc(scaled, 1)
                    if live(3):
                        silus(4, 5)
                    if live(1):
                        u = t - 1
                        apart(act, k)
                        act.wait_ge(clipped, u + 1)
                        waits(act, x_turned2, u - 1)
                        act.activation(x_ints[:, other, :, :].rearrange("p s d -> p (s d)"),
                                       unit(xn_all, u), ACT.Copy, bias=-ROUND
                                       ).then_inc(x_ints_done, 1)
                    if live(3):
                        silus(5, IC)
                pipeline(act, body, 4, 2, UNITS)

            @block.vector
            def _(dve):
                dve.memset(hidden_max[:], 0.0).then_inc(zeroed, 1)
                dve.wait_ge(zeroed, 1)

                def body(t, par, live):
                    if live(1):
                        u = t - 1
                        dve.wait_ge(scaled, u + 1)
                        dve.tensor_scalar(unit(xn_all, u), unit(xn_all, u), ROUND - QMAX - 1.0,
                                          ROUND + QMAX, ALU.max, ALU.min).then_inc(clipped, 1)
                    if live(3):
                        u = t - 3
                        for i in range(IC):
                            n = IC * u + i
                            r = rows(i)
                            if isinstance(u, int):
                                dst = hidden[0:r, u, i * UT:(i + 1) * UT]
                                peak = hidden_max[0:r, n:n + 1]
                            else:
                                dst = hidden[0:r, bass.ds(u, 1), i * UT:(i + 1) * UT].rearrange(
                                    "p a n -> p (a n)")
                                peak = hidden_max[0:r, bass.ds(n, 1)]
                            dve.wait_ge(up_done, n + 1)
                            dve.wait_ge(silu_done, n + 1)
                            dve.scalar_tensor_tensor(dst, up_banks[i % 3][0:r, :],
                                                     up_scale[0:r, i:i + 1], silu[0:r, i % 3, :],
                                                     ALU.mult, ALU.mult).then_inc(hidden_done, 1)
                            if i > 0:
                                dve.wait_ge(hidden_done, n)
                                dve.tensor_reduce(*former, axis=AX.X, op=ALU.max,
                                                  apply_absolute_value=True).then_inc(hidden_maxed, 1)
                            former = peak, dst
                        dve.wait_ge(hidden_done, IC * u + IC)
                        dve.tensor_reduce(*former, axis=AX.X, op=ALU.max,
                                          apply_absolute_value=True).then_inc(hidden_maxed, 1)
                pipeline(dve, body, 4, 2, UNITS)
                dve.wait_ge(hidden_maxed, UNITS * IC)
                whole_max(dve, 1, hidden_max[:], max_bank, h_maxed, h_turned, h_taken, h_spread)
                dve.tensor_scalar(act_scale[:, 1:2], max_bank[:, P:P + 1], sig[:, 1:2], 1.0 / QMAX,
                                  ALU.mult, ALU.mult).then_inc(sc, 1)
                dve.wait_ge(sc, 1)
                dve.reciprocal(act_inverse[:, 1:2], act_scale[:, 1:2])
                dve.tensor_scalar(down_row[:], down_row[:], act_scale[:, 1:2], None, ALU.mult
                                  ).then_inc(sc, 1)
                dve.wait_ge(sc, 2)

        with ExitStack() as part:
            h_ints = sb("h_ints", [P, 2, IC * UT], BF16, part)
            addend = sb("addend", [P, U, D], F32, part)
            out_banks = [bank(f"out{i}", part) for i in range(4)]
            h_scaled, h_clipped, h_ints_done, down_done, addend_done, x_done = map(sem, (
                "h_scaled", "h_clipped", "h_ints_done", "down_done", "addend_done", "x_done"))
            stored = [sem(f"stored{i}") for i in range(UNITS)]
            block = part.enter_context(nc.Block())
            full = (IC - 1) * UT
            parts = ((P, 0, full), (rows(IC - 1), full, IC * UT))

            def hidden_part(t, r, lo, hi):
                if isinstance(t, int):
                    return hidden[0:r, t, lo:hi]
                return hidden[0:r, bass.ds(t, 1), lo:hi].rearrange("p a n -> p (a n)")

            @block.vector
            def _(dve):
                def body(t, par, live):
                    if live(0):
                        for r, lo, hi in parts:
                            h = hidden_part(t, r, lo, hi)
                            dve.tensor_scalar(h, h, act_inverse[0:r, 1:2], ROUND,
                                              ALU.mult, ALU.add).then_inc(h_scaled, 1)
                        for i, (r, lo, hi) in enumerate(parts):
                            h = hidden_part(t, r, lo, hi)
                            dve.wait_ge(h_scaled, 2 * t + i + 1)
                            dve.tensor_scalar(h, h,
                                              ROUND - QMAX - 1.0, ROUND + QMAX, ALU.max, ALU.min
                                              ).then_inc(h_clipped, 1)
                    if live(1):
                        u = t - 1
                        for s in range(U):
                            n = U * u + s
                            dve.wait_ge(down_done, n + 1)
                            waits(dve, x_done, n - U + 1)
                            dve.tensor_tensor(addend[:, s, :], out_banks[s][:, 0:D], down_row[:],
                                              ALU.mult).then_inc(addend_done, 1)
                pipeline(dve, body, 2, 2, UNITS)

            @block.scalar
            def _(act):
                def body(t, par, live):
                    if live(0):
                        apart(act, k)
                        waits(act, down_done, U * (t - 1))
                        for i, (r, lo, hi) in enumerate(parts):
                            apart(act, k)
                            act.wait_ge(h_clipped, 2 * t + i + 1)
                            act.activation(h_ints[0:r, par, lo:hi], hidden_part(t, r, lo, hi), ACT.Copy,
                                           bias=-ROUND).then_inc(h_ints_done, 1)
                pipeline(act, body, 1, 2, UNITS)

            @block.tensor
            def _(pe):
                def body(t, par, live):
                    pe.wait_ge(h_ints_done, 2 * t + 2)
                    for s in range(U):
                        waits(pe, addend_done, U * (t - 1) + s + 1)
                        for i in range(IC):
                            at = i * UT + s * S
                            last = pe.matmul(out_banks[s][:, 0:D], h_ints[0:rows(i), par, at:at + S],
                                             down_t[0:rows(i), i, :], start=i == 0, stop=i == IC - 1)
                        last.then_inc(down_done, 1)
                pipeline(pe, body, 1, 2, UNITS)

            @block.gpsimd
            def _(pool):
                def body(t, par, live):
                    for s in range(U):
                        n = U * t + s
                        pool.wait_ge(addend_done, n + 1)
                        pool.tensor_tensor(seq(x, n), seq(x, n), addend[:, s, :], ALU.add
                                           ).then_inc(x_done, 1)
                pipeline(pool, body, 1, 2, UNITS)

            @block.sync
            def _(sp):
                for u in range(UNITS):
                    sp.wait_ge(x_done, U * (u + 1))
                    sp.dma_start(out[U * u:U * u + U].rearrange("b t d -> t b d"),
                                 x[:, U * u:U * u + U, :]).then_inc(stored[u], 16)
                for u in range(UNITS):
                    sp.wait_ge(stored[u], 16)


class Constants:
    pass


def decoder(nc, a, out):
    with ExitStack() as ctx:
        def sb(n, shape, dt=F32, c=ctx):
            return c.enter_context(nc.sbuf_tensor(n, shape, dt))

        def sem(n):
            return ctx.enter_context(nc.semaphore(n))

        x = sb("x_all", [P, B, D])
        k = Constants()
        at, widths = 0, (("ident", P), ("causal", S), ("window", S), ("even_rows", 1),
                         ("odd_rows", 1), ("iota", E), ("l0_rope", 4 * HD), ("freq", HD // 2))
        tables = sb("tables", [P, sum(w for _, w in widths)])
        table = {}
        for n, w in widths:
            table[n] = tables[:, at:at + w]
            at += w
        k.ident, k.even_rows, k.odd_rows, k.iota = (
            table[n] for n in ("ident", "even_rows", "odd_rows", "iota"))
        k.ident_bf = sb("ident_bf", [P, P], BF16)
        k.ones = sb("ones", [P, P])
        k.minus_half = sb("minus_half", [P, 2 * H])
        k.eps = sb("eps", [P, 1])
        k.rms_eps = sb("rms_eps", [P, 2 * H])
        clips = sb("clips", [P, 2])
        x_loaded = [sem("x_loaded0"), sem("x_loaded1")]
        k.constants_done = sem("constants_done")

        with ExitStack() as early:
            def big(n, shape, dt=F32):
                return sb(n, shape, dt, early)

            causal = big("causal", [P, S], BF16)
            window = big("window", [P, S], BF16)
            l0_rope = table["l0_rope"]
            l1_rope = big("l1_rope", [P, B, 4 * HD])
            weights, loaded = {}, {}
            for n, shape in (("L0_attn_w_in", [P, KC, 3 * D]), ("L0_attn_w_out", [P, KC, D]),
                             ("L0_xattn_w_in", [P, KC, 3 * D]), ("L0_router", [P, KC, E]),
                             ("L0_experts", [P, KC, E * D]), ("L1_attn_w_in", [P, KC, 3 * D]),
                             ("L1_attn_w_out", [P, KC, D]), ("L1_xattn_w_in", [P, KC, 3 * D]),
                             ("L1_xattn_w_out", [P, KC, D])):
                weights[n] = big(f"{n}_sb", shape)
                loaded[n] = (sem(f"{n}_loaded"), 16)
            rows_of = {}
            for n, width in (("L0_attn_bias", 3 * D), ("L0_attn_bo", D), ("L0_xattn_bv", D),
                             ("L0_router_b", E)):
                rows_of[n] = big(f"{n}_sb", [P, width])
            l0_xattn_bq = big("l0_xattn_bq", [P, KC])
            l0_xattn_bk = big("l0_xattn_bk", [P, KC])
            expert_bias = big("expert_bias", [E, D])
            experts_high = big("experts_high", [P, KC, E * D], F32R)
            experts_low = big("experts_low", [P, KC, E * D], F32R)
            experts_split = sem("experts_split")
            attn_high = big("attn_high", [P, KC, 3 * D], F32R)
            attn_low = big("attn_low", [P, KC, 3 * D], F32R)
            attn_split = sem("attn_split")

            with ExitStack() as part:
                scale = sb("l0_scale", [P, 1], F32, part)
                pos = sb("pos", [P, B], F32, part)
                norm_w = sb("norm_w", [P, 2, HD], F32, part)
                angle = sb("angle", [P, B, HD // 2], F32, part)
                turns = sb("turns", [P, B, HD // 2], F32, part)
                cosine = sb("cosine", [P, B, HD // 2], F32, part)
                sine = sb("sine", [P, B, HD // 2], F32, part)
                minus_sine = sb("minus_sine", [P, B, HD // 2], F32, part)
                small = [sem(f"small{i}") for i in range(10)]
                sin_angle, cos_angle, sin_done, chain = map(sem, ("sin_angle", "cos_angle",
                                                                   "sin_done", "setup_chain"))
                block = part.enter_context(nc.Block())

                def spread(row, width):
                    return row.rearrange("(a n) -> a n", a=1).broadcast_to([P, width])

                smalls = [(tables[:], a["tables"]), (pos[:], a["pos_t"]),
                          (scale[:], spread(a["L0_scale"], 1)),
                          (norm_w[:, 0, :], spread(a["L1_q_norm"], HD)),
                          (norm_w[:, 1, :], spread(a["L1_k_norm"], HD)),
                          (clips[:, 0:1], spread(a["clip_x"], 1)),
                          (clips[:, 1:2], spread(a["clip_down"], 1)),
                          (l0_xattn_bq[:], a["L0_xattn_bq"]),
                          (l0_xattn_bk[:], a["L0_xattn_bk"]),
                          (expert_bias[:], a["L0_expert_b"])]
                row_loads = [sem(f"row{i}") for i in range(4)]

                @block.sync
                def _(sp):
                    for n in ("L0_attn_w_in", "L0_attn_w_out"):
                        sp.dma_start(weights[n][:], a[n].rearrange("(c p) n -> p c n", p=P)
                                     ).then_inc(loaded[n][0], 16)
                    sp.dma_start(x[:, 0:4, :], a["x"][0:4].rearrange("b t d -> t b d")
                                 ).then_inc(x_loaded[0], 16)
                    for i, (n, row) in enumerate(rows_of.items()):
                        sp.dma_start(row[:], spread(a[n], row.shape[1])).then_inc(row_loads[i], 16)
                    for s in (row_loads[-1], small[-1]):
                        sp.wait_ge(s, 16)
                    sp.dma_start(x[:, 4:B, :], a["x"][4:B].rearrange("b t d -> t b d")
                                 ).then_inc(x_loaded[1], 16)
                    for n in list(weights)[2:]:
                        src = a[n].rearrange("(c p) n -> p c n", p=P)
                        sp.dma_start(weights[n][:], src).then_inc(loaded[n][0], 16)

                @block.gpsimd
                def _(pool):
                    pool.wait_ge(loaded["L0_attn_w_in"][0], 16)
                    pool.tensor_copy(attn_high[:], weights["L0_attn_w_in"][:]).then_inc(attn_split, 1)
                    pool.wait_ge(attn_split, 1)
                    pool.tensor_tensor(attn_low[:], weights["L0_attn_w_in"][:],
                                       attn_high[:].bitcast(F32), ALU.subtract
                                       ).then_inc(attn_split, 1)

                @block.scalar
                def _(act):
                    for i, (dst, src) in enumerate(smalls):
                        act.dma_start(dst, src).then_inc(small[i], 16)
                    act.wait_ge(sin_angle, 1)
                    act.activation(sine[:], angle[:], ACT.Sin).then_inc(sin_done, 1)
                    act.wait_ge(cos_angle, 1)
                    act.activation(cosine[:], turns[:], ACT.Sin).then_inc(sin_done, 1)

                @block.vector
                def _(dve):
                    steps = [0]

                    def step(instruction):
                        steps[0] += 1
                        instruction.then_inc(chain, 1)
                        dve.wait_ge(chain, steps[0])

                    dve.memset(k.ones[:], 1.0)
                    dve.memset(k.minus_half[:], -0.5)
                    dve.memset(k.eps[:], EPS)
                    dve.memset(k.rms_eps[:], HD * RMS_EPS)
                    for s in small[0:5]:
                        dve.wait_ge(s, 16)
                    dve.tensor_copy(k.ident_bf[:], k.ident[:])
                    dve.tensor_copy(causal[:], table["causal"])
                    dve.tensor_copy(window[:], table["window"])
                    for lo in (0, 2 * HD):
                        dve.tensor_scalar(l0_rope[:, lo:lo + HD], l0_rope[:, lo:lo + HD], scale[:],
                                          None, ALU.mult)
                    dve.tensor_scalar(norm_w[:, 1, :], norm_w[:, 1, :], HD ** 0.5, None, ALU.mult)
                    step(dve.tensor_tensor(angle[:], pos[:, :, None].broadcast_to([P, B, HD // 2]),
                                           table["freq"][:, None, :].broadcast_to([P, B, HD // 2]), ALU.mult))
                    step(dve.tensor_scalar(turns[:], angle[:], 1.0 / TWO_PI, ROUND, ALU.mult, ALU.add))
                    step(dve.tensor_scalar(turns[:], turns[:], -ROUND, None, ALU.add))
                    for part_of in PI_PARTS:
                        step(dve.scalar_tensor_tensor(angle[:], turns[:], -part_of, angle[:],
                                                      ALU.mult, ALU.add))
                    dve.tensor_scalar(angle[:], angle[:], -PI_BELOW, PI_BELOW, ALU.max, ALU.min
                                      ).then_inc(sin_angle, 1)
                    dve.wait_ge(sin_angle, 1)
                    step(dve.tensor_scalar(minus_sine[:], angle[:], PI_BELOW / 2, -TWO_PI, ALU.is_gt,
                                           ALU.mult))
                    step(dve.tensor_scalar(turns[:], angle[:], float(np.pi / 2), None, ALU.add))
                    step(dve.tensor_tensor(turns[:], turns[:], minus_sine[:], ALU.add))
                    dve.tensor_scalar(turns[:], turns[:], -PI_BELOW, PI_BELOW, ALU.max, ALU.min
                                      ).then_inc(cos_angle, 1)
                    dve.wait_ge(sin_done, 2)
                    step(dve.tensor_scalar(minus_sine[:], sine[:], -1.0, None, ALU.mult))
                    for s in small[5:] + row_loads:
                        dve.wait_ge(s, 16)
                    half = HD // 2
                    for which in range(2):
                        for f in range(2):
                            w = norm_w[:, which, f * half:(f + 1) * half]
                            v = norm_w[:, which, (1 - f) * half:(2 - f) * half]
                            at = which * HD + f * half
                            dve.tensor_tensor(l1_rope[:, :, at:at + half], cosine[:],
                                              w[:, None, :].broadcast_to([P, B, half]), ALU.mult)
                            last = dve.tensor_tensor(
                                l1_rope[:, :, 2 * HD + at:2 * HD + at + half],
                                (minus_sine, sine)[f][:],
                                v[:, None, :].broadcast_to([P, B, half]), ALU.mult)
                    last.then_inc(k.constants_done, 1)

            w = weights

            def split_experts(pool):
                pool.wait_ge(loaded["L0_experts"][0], 16)
                for c in range(KC):
                    pool.tensor_copy(experts_high[:, c, :], w["L0_experts"][:, c, :]
                                     ).then_inc(experts_split, 1)
                for c in range(KC):
                    pool.wait_ge(experts_split, KC + c)
                    pool.tensor_tensor(experts_low[:, c, :], w["L0_experts"][:, c, :],
                                       experts_high[:, c, :].bitcast(F32), ALU.subtract
                                       ).then_inc(experts_split, 1)

            heads_attention(nc, "l0a", x, k, (attn_high, attn_low), w["L0_attn_w_out"],
                            qkv_bias=rows_of["L0_attn_bias"], out_bias=rows_of["L0_attn_bo"],
                            mask=causal, rope=l0_rope,
                            loads=[(attn_split, 2), loaded["L0_attn_w_out"]],
                            x_arrives={0: x_loaded[0], 4: x_loaded[1]},
                            pool_after=split_experts)
            context_attention(nc, "l0x", x, k, w["L0_xattn_w_in"], l0_xattn_bq, l0_xattn_bk,
                              rows_of["L0_xattn_bv"], a["ctx_t"], [loaded["L0_xattn_w_in"]])
            experts(nc, "l0f", x, k, w["L0_router"], rows_of["L0_router_b"], (experts_high, experts_low),
                    expert_bias, [loaded["L0_router"], (experts_split, 2 * KC)])
            heads_attention(nc, "l1a", x, k, w["L1_attn_w_in"], w["L1_attn_w_out"], mask=window,
                            scale=HD ** -0.5,
                            loads=[loaded["L1_attn_w_in"], loaded["L1_attn_w_out"]])
            heads_attention(nc, "l1x", x, k, w["L1_xattn_w_in"], w["L1_xattn_w_out"],
                            batch_rope=l1_rope, ctx_t=a["ctx_t"],
                            loads=[loaded["L1_xattn_w_in"], loaded["L1_xattn_w_out"]])
        quantised_ffn(nc, "l1f", x, k, a["w_gate"], a["w_up"], a["w_down"], clips, out, [])


PI_PARTS = [6.28125, float(np.float32(0.0019350051879882812)),
            float(TWO_PI - 6.28125 - np.float32(0.0019350051879882812))]
PI_BELOW = float(np.nextafter(np.float32(np.pi), np.float32(0)))


def constants():
    half = HD // 2
    freq = (10000.0 ** (-np.arange(0, HD, 2, dtype=np.float32) / np.float32(HD))).astype(np.float32)
    angle = (np.arange(S, dtype=np.float32)[:, None] * freq).astype(np.float32).astype(np.float64)
    cos, sin = np.cos(angle), np.sin(angle)
    rope = np.concatenate([cos, cos, cos, cos, -sin, sin, -sin, sin], 1).astype(np.float32)
    q, key = np.arange(S)[:, None], np.arange(S)[None, :]
    odd = (np.arange(P) // HD % 2).astype(np.float32)[:, None]
    return {"tables": np.concatenate([
        np.eye(P), np.where(key > q, NEG, 0.0), np.where((key > q) | (key <= q - 64), NEG, 0.0),
        1 - odd, odd, np.broadcast_to(np.arange(E), (P, E)), rope,
        np.broadcast_to(freq, (P, half))], 1).astype(np.float32)}


def kernel(**inputs):
    import numpy as _np
    import concourse.bacc as _bacc
    from concourse import mybir as _mybir
    from concourse.bass_utils import run_bass_kernel_spmd as _run

    i = {n: _np.asarray(v) for n, v in inputs.items()}
    order = _np.arange(D).reshape(H, HD // 2, 2).transpose(0, 2, 1).reshape(D)
    arrays = {
        "x": i["x"], "ctx_t": i["ctx_1024"].transpose(0, 2, 1), "pos_t": i["fside_BxS2_0"].T,
        "L0_attn_w_in": _np.concatenate([i["L0_attn_Wq"][order].T, i["L0_attn_Wk"][order].T,
                                         i["L0_attn_Wv"].T], 1),
        "L0_attn_w_out": i["L0_attn_Wo"].T,
        "L0_attn_bias": _np.concatenate([i["L0_attn_bq"][order], i["L0_attn_bk"][order],
                                         i["L0_attn_bv"]]),
        "L0_attn_bo": i["L0_attn_bo"], "L0_scale": i["L0_attn_scale"],
        "L0_xattn_w_in": _np.concatenate([i["L0_xattn_Wq_w"].T, i["L0_xattn_Wk_w"].T,
                                          i["L0_xattn_Wv_w"].T], 1),
        "L0_xattn_bq": i["L0_xattn_Wq_b"].reshape(KC, P).T,
        "L0_xattn_bk": i["L0_xattn_Wk_b"].reshape(KC, P).T,
        "L0_xattn_bv": i["L0_xattn_Wv_b"],
        "L0_router": i["L0_ffn_router_w"], "L0_router_b": i["L0_ffn_router_b"],
        "L0_experts": i["L0_ffn_expert_w"].transpose(1, 0, 2).reshape(D, E * D),
        "L0_expert_b": i["L0_ffn_expert_b"],
        "L1_attn_w_in": i["L1_attn_W_qkv"], "L1_attn_w_out": i["L1_attn_W_out"],
        "L1_xattn_w_in": _np.concatenate([i["L1_xattn_Wq"], i["L1_xattn_Wkv"]], 1),
        "L1_xattn_w_out": i["L1_xattn_Wo"],
        "L1_q_norm": i["L1_xattn_q_norm_w"], "L1_k_norm": i["L1_xattn_k_norm_w"],
        "clip_x": i["L1_ffn_clip_x"], "clip_down": i["L1_ffn_clip_down"],
        "w_gate": i["L1_ffn_w_gate"], "w_up": i["L1_ffn_w_up"], "w_down": i["L1_ffn_w_down"],
        **constants(),
    }
    nc = _bacc.Bacc("TRN2", target_bir_lowering=False, num_devices=1)
    launched, aps = {}, {}
    for name, value in arrays.items():
        value = _np.ascontiguousarray(value)
        launched[f"in_{name}"] = value
        aps[name] = nc.dram_tensor(f"in_{name}", value.shape, _mybir.dt.from_np(value.dtype),
                                   kind="ExternalInput").ap()
    out = nc.dram_tensor("out", (B, S, D), _mybir.dt.float32, kind="ExternalOutput").ap()
    decoder(nc, aps, out)
    r = _run(nc, [launched], core_ids=[0])
    return r.results[0]["out"]
```
